# Optimizing a Trainium2 kernel written in Bass

```python
import numpy as np
import jax
import jax.numpy as jnp

def _softmax(x, axis=-1):
    return jax.nn.softmax(x, axis=axis)

def _gelu(x):
    return jax.nn.gelu(x, approximate=True)

def _silu(x):
    return jax.nn.silu(x)

def _sigmoid(x):
    return jax.nn.sigmoid(x)

def _layernorm(x, axis=-1, eps=1e-05):
    m = jnp.mean(x, axis=axis, keepdims=True)
    v = jnp.var(x, axis=axis, keepdims=True)
    return (x - m) / jnp.sqrt(v + eps)

def _scatter_add(tgt, idx, src, axis=0):
    return tgt.at[idx].add(src)

def _segment_sum(src, seg, n):
    return jax.ops.segment_sum(src, seg, n)
kernel_name = 'mk_early_fusion_embed_d1_tok_img768_r4_804004'

def setup_inputs(seed: int=0):
    np.random.seed(seed)
    _w = jnp.asarray

    def _rec_inputs():
        import jax
        import jax.numpy as jnp
        _rk = jax.random.key(seed)
        x = -0.00016672 + 0.999947 * jax.random.normal(jax.random.fold_in(_rk, 1), (64, 3, 64, 64), jnp.float32)
        x_txt = jax.random.randint(jax.random.fold_in(_rk, 51), (64, 77), 0, 30522, jnp.int32)
        mask_BS_i1_0 = jnp.where(jnp.ones((64, 77), dtype=bool), 1, 0).astype(jnp.int32)
        pos_BS = jnp.broadcast_to(jnp.arange(77, dtype=jnp.int32), (64, 77))
        mask_BS_i0_1 = jnp.where(jnp.ones((64, 77), dtype=bool), 0, 1).astype(jnp.int32)
        itok_BS_0_3 = jax.random.randint(jax.random.fold_in(_rk, 74), (64, 77), 0, 4, jnp.int32)
        itok_BS_0_9 = jax.random.randint(jax.random.fold_in(_rk, 75), (64, 77), 0, 10, jnp.int32)
        return (x, x_txt, mask_BS_i1_0, pos_BS, mask_BS_i0_1, itok_BS_0_3, itok_BS_0_9)
    x, x_txt, mask_BS_i1_0, pos_BS, mask_BS_i0_1, itok_BS_0_3, itok_BS_0_9 = _rec_inputs()

    def _L0_tok_setup():
        import jax, jax.numpy as jnp
        import numpy as np
        PATCH = 16
        EMB = 192
        key = jax.random.key(seed)
        k1, k2, k3 = jax.random.split(key, 3)
        x = jax.random.normal(k1, (64, 3, 96, 96), dtype=jnp.float32)
        in_dim = 3 * PATCH * PATCH
        W = jax.random.uniform(k2, (EMB, in_dim), dtype=jnp.float32, minval=-1.0, maxval=1.0) / np.sqrt(in_dim)
        b = jax.random.uniform(k3, (EMB,), dtype=jnp.float32, minval=-1.0, maxval=1.0) / np.sqrt(in_dim)
        return {'x': x, 'W': W, 'b': b}
    _L0_tok_all = _L0_tok_setup()
    _L0_tok_in = {k: v for k, v in _L0_tok_all.items() if k in ('W', 'b')}
    del _L0_tok_all

    def _L0_txt_setup():
        import jax, jax.numpy as jnp
        import numpy as np
        B, S, H = (64, 128, 192)
        VOCAB, MAX_POS, SF_LEVEL, N_ETYPES = (30522, 128, 4, 10)
        EPS = 1e-12

        def _layer_norm(x, gamma, beta):
            mu = jnp.mean(x, axis=-1, keepdims=True)
            var = jnp.mean(jnp.square(x - mu), axis=-1, keepdims=True)
            return (x - mu) * jax.lax.rsqrt(var + EPS) * gamma + beta
        key = jax.random.key(seed)
        ks = jax.random.split(key, 24)
        inp = {'input_ids': jax.random.randint(ks[0], (B, S), 0, VOCAB), 'token_type_ids': jax.random.randint(ks[1], (B, S), 0, 2), 'position_ids': jnp.broadcast_to(jnp.arange(S, dtype=jnp.int64 if jax.config.jax_enable_x64 else jnp.int32), (B, S)), 'match_entity': jax.random.randint(ks[2], (B, S), 0, 2), 'sf_entity': jax.random.randint(ks[3], (B, S), 0, SF_LEVEL), 'match_token': jax.random.randint(ks[4], (B, S), 0, 2), 'sf_token': jax.random.randint(ks[5], (B, S), 0, SF_LEVEL), 'etype_ids': jax.random.randint(ks[6], (B, S), 0, N_ETYPES), 'atype_ent_match': jax.random.randint(ks[7], (B, S), 0, 2), 'amatch_type': jax.random.randint(ks[8], (B, S), 0, 4), 'W_word': jax.random.normal(ks[9], (VOCAB, H), jnp.float32) * 0.02, 'W_type': jax.random.normal(ks[10], (2, H), jnp.float32) * 0.02, 'W_pos': jax.random.normal(ks[11], (MAX_POS, H), jnp.float32) * 0.02, 'W_match_ent': jax.random.normal(ks[12], (2, H), jnp.float32) * 0.02, 'W_sf_ent': jax.random.normal(ks[13], (SF_LEVEL, H), jnp.float32) * 0.02, 'W_match_tok': jax.random.normal(ks[14], (2, H), jnp.float32) * 0.02, 'W_sf_tok': jax.random.normal(ks[15], (SF_LEVEL, H), jnp.float32) * 0.02, 'W_etype': jax.random.normal(ks[16], (N_ETYPES, H), jnp.float32) * 0.02, 'W_atype_ent': jax.random.normal(ks[17], (2, H), jnp.float32) * 0.02, 'W_amatch': jax.random.normal(ks[18], (4, H), jnp.float32) * 0.02, 'ln_gamma': jnp.ones((H,), jnp.float32), 'ln_beta': jnp.zeros((H,), jnp.float32)}
        return inp
    _L0_txt_all = _L0_txt_setup()
    _L0_txt_in = {k: v for k, v in _L0_txt_all.items() if k in ('W_word', 'W_type', 'W_pos', 'W_match_ent', 'W_sf_ent', 'W_match_tok', 'W_sf_tok', 'W_etype', 'W_atype_ent', 'W_amatch', 'ln_gamma', 'ln_beta')}
    del _L0_txt_all

    def _L0_attn_setup():
        import jax, jax.numpy as jnp
        import numpy as np
        B, N, D = (4, 2048, 192)
        H, DH = (12, 64)
        INNER = H * DH
        key = jax.random.key(seed)
        k0, k1, k2 = jax.random.split(key, 3)
        return {'x': jax.random.normal(k0, (B, N, D), dtype=jnp.float32), 'w_qkv': jax.random.normal(k1, (D, INNER), dtype=jnp.float32) * 0.02, 'temp': jnp.ones((H, 1), dtype=jnp.float32), 'w_out': jax.random.normal(k2, (INNER, D), dtype=jnp.float32) * 0.02, 'b_out': jnp.zeros((D,), dtype=jnp.float32)}
    _L0_attn_all = _L0_attn_setup()
    _L0_attn_in = {k: v for k, v in _L0_attn_all.items() if k in ('w_qkv', 'temp', 'w_out', 'b_out')}
    del _L0_attn_all

    def _L0_ffn_setup():
        import jax, jax.numpy as jnp
        import numpy as np
        B, T, D = (2, 512, 192)
        S, R, M, K = (8, 16, 64, 4)
        H, G = (32, 64)

        def _ssinf3(x, P, C, W1, b1, W2, b2, G1, g1b, G2, g2b):
            shp = x.shape
            xf = x.reshape(-1, shp[-1])
            z = jnp.einsum('nd,sdr->nsr', xf, P)
            scores = jnp.einsum('nsr,smr->nsm', z, C)
            topv, topi = jax.lax.top_k(scores, K)
            w = jax.nn.softmax(topv, axis=-1)
            sidx = jnp.arange(S)[None, :, None]
            W1g = W1[sidx, topi]
            b1g = b1[sidx, topi]
            W2g = W2[sidx, topi]
            b2g = b2[sidx, topi]
            h = jax.nn.gelu(jnp.einsum('nsr,nskrh->nskh', z, W1g) + b1g)
            yl = jnp.einsum('nskh,nskhr->nskr', h, W2g) + b2g
            comb = jnp.einsum('nskr,nsk->nsr', yl, w)
            comb = comb.reshape(xf.shape[0], S * R)
            out = jax.nn.gelu(comb @ G1 + g1b) @ G2 + g2b
            return out.reshape(shp)
        key = jax.random.key(seed)
        k = jax.random.split(key, 8)
        rn = lambda kk, shape, s: jax.random.normal(kk, shape, dtype=jnp.float32) * s
        return {'x': rn(k[0], (B, T, D), 1.0), 'P': rn(k[1], (S, D, R), D ** (-0.5)), 'C': rn(k[2], (S, M, R), R ** (-0.5)), 'W1': rn(k[3], (S, M, R, H), R ** (-0.5)), 'b1': jnp.zeros((S, M, H), jnp.float32), 'W2': rn(k[4], (S, M, H, R), H ** (-0.5)), 'b2': jnp.zeros((S, M, R), jnp.float32), 'G1': rn(k[5], (S * R, G), (S * R) ** (-0.5)), 'g1b': jnp.zeros((G,), jnp.float32), 'G2': rn(k[6], (G, D), G ** (-0.5)), 'g2b': jnp.zeros((D,), jnp.float32)}
    _L0_ffn_all = _L0_ffn_setup()
    _L0_ffn_in = {k: v for k, v in _L0_ffn_all.items() if k in ('P', 'C', 'W1', 'b1', 'W2', 'b2', 'G1', 'g1b', 'G2', 'g2b')}
    del _L0_ffn_all
    return {'x': x, 'x_txt': x_txt, 'mask_BS_i1_0': mask_BS_i1_0, 'pos_BS': pos_BS, 'mask_BS_i0_1': mask_BS_i0_1, 'itok_BS_0_3': itok_BS_0_3, 'itok_BS_0_9': itok_BS_0_9, 'L0_tok_W': _L0_tok_in['W'], 'L0_tok_b': _L0_tok_in['b'], 'L0_txt_W_word': _L0_txt_in['W_word'], 'L0_txt_W_type': _L0_txt_in['W_type'], 'L0_txt_W_pos': _L0_txt_in['W_pos'], 'L0_txt_W_match_ent': _L0_txt_in['W_match_ent'], 'L0_txt_W_sf_ent': _L0_txt_in['W_sf_ent'], 'L0_txt_W_match_tok': _L0_txt_in['W_match_tok'], 'L0_txt_W_sf_tok': _L0_txt_in['W_sf_tok'], 'L0_txt_W_etype': _L0_txt_in['W_etype'], 'L0_txt_W_atype_ent': _L0_txt_in['W_atype_ent'], 'L0_txt_W_amatch': _L0_txt_in['W_amatch'], 'L0_txt_ln_gamma': _L0_txt_in['ln_gamma'], 'L0_txt_ln_beta': _L0_txt_in['ln_beta'], 'L0_attn_w_qkv': _L0_attn_in['w_qkv'], 'L0_attn_temp': _L0_attn_in['temp'], 'L0_attn_w_out': _L0_attn_in['w_out'], 'L0_attn_b_out': _L0_attn_in['b_out'], 'L0_ffn_P': _L0_ffn_in['P'], 'L0_ffn_C': _L0_ffn_in['C'], 'L0_ffn_W1': _L0_ffn_in['W1'], 'L0_ffn_b1': _L0_ffn_in['b1'], 'L0_ffn_W2': _L0_ffn_in['W2'], 'L0_ffn_b2': _L0_ffn_in['b2'], 'L0_ffn_G1': _L0_ffn_in['G1'], 'L0_ffn_g1b': _L0_ffn_in['g1b'], 'L0_ffn_G2': _L0_ffn_in['G2'], 'L0_ffn_g2b': _L0_ffn_in['g2b']}

def reference(x, x_txt, mask_BS_i1_0, pos_BS, mask_BS_i0_1, itok_BS_0_3, itok_BS_0_9, L0_tok_W, L0_tok_b, L0_txt_W_word, L0_txt_W_type, L0_txt_W_pos, L0_txt_W_match_ent, L0_txt_W_sf_ent, L0_txt_W_match_tok, L0_txt_W_sf_tok, L0_txt_W_etype, L0_txt_W_atype_ent, L0_txt_W_amatch, L0_txt_ln_gamma, L0_txt_ln_beta, L0_attn_w_qkv, L0_attn_temp, L0_attn_w_out, L0_attn_b_out, L0_ffn_P, L0_ffn_C, L0_ffn_W1, L0_ffn_b1, L0_ffn_W2, L0_ffn_b2, L0_ffn_G1, L0_ffn_g1b, L0_ffn_G2, L0_ffn_g2b):
    import jax
    import jax.numpy as jnp

    def _L0_tok_ref(x, W, b):
        import jax, jax.numpy as jnp
        import numpy as np
        PATCH = 16
        EMB = 192
        B, C, H, Wd = x.shape
        p = PATCH
        nH, nW = (H // p, Wd // p)
        x = x.reshape(B, C, nH, p, nW, p).transpose(0, 1, 3, 5, 2, 4)
        x = x.reshape(B, C * p * p, nH * nW).transpose(0, 2, 1)
        return jnp.einsum('bnd,ed->bne', x, W) + b

    def _L0_txt_ref(input_ids, token_type_ids, position_ids, match_entity, sf_entity, match_token, sf_token, etype_ids, atype_ent_match, amatch_type, W_word, W_type, W_pos, W_match_ent, W_sf_ent, W_match_tok, W_sf_tok, W_etype, W_atype_ent, W_amatch, ln_gamma, ln_beta):
        import jax, jax.numpy as jnp
        import numpy as np
        B, S, H = (64, 128, 192)
        VOCAB, MAX_POS, SF_LEVEL, N_ETYPES = (30522, 128, 4, 10)
        EPS = 1e-12

        def _layer_norm(x, gamma, beta):
            mu = jnp.mean(x, axis=-1, keepdims=True)
            var = jnp.mean(jnp.square(x - mu), axis=-1, keepdims=True)
            return (x - mu) * jax.lax.rsqrt(var + EPS) * gamma + beta
        emb = W_word[input_ids] + W_pos[position_ids] + W_type[(token_type_ids > 0).astype(jnp.int32)] + W_match_tok[match_token] + W_match_ent[match_entity] + W_sf_tok[sf_token] + W_sf_ent[sf_entity] + W_etype[etype_ids] + W_atype_ent[atype_ent_match]
        return _layer_norm(emb, ln_gamma, ln_beta)

    def _L0_attn_ref(x, w_qkv, temp, w_out, b_out):
        import jax, jax.numpy as jnp
        import numpy as np
        B, N, D = (4, 2048, 192)
        H, DH = (12, 64)
        INNER = H * DH
        b, n, _ = x.shape
        h = temp.shape[0]
        w = (x @ w_qkv).reshape(b, n, h, -1).transpose(0, 2, 1, 3)
        norm = jnp.sqrt(jnp.sum(w * w, axis=2, keepdims=True))
        w_normed = w / jnp.maximum(norm, 1e-12)
        logits = jnp.sum(w_normed * w_normed, axis=-1) * temp
        Pi = jax.nn.softmax(logits, axis=-1)
        Pi_norm = Pi / (jnp.sum(Pi, axis=-1, keepdims=True) + 1e-08)
        dots = jnp.einsum('bhn,bhnd->bhd', Pi_norm, w * w)[:, :, None, :]
        attn = 1.0 / (1.0 + dots)
        out = -(w * Pi[..., None]) * attn
        out = out.transpose(0, 2, 1, 3).reshape(b, n, -1)
        return out @ w_out + b_out

    def _L0_ffn_ref(x, P, C, W1, b1, W2, b2, G1, g1b, G2, g2b):
        import jax, jax.numpy as jnp
        import numpy as np
        B, T, D = (2, 512, 192)
        S, R, M, K = (8, 16, 64, 4)
        H, G = (32, 64)

        def _ssinf3(x, P, C, W1, b1, W2, b2, G1, g1b, G2, g2b):
            shp = x.shape
            xf = x.reshape(-1, shp[-1])
            z = jnp.einsum('nd,sdr->nsr', xf, P)
            scores = jnp.einsum('nsr,smr->nsm', z, C)
            topv, topi = jax.lax.top_k(scores, K)
            w = jax.nn.softmax(topv, axis=-1)
            sidx = jnp.arange(S)[None, :, None]
            W1g = W1[sidx, topi]
            b1g = b1[sidx, topi]
            W2g = W2[sidx, topi]
            b2g = b2[sidx, topi]
            h = jax.nn.gelu(jnp.einsum('nsr,nskrh->nskh', z, W1g) + b1g)
            yl = jnp.einsum('nskh,nskhr->nskr', h, W2g) + b2g
            comb = jnp.einsum('nskr,nsk->nsr', yl, w)
            comb = comb.reshape(xf.shape[0], S * R)
            out = jax.nn.gelu(comb @ G1 + g1b) @ G2 + g2b
            return out.reshape(shp)
        return _ssinf3(x, P, C, W1, b1, W2, b2, G1, g1b, G2, g2b)
    h = _L0_tok_ref(x, L0_tok_W, L0_tok_b)
    h = jnp.concatenate([h, _L0_txt_ref(x_txt, mask_BS_i1_0, pos_BS, mask_BS_i0_1, itok_BS_0_3, mask_BS_i1_0, itok_BS_0_3, itok_BS_0_9, mask_BS_i1_0, itok_BS_0_3, L0_txt_W_word, L0_txt_W_type, L0_txt_W_pos, L0_txt_W_match_ent, L0_txt_W_sf_ent, L0_txt_W_match_tok, L0_txt_W_sf_tok, L0_txt_W_etype, L0_txt_W_atype_ent, L0_txt_W_amatch, L0_txt_ln_gamma, L0_txt_ln_beta)], axis=1)
    h = h + _L0_attn_ref(_layernorm(h, axis=-1), L0_attn_w_qkv, L0_attn_temp, L0_attn_w_out, L0_attn_b_out)
    h = h + _L0_ffn_ref(_layernorm(h, axis=-1), L0_ffn_P, L0_ffn_C, L0_ffn_W1, L0_ffn_b1, L0_ffn_W2, L0_ffn_b2, L0_ffn_G1, L0_ffn_g1b, L0_ffn_G2, L0_ffn_g2b)
    return h

_drawn_inputs = setup_inputs


def setup_inputs(seed=0):
    import zlib

    import numpy as np

    out = dict(_drawn_inputs(seed))
    spreads = {'L0_txt_ln_gamma': (1.0, 0.2),
     'L0_txt_ln_beta': (0.0, 0.1),
     'L0_attn_temp': (1.0, 0.6),
     'L0_attn_b_out': (0.0, 0.1),
     'L0_ffn_b1': (0.0, 0.424),
     'L0_ffn_b2': (0.0, 0.279),
     'L0_ffn_g1b': (0.0, 0.1),
     'L0_ffn_g2b': (0.0, 0.1)}
    factors = {'L0_tok_b': 3.851, 'L0_attn_w_qkv': 8.0, 'L0_attn_w_out': 8.0}
    for name, (base, spread) in spreads.items():
        noise = np.random.default_rng([zlib.crc32(name.encode()), seed]).standard_normal(out[name].shape)
        drawn = base * np.exp(spread * noise) if base else spread * noise
        out[name] = jnp.asarray(drawn.astype(out[name].dtype))
    for name, factor in factors.items():
        out[name] = (out[name] * factor).astype(out[name].dtype)
    return out
```

```python
from contextlib import ExitStack

import numpy as np

import concourse.bass as bass
from concourse import mybir
from concourse.alu_op_type import AluOpType as ALU

ACT = mybir.ActivationFunctionType
AX = mybir.AxisListType
F32 = mybir.dt.float32
BF16 = mybir.dt.bfloat16
I32 = mybir.dt.int32

B = 64
NI, NT = 16, 77
N = NI + NT
TOK = B * N
D = 192
D1 = D - 128
KIN = 768
KC = KIN // 128
JJ = 11
TT = 112
SMALL = 26
HEADS, DH = 12, 64
INNER = HEADS * DH
CH = INNER // 128
UB = 4
UT = UB * N
ST = 124
SUB = UT // ST
UNITS = B // UB
S, R, M, H, G = 8, 16, 64, 32, 64
E = S * M
TN = 496
TILES = TOK // TN
TSUB = TN // ST
STEPS = 32
PAIRS = S // 2
ZP = [0, 0, 0, 1, 1, 2]
WP = [0, 1, 2, 0, 1, 0]
ZROWS = 6 * R + 3
SENTINEL = -3.0e38
ARENA = 38000
CHOSEN = 3.0e38
EPS_TXT, EPS_LN = 1e-12, 1e-5


def wait(eng, sem, value):
    if isinstance(value, int) and value <= 0:
        return
    eng.wait_ge(sem, value)


def build(nc, t):
    with ExitStack() as ctx:
        def sem(name):
            return ctx.enter_context(nc.semaphore(name))

        def sb(name, shape, dt=F32):
            return ctx.enter_context(nc.sbuf_tensor(name, shape, dt))

        h0 = nc.dram_tensor("h0_scratch", (TOK, D), F32, kind="Internal").ap()
        h1d = nc.dram_tensor("h1_scratch", (TOK, D), F32, kind="Internal").ap()
        zq = nc.dram_tensor("z_parts", (3, S * R, TOK), BF16, kind="Internal").ap()
        gq = nc.dram_tensor("gate_parts", (3, E, TOK), BF16, kind="Internal").ap()

        ident = sb("ident", [128, 128])
        w1s = sb("w1_stack", [ZROWS, E * H], BF16)
        w2p = sb("w2_pad", [128, S * 16, 32])
        b2p = sb("b2_pad", [96, S * 2, 3, 32], BF16)
        sel = sb("sel", [96, 8, 128], BF16)
        g1w = sb("g1w", [128, G])
        g1b = sb("g1b", [G, 1])
        g2w = sb("g2w", [G + 1, D])
        arena = sb("arena", [128, ARENA])

        class Carver:
            def __init__(self):
                self.at = 0

            def __call__(self, rows, shape, dt=F32):
                words = int(np.prod(shape)) * (2 if dt == BF16 else 4)
                words = -(-words // 4)
                ap = arena[0:rows, self.at:self.at + words]
                self.at += words
                assert self.at <= ARENA, self.at
                if dt != F32:
                    ap = ap.bitcast(dt)
                if len(shape) > 1:
                    names = "abcd"[:len(shape)]
                    ap = ap.rearrange(f"p ({' '.join(names)}) -> p {' '.join(names)}",
                                      **{n: k for n, k in zip(names, shape)})
                return ap

        banks = [ctx.enter_context(nc.psum_tensor(f"bank{i}", [128, 512], F32)) for i in range(2)]
        pair0 = ctx.enter_context(nc.psum_tensor("pair0", [128, 2, 512], F32))
        pair1 = ctx.enter_context(nc.psum_tensor("pair1", [128, 2, 512], F32))
        banks += [ctx.enter_context(nc.psum_tensor(f"bank{i}", [128, 512], F32)) for i in range(6, 8)]

        c1 = Carver()
        xt = c1(128, [KC, B * NI])
        wtok = c1(128, [KC, D])
        tokb = c1(1, [D])
        ones_row = c1(1, [128])
        wpos = c1(128, [D])
        wsmall = c1(SMALL, [D])
        rowidx = c1(SMALL, [1])
        iota_i = c1(128, [1], I32)
        iota_f = c1(128, [1])
        widx = c1(TT, [JJ * 4], I32)
        wnow = c1(TT, [2, 4], I32)
        pos_ids = c1(128, [B * NT], I32)
        small_ids = c1(SMALL, [B * NT], I32)
        word = c1(TT, [2, 4, D])
        ohp = c1(128, [2, 4, TT])
        ohs = c1(SMALL, [2, 4, TT])
        emb = c1(TT, [2, 4 * D])
        tst = c1(TT, [4, 6])
        tmv = c1(TT, [4, 2])
        tve = c1(TT, [4])
        trs = c1(TT, [4])
        mhalf = c1(TT, [4])
        tnorm = c1(TT, [2, 4, D])
        tgam = c1(TT, [D])
        tbet = c1(TT, [D])
        tmul = c1(TT, [4, D])
        tout = c1(TT, [2, 4, D])
        img = c1(128, [2, D])
        w1f = c1(128, [2048])
        w1r = c1(128, [2048])
        w1h = c1(128, [3, 2048], BF16)
        b1f = c1(128, [128])
        b1r = c1(128, [128])
        b1h = c1(128, [3, 128], BF16)
        w2f = w1r
        b2f = c1(96, [S * 2, R])
        b2r = c1(96, [S * 2, R])

        c2 = Carver()
        wq0, wq1 = c2(128, [INNER]), c2(D1, [INNER])
        wout = c2(128, [CH, D])
        bout = c2(1, [D])
        ones2 = c2(1, [ST])
        tempc = c2(128, [1])
        maskh = c2(128, [CH, HEADS])
        headsel = c2(128, [UB, CH, 128])
        pz0, pz1 = c2(128, [128]), c2(D1, [128])
        cbd = c2(128, [E])
        mh2 = c2(ST, [SUB])
        x0 = c2(ST, [2, SUB, D])
        st = {k: c2(ST, [SUB, 6]) for k in "AG"}
        mv = {k: c2(ST, [SUB, 2]) for k in "AG"}
        ve = {k: c2(ST, [SUB]) for k in "AG"}
        rs = {k: c2(ST, [SUB]) for k in "AG"}
        xn = {k: c2(ST, [SUB, D]) for k in "AG"}
        xt0 = {k: c2(128, [UT]) for k in "AG"}
        xt1 = {k: c2(D1, [UT]) for k in "AG"}
        wv = c2(128, [CH, UT])
        wsq = c2(128, [CH, UT])
        wpi = c2(128, [CH, UT])
        n2 = c2(128, [CH, UB])
        n2m = c2(128, [CH, UB])
        inv = c2(128, [CH, UB])
        lsel = c2(128, [UB, CH, 32])
        lg = c2(128, [N])
        nmax = c2(128, [1])
        pe_ = c2(128, [N])
        psm = c2(128, [1])
        prc = c2(128, [1])
        pi = c2(128, [N + 1])
        pss = c2(128, [1])
        pse = c2(128, [1])
        rsc = c2(128, [CH, UB])
        dots = c2(128, [CH, UB])
        dsc = c2(128, [CH, UB])
        dmi = c2(128, [CH, UB])
        natt = c2(128, [CH, UB])
        h1 = c2(ST, [SUB, D])
        zf = c2(128, [UT])
        zr = c2(128, [UT])
        zh = c2(128, [3, UT], BF16)
        sc = c2(ST, [SUB, S, M + 8])
        v8 = c2(ST, [SUB, S, 8])
        v4 = c2(ST, [SUB, S, 8])
        mr = c2(ST, [SUB, S, M + 8])
        sd = c2(ST, [SUB, E])
        se = c2(ST, [SUB, E])
        gu = c2(ST, [SUB, E])
        gs = c2(ST, [SUB, S])
        gr = c2(ST, [SUB, S])
        gg = c2(ST, [SUB, E])
        grr = c2(128, [SUB, 4, ST])
        gh = c2(128, [3, 4, UT], BF16)

        c3 = Carver()
        gst = c3(96, [4, PAIRS, TN], BF16)
        zst = c3(ZROWS, [2, PAIRS, TN], BF16)
        hid = c3(128, [4, 2, TN])
        gated = c3(128, [4, 4, TN])
        comb = c3(128, [TN])
        y1 = c3(G + 1, [TN])
        h1t = c3(ST, [TSUB, D])
        outt = c3(ST, [2, TSUB, D])

        s_w = sem("weights_loaded")
        s_w1f, s_w2f, s_b2f = sem("w1_raw_loaded"), sem("w2_raw_loaded"), sem("b2_raw_loaded")
        s_const = sem("pool_constants")
        s_cstd = sem("dve_constants")
        s_split = sem("weight_split_steps")
        s_stack = sem("w1_stack_written")
        s_xt = sem("patches_loaded")
        s_tl = sem("text_tables_loaded")
        s_word = [sem("words_gathered0"), sem("words_gathered1")]
        s_oh, s_tps, s_emb, s_tst = sem("onehots_made"), sem("table_rows_summed"), sem("emb_summed"), sem("text_stats")
        s_tmv, s_tve, s_trs, s_tn = sem("text_moments"), sem("text_var_eps"), sem("text_rstd"), sem("text_normed")
        s_tmul, s_to = sem("text_scaled"), sem("text_ready")
        s_todma = [sem("text_stored0"), sem("text_stored1")]
        s_ips, s_iev = sem("image_summed"), sem("image_copied")
        s_idma = [sem("image_stored0"), sem("image_stored1")]
        s_w2l = sem("attention_weights_loaded")
        s_c2 = sem("attention_constants")
        s_c2d = sem("attention_constants_dve")

        s_x0 = sem("x0_loaded")
        s_st = {k: sem(f"stats_{k}") for k in "AG"}
        s_mv = {k: sem(f"moments_{k}") for k in "AG"}
        s_ve = {k: sem(f"var_eps_{k}") for k in "AG"}
        s_rs = {k: sem(f"rstd_{k}") for k in "AG"}
        s_xn = {k: sem(f"normed_{k}") for k in "AG"}
        s_tp = {k: sem(f"transposed_{k}") for k in "AG"}
        s_xt_ = {k: sem(f"xT_copied_{k}") for k in "AG"}
        s_wp = sem("w_product")
        s_wv, s_wsq = sem("w_copied"), sem("w_squared")
        s_n2, s_nm, s_inv, s_L = sem("norms_summed"), sem("norms_floored"), sem("norms_inverted"), sem("head_weights")
        s_lg, s_lt, s_lm, s_pe = sem("logits"), sem("logits_tempered"), sem("logits_max"), sem("logits_exp")
        s_pr, s_pi, s_ps, s_pse, s_pix = (sem("pi_recip"), sem("pi_made"), sem("pi_sum"), sem("pi_sum_eps"),
                                          sem("pi_complete"))
        s_pb = sem("pi_spread")
        s_wpi, s_rsc = sem("w_pi"), sem("pi_scale_copied")
        s_w2pi = sem("w2_pi")
        s_dt, s_ds, s_dm, s_na = sem("dots_summed"), sem("dots_scaled"), sem("dots_negated"), sem("neg_attn")
        s_o, s_hp, s_h1, s_h1d = sem("attended"), sem("out_product"), sem("h1_ready"), sem("h1_stored")
        s_z, s_zf, s_z1, s_zr, s_z2, s_z3, s_zd = (sem("z_product"), sem("z_copied"), sem("z_part1"), sem("z_rest"),
                                                   sem("z_part2"), sem("z_part3"), sem("z_stored"))
        s_sp, s_sc, s_v8, s_v4, s_mr = (sem("scores"), sem("scores_copied"), sem("top8"), sem("top4"),
                                        sem("chosen_marked"))
        s_sd, s_se, s_gu, s_gs, s_gr, s_gg = (sem("scores_shifted"), sem("scores_exp"), sem("gates_raw"),
                                              sem("gates_summed"), sem("gates_recip"), sem("gates_ready"))
        s_gt, s_g1, s_grr, s_g2, s_g3, s_gd = (sem("gates_transposed"), sem("gate_part1"), sem("gate_rest"),
                                               sem("gate_part2"), sem("gate_part3"), sem("gates_stored"))

        s_gl = [sem(f"gates_loaded{q}") for q in range(4)]
        s_zl = [sem(f"codes_loaded{q}") for q in range(2)]
        s_ones = sem("one_rows_set")
        s_hp1, s_hid = sem("hidden_product"), sem("hidden_gelu")
        s_gb, s_gat = sem("gates_spread"), sem("hidden_gated")
        s_code, s_comb = sem("chunk_decoded"), sem("code_copied")
        s_f1, s_y1, s_f2, s_out = sem("g1_product"), sem("g1_gelu"), sem("g2_product"), sem("out_added")
        s_h1l, s_od = sem("h1_loaded"), [sem("out_stored0"), sem("out_stored1")]

        def wait_apart(eng, *waits):
            held = [(sm, v if isinstance(v, int) else eng.to_reg(v)) for sm, v in waits]
            if any(not isinstance(v, int) for _, v in held):
                eng.wait_ge(s_const, 1)
            for sm, v in held:
                wait(eng, sm, v)

        h0_b = h0.rearrange("(b n) d -> b n d", b=B)
        h0_u = h0.rearrange("(u s p) d -> u p s d", s=SUB, p=ST)
        h1_u = h1d.rearrange("(u s p) d -> u p s d", s=SUB, p=ST)
        h1_t = h1d.rearrange("(u s p) d -> u p s d", s=TSUB, p=ST)
        out_t = t["out"].rearrange("b n d -> (b n) d").rearrange("(u s p) d -> u p s d", s=TSUB, p=ST)
        gq_w = gq.rearrange("p (q e) t -> p e q t", e=128)
        gq_r = gq.rearrange("p (j o f m) t -> p o f m j t", j=PAIRS, o=2, f=2)
        zq_r = zq.rearrange("p (j o r) t -> p o r j t", j=PAIRS, o=2)

        s_b2s = sem("b2_rest")
        s_wnow = sem("word_indices_placed")
        s_bp = sem("bias_product")

        def stage1_over(eng):
            wait(eng, s_todma[0], 64 * 6)
            wait(eng, s_todma[1], 64 * 5)
            wait(eng, s_idma[0], 16 * 4)
            wait(eng, s_idma[1], 16 * 4)
            wait(eng, s_stack, 16 * 9)
            wait(eng, s_split, 8)

        def stage2_over(eng):
            wait(eng, s_h1d, 16 * UNITS)
            wait(eng, s_zd, 48 * UNITS)
            wait(eng, s_gd, 48 * UNITS)

        block = ctx.enter_context(nc.Block())

        @block.sync
        def _(sp):
            sp.dma_start(wtok, t["tok_w"].rearrange("(c p) e -> p c e", p=128)).then_inc(s_xt, 16)
            sp.dma_start(xt, t["x"].rearrange("(c p) n -> p c n", p=128)).then_inc(s_xt, 16)
            sp.dma_start(tokb, t["tok_b"]).then_inc(s_xt, 16)
            sp.dma_start(pos_ids, t["pos_ids"][0:1, :].to_broadcast([128, B * NT])).then_inc(s_tl, 16)
            sp.dma_start(small_ids, t["small_ids"]).then_inc(s_tl, 16)
            sp.dma_start(rowidx, t["row_index"]).then_inc(s_tl, 16)
            sp.dma_start(wpos, t["w_pos"]).then_inc(s_tl, 16)
            sp.dma_start(wsmall, t["w_small"]).then_inc(s_tl, 16)
            sp.dma_start(tgam, t["gamma"][0:1, :].to_broadcast([TT, D])).then_inc(s_tl, 16)
            sp.dma_start(tbet, t["beta"][0:1, :].to_broadcast([TT, D])).then_inc(s_tl, 16)
            sp.dma_start(w1f, t["w1"]).then_inc(s_w1f, 16)
            sp.dma_start(b1f, t["b1"]).then_inc(s_w1f, 16)
            for p in range(3):
                sp.dma_start(b2f[32 * p:32 * p + 32], t["b2"]).then_inc(s_b2f, 16)
            sp.dma_start(g1w[:], t["g1"]).then_inc(s_w, 16)
            sp.dma_start(g1b[:], t["g1b"]).then_inc(s_w, 16)
            sp.dma_start(g2w[0:G], t["g2"]).then_inc(s_w, 16)
            sp.dma_start(g2w[G:G + 1], t["g2b"]).then_inc(s_w, 16)

            def store_text(jj, par):
                wait(sp, s_to, jj + 1)
                for bb in range(4):
                    dst = h0_b[16 * bb:16 * bb + 16, bass.ds(NI + 7 * jj, 7), :]
                    sp.dma_start(dst, tout[:, par, bb]).then_inc(s_todma[par], 16)

            store_text(0, 0)
            wait(sp, s_split, 4)
            for i in range(6):
                sp.dma_start(w1s[R * i:R * i + R].rearrange("r (s x) -> r s x", s=S),
                             w1h[:, WP[i]]).then_inc(s_stack, 16)
            for p in range(3):
                sp.dma_start(w1s[6 * R + p:6 * R + p + 1], b1h[:, p]).then_inc(s_stack, 16)
            sp.dma_start(w2f, t["w2"]).then_inc(s_w2f, 16)
            store_text(1, 1)
            store_text(2, 0)
            with sp.Fori(0, 4) as pr:
                store_text(2 * pr + 3, 1)
                store_text(2 * pr + 4, 0)

            stage1_over(sp)
            sp.dma_start(wq0, t["w_qkv"][0:128]).then_inc(s_w2l, 16)
            sp.dma_start(wq1, t["w_qkv"][128:D]).then_inc(s_w2l, 16)
            sp.dma_start(wout, t["w_out"].rearrange("(c p) e -> p c e", p=128)).then_inc(s_w2l, 16)
            sp.dma_start(bout, t["b_out"]).then_inc(s_w2l, 16)
            sp.dma_start(pz0, t["pz"][0:128]).then_inc(s_w2l, 16)
            sp.dma_start(pz1, t["pz"][128:D]).then_inc(s_w2l, 16)
            wait(sp, s_c2d, 1)
            for b in range(UB):
                sp.dma_start(tempc[32 * b:32 * b + HEADS], t["temp"]).then_inc(s_w2l, 16)
            for s in range(S):
                sp.dma_start(cbd[R * s:R * s + R, M * s:M * s + M], t["ct"][R * s:R * s + R]).then_inc(s_w2l, 16)

            def load_x0(u, slot):
                wait_apart(sp, (s_x0, 16 * u))
                wait(sp, s_h1, u - 1)
                sp.dma_start(x0[:, slot], h0_u[u]).then_inc(s_x0, 16)

            load_x0(0, 0)
            load_x0(1, 1)

            def store_h1(u):
                wait(sp, s_h1, u + 1)
                sp.dma_start(h1_u[u], h1).then_inc(s_h1d, 16)

            def store_codes(u):
                wait(sp, s_z3, u + 1)
                for p in range(3):
                    sp.dma_start(zq[p, :, bass.ds(u * UT, UT)], zh[:, p]).then_inc(s_zd, 16)

            def store_gates(u):
                wait(sp, s_g3, SUB * (u + 1))
                for p in range(3):
                    sp.dma_start(gq_w[p, :, :, bass.ds(u * UT, UT)], gh[:, p]).then_inc(s_gd, 16)

            def unit_sp(u, slot):
                load_x0(u + 1, slot)
                store_codes(u - 1)
                store_gates(u - 1)
                store_h1(u)

            store_h1(0)
            unit_sp(1, 0)
            with sp.Fori(0, (UNITS - 4) // 2) as i:
                unit_sp(2 * i + 2, 1)
                unit_sp(2 * i + 3, 0)
            unit_sp(UNITS - 2, 1)
            store_codes(UNITS - 2)
            store_gates(UNITS - 2)
            store_h1(UNITS - 1)
            store_codes(UNITS - 1)
            store_gates(UNITS - 1)

            stage2_over(sp)

            def load_codes(tile, half):
                for i in range(6):
                    sp.dma_start(zst[R * i:R * i + R, half],
                                 zq_r[ZP[i], half, :, :, bass.ds(tile * TN, TN)]).then_inc(s_zl[half], 16)

            def load_gates(tile, q):
                for p in range(3):
                    sp.dma_start(gst[32 * p:32 * p + 32, q],
                                 gq_r[p, q // 2, q % 2, :, :, bass.ds(tile * TN, TN)]).then_inc(s_gl[q], 16)

            def load_h1(tile):
                wait(sp, s_out, TSUB // 2 * tile)
                sp.dma_start(h1t, h1_t[tile]).then_inc(s_h1l, 16)

            def store_out(tile, par):
                wait(sp, s_out, TSUB // 2 * (tile + 1))
                sp.dma_start(out_t[tile], outt[:, par]).then_inc(s_od[par], 16)

            load_codes(0, 0)
            for q in range(4):
                load_gates(0, q)
                if q == 1:
                    load_codes(0, 1)
            load_h1(0)
            for par in range(2):
                sp.sem_inc(s_od[par], 16)

            def refill(tile, q):
                wait_apart(sp, (s_gb, 128 * (tile - 1) + 32 * (q + 1)), (s_bp, 4 * (tile - 1) + q + 1))
                load_gates(tile, q)
                if q % 2 == 1:
                    load_codes(tile, q // 2)

            refill(1, 0)
            refill(1, 1)
            refill(1, 2)
            refill(1, 3)
            with sp.Fori(0, (TILES - 2) // 2) as i:
                for k in range(2):
                    tile = 2 * i + 1 + k
                    store_out(tile - 1, k % 2)
                    load_h1(tile)
                    for q in range(4):
                        refill(tile + 1, q)
            store_out(TILES - 2, 0)
            load_h1(TILES - 1)
            store_out(TILES - 1, 1)
            for par in range(2):
                wait(sp, s_od[par], 16 * (TILES // 2 + 1))

        @block.gpsimd
        def _(pool):
            p_ = nc.gpsimd
            pool.dma_start(widx, t["word_ids"]).then_inc(s_word[0], 16)
            p_.iota(iota_i, pattern=[[0, 1]], base=0, channel_multiplier=1).then_inc(s_const, 1)
            p_.memset(ident[:], 0.0).then_inc(s_const, 1)
            p_.memset(sel[:], 0.0).then_inc(s_const, 1)
            p_.memset(ones_row, 1.0)
            p_.memset(mhalf, -0.5).then_inc(s_const, 1)
            pool.wait_ge(s_const, 4)
            p_.affine_select(out=ident[:], in_=ident[:], compare_op=ALU.not_equal, fill=1.0, base=0,
                             pattern=[[-1, 128]], channel_multiplier=1).then_inc(s_const, 1)
            for p in range(3):
                pool.wait_ge(s_const, 5 + p)
                v = sel[32 * p:32 * p + 32].rearrange("p k (e h) -> p k e h", e=4)
                p_.affine_select(out=v, in_=v, compare_op=ALU.not_equal, fill=1.0, base=0,
                                 pattern=[[-4, 8], [-1, 4], [0, 32]], channel_multiplier=1).then_inc(s_const, 1)
            pool.wait_ge(s_const, 8)
            p_.memset(w2p[:], 0.0)
            p_.memset(b2p[:], 0.0).then_inc(s_const, 1)

            def gather(jj, par):
                wait_apart(pool, (s_emb, jj - 1))
                p_.tensor_copy(wnow[:, par], widx[:, bass.ds(4 * jj, 4)]).then_inc(s_wnow, 1)
                wait_apart(pool, (s_wnow, jj + 1))
                for bb in range(4):
                    p_.indirect_dma_start(
                        word[:, par, bb], None, t["w_word"],
                        bass.IndirectOffsetOnAxis(ap=wnow[:, par, bb:bb + 1], axis=0)).then_inc(s_word[par], 16)

            def text_rows(jj, par):
                wait_apart(pool, (s_tmv, jj + 1))
                p_.tensor_scalar_add(tve, tmv[:, :, 1], EPS_TXT).then_inc(s_tve, 1)
                wait(pool, s_tve, jj + 1)
                p_.tensor_tensor(trs, tve, mhalf, ALU.pow).then_inc(s_trs, 1)
                wait(pool, s_tn, jj + 1)
                p_.tensor_tensor(tmul, tnorm[:, par], tgam.unsqueeze(1).to_broadcast([TT, 4, D]),
                                 ALU.mult).then_inc(s_tmul, 1)
                wait(pool, s_tmul, jj + 1)
                wait(pool, s_todma[par], use_count(jj, par))
                p_.tensor_tensor(tout[:, par], tmul, tbet.unsqueeze(1).to_broadcast([TT, 4, D]),
                                 ALU.add).then_inc(s_to, 1)

            def use_count(jj, par):
                if isinstance(jj, int):
                    return 64 * (jj // 2)
                return 32 * (jj - par)

            pool.wait_ge(s_word[0], 16)
            gather(0, 0)
            gather(1, 1)
            pool.wait_ge(s_tl, 16 * 7)
            text_rows(0, 0)
            wait(pool, s_cstd, 3)
            p_.tensor_tensor(w1r, w1f, w1h[:, 0], ALU.subtract)
            p_.tensor_tensor(b1r, b1f, b1h[:, 0], ALU.subtract).then_inc(s_split, 1)
            pool.wait_ge(s_split, 1)
            p_.tensor_copy(w1h[:, 1], w1r)
            p_.tensor_copy(b1h[:, 1], b1r).then_inc(s_split, 1)
            pool.wait_ge(s_split, 2)
            p_.tensor_tensor(w1h[:, 2], w1r, w1h[:, 1], ALU.subtract)
            p_.tensor_tensor(b1h[:, 2], b1r, b1h[:, 1], ALU.subtract).then_inc(s_split, 2)
            gather(2, 0)
            for jj in (1, 2):
                text_rows(jj, jj % 2)
                gather(jj + 2, jj % 2)
            with pool.Fori(0, 3) as pr:
                for k in range(2):
                    jj = 2 * pr + 3 + k
                    text_rows(jj, 1 - k)
                    gather(jj + 2, 1 - k)
            text_rows(9, 1)
            text_rows(10, 0)
            pool.wait_ge(s_w2f, 16)
            w2v = w2f.rearrange("p (j o g r) -> p j o g r", j=PAIRS, o=2, g=16)
            w2o = w2p[:].rearrange("p (j o g) c -> p j o g c", j=PAIRS, o=2)
            pool.wait_ge(s_const, 9)
            for o in range(2):
                last = p_.tensor_copy(w2o[:, :, o, :, 16 * o:16 * o + 16], w2v[:, :, o])
            last.then_inc(s_split, 1)
            pool.wait_ge(s_b2f, 48)
            b2v = b2f.rearrange("p (j o f) r -> p j o f r", j=PAIRS, o=2)
            b2w = b2r.rearrange("p (j o f) r -> p j o f r", j=PAIRS, o=2)
            b2o = b2p[:].rearrange("p (j o f) q c -> p j o f q c", j=PAIRS, o=2)
            src = b2v
            for part in range(3):
                for o in range(2):
                    last = p_.tensor_copy(b2o[:, :, o, :, part, 16 * o:16 * o + 16], src[:, :, o])
                last.then_inc(s_split, 1)
                if part == 2:
                    break
                pool.wait_ge(s_split, 6 + part if part == 0 else 7)
                if part == 0:
                    for o in range(2):
                        last = p_.tensor_tensor(b2w[:, :, o], b2v[:, :, o],
                                                b2o[:, :, o, :, 0, 16 * o:16 * o + 16], ALU.subtract)
                else:
                    for o in range(2):
                        last = p_.tensor_tensor(b2w[:, :, o], b2w[:, :, o],
                                                b2o[:, :, o, :, 1, 16 * o:16 * o + 16], ALU.subtract)
                last.then_inc(s_b2s, 1)
                pool.wait_ge(s_b2s, part + 1)
                src = b2w

            stage1_over(pool)
            p_.memset(maskh, 0.0)
            p_.memset(headsel, 0.0)
            p_.memset(ones2, 1.0)
            p_.memset(lsel, 0.0)
            p_.memset(mh2, -0.5).then_inc(s_c2, 1)
            for o in range(2):
                pool.wait_ge(s_c2, 1 + o)
                v = maskh[64 * o:64 * o + 64]
                p_.affine_select(out=v, in_=v, compare_op=ALU.not_equal, fill=1.0, base=-o,
                                 pattern=[[-2, CH], [1, HEADS]], channel_multiplier=0).then_inc(s_c2, 1)
            for b in range(UB):
                pool.wait_ge(s_c2, 3 + b)
                v = headsel[32 * b:32 * b + 32, b].rearrange("p c (o d) -> p c o d", o=2)
                p_.affine_select(out=v, in_=v, compare_op=ALU.not_equal, fill=1.0, base=0,
                                 pattern=[[-2, CH], [-1, 2], [0, DH]], channel_multiplier=1).then_inc(s_c2, 1)
            pool.wait_ge(s_c2, 7)

            def rstd(k, u, eps):
                wait_apart(pool, (s_mv[k], u + 1), (s_xn[k], u))
                p_.tensor_scalar_add(ve[k], mv[k][:, :, 1], eps).then_inc(s_ve[k], 1)
                wait(pool, s_ve[k], u + 1)
                p_.tensor_tensor(rs[k], ve[k], mh2, ALU.pow).then_inc(s_rs[k], 1)

            def z_parts(u):
                wait(pool, s_z1, u + 1)
                wait(pool, s_zd, 48 * u)
                p_.tensor_tensor(zr, zf, zh[:, 0], ALU.subtract).then_inc(s_zr, 1)
                wait_apart(pool, (s_zr, u + 1))
                p_.tensor_copy(zh[:, 1], zr).then_inc(s_z2, 1)
                wait(pool, s_z2, u + 1)
                p_.tensor_tensor(zh[:, 2], zr, zh[:, 1], ALU.subtract).then_inc(s_z3, 1)

            def shift(u, s):
                wait(pool, s_v8, SUB * u + s + 1)
                wait(pool, s_se, SUB * u)
                p_.tensor_tensor(sd[:, s].rearrange("p (a b) -> p a b", a=S), sc[:, s, :, 0:M],
                                 v8[:, s, :, 0:1].to_broadcast([ST, S, M]), ALU.subtract).then_inc(s_sd, 1)

            def gates(u, s):
                wait(pool, s_gr, SUB * u + s + 1)
                wait(pool, s_gt, SUB * u)
                p_.tensor_tensor(gg[:, s].rearrange("p (a b) -> p a b", a=S),
                                 gu[:, s].rearrange("p (a b) -> p a b", a=S),
                                 gr[:, s].unsqueeze(2).to_broadcast([ST, S, M]), ALU.mult).then_inc(s_gg, 1)

            def gate_parts(u, s):
                n = SUB * u + s
                wait_apart(pool, (s_grr, n + 1))
                p_.tensor_copy(gh[:, 1, :, ST * s:ST * s + ST], grr[:, s]).then_inc(s_g2, 1)
                wait_apart(pool, (s_g2, n + 1))
                p_.tensor_tensor(gh[:, 2, :, ST * s:ST * s + ST], grr[:, s],
                                 gh[:, 1, :, ST * s:ST * s + ST], ALU.subtract).then_inc(s_g3, 1)

            def unit_pool(u, do_a, do_g):
                if do_a:
                    rstd("A", u, EPS_LN)
                if do_g:
                    rstd("G", u - 1, EPS_LN)
                    z_parts(u - 1)
                    for s in range(SUB):
                        shift(u - 1, s)
                    gates(u - 1, 0)
                if do_a:
                    wait(pool, s_lg, u + 1)
                    for c in range(CH):
                        wait(pool, s_wpi, CH * u + c + 1)
                        p_.tensor_tensor(wsq[:, c], wpi[:, c], wv[:, c], ALU.mult).then_inc(s_w2pi, 1)
                if do_g:
                    gates(u - 1, 1)
                    gates(u - 1, 2)
                if do_a:
                    wait(pool, s_na, u + 1)
                    wait(pool, s_w2pi, CH * (u + 1))
                    for c in range(CH):
                        p_.tensor_tensor(wv[:, c].rearrange("p (b n) -> p b n", b=UB),
                                         wpi[:, c].rearrange("p (b n) -> p b n", b=UB),
                                         natt[:, c].unsqueeze(2).to_broadcast([128, UB, N]),
                                         ALU.mult).then_inc(s_o, 1)
                if do_g:
                    for s in range(SUB):
                        gate_parts(u - 1, s)

            unit_pool(0, True, False)
            unit_pool(1, True, True)
            with pool.Fori(2, UNITS) as u:
                unit_pool(u, True, True)
            unit_pool(UNITS, False, True)
            stage2_over(pool)
            p_.memset(zst[96:ZROWS], 1.0).then_inc(s_ones, 1)
            pool.wait_ge(s_ones, 1)
            p_.memset(y1[G:G + 1], 1.0).then_inc(s_ones, 1)

        @block.scalar
        def _(act):
            a_ = nc.scalar
            for k in range(8):
                wait(act, s_ips, k + 1)
                wait(act, s_idma[k % 2], 16 * (k // 2))
                a_.copy(img[:, k % 2], banks[k % 2][:, 0:D]).then_inc(s_iev, 1)
                wait(act, s_iev, k + 1)
                act.dma_start(h0_b[8 * k:8 * k + 8, 0:NI, :], img[:, k % 2]).then_inc(s_idma[k % 2], 16)

            stage1_over(act)

            def xT(k, u):
                wait(act, s_tp[k], u + 1)
                a_.copy(xt0[k], banks[0][:, 0:UT])
                a_.copy(xt1[k], banks[1][0:D1, 0:UT]).then_inc(s_xt_[k], 1)

            def w_copy(u, c):
                wait(act, s_wp, CH * u + c + 1)
                if c == 0:
                    wait(act, s_hp, u)
                    wait(act, s_dt, CH * u)
                src = pair0[:, c % 2, 0:UT]
                a_.copy(wv[:, c], src).then_inc(s_wv, 1)
                a_.activation(wsq[:, c], src, ACT.Square).then_inc(s_wsq, 1)

            def unit_act(u, do_a, do_g):
                if do_a:
                    xT("A", u)
                if do_g:
                    xT("G", u - 1)
                if do_a:
                    w_copy(u, 0)
                    w_copy(u, 1)
                if do_g:
                    wait(act, s_z, u)
                    wait(act, s_zd, 48 * (u - 1))
                    wait(act, s_z3, u - 1)
                    a_.copy(zf, pair1[:, 1, 0:UT]).then_inc(s_zf, 1)
                    a_.copy(zh[:, 0], pair1[:, 1, 0:UT]).then_inc(s_z1, 1)
                if do_a:
                    for c in range(2, CH):
                        w_copy(u, c)
                if do_g:
                    for s in range(SUB):
                        n = SUB * (u - 1) + s
                        wait(act, s_sp, n + 1)
                        wait(act, s_mr, n - s)
                        wait(act, s_sd, n - s)
                        a_.copy(sc[:, s, :, 0:M],
                                banks[2][0:ST, :].rearrange("p (a b) -> p a b", a=S)).then_inc(s_sc, 1)
                if do_a:
                    wait(act, s_lm, u + 1)
                    a_.activation(pe_, lg, ACT.Exp, bias=nmax, accum_out=psm).then_inc(s_pe, 1)
                if do_g:
                    for s in range(SUB):
                        n = SUB * (u - 1) + s
                        wait(act, s_sd, n + 1)
                        wait(act, s_gu, n - s)
                        a_.activation(se[:, s], sd[:, s], ACT.Exp).then_inc(s_se, 1)
                    for s in range(SUB):
                        n = SUB * (u - 1) + s
                        wait(act, s_gt, n + 1)
                        if s == 0:
                            wait(act, s_gd, 48 * (u - 1))
                        a_.copy(gh[:, 0, :, ST * s:ST * s + ST],
                                pair1[:, 1, 0:4 * ST].rearrange("p (a b) -> p a b", a=4)).then_inc(s_g1, 1)

            unit_act(0, True, False)
            unit_act(1, True, True)
            with act.Fori(2, UNITS) as u:
                unit_act(u, True, True)
            unit_act(UNITS, False, True)

            stage2_over(act)
            wait(act, s_ones, 2)
            wait(act, s_w, 64)

            def gelu(tile, m):
                n = 64 * tile + m
                wait(act, s_hp1, n + 1)
                wait(act, s_gat, 2 * (n - 4) + 2)
                a_.activation(hid[:, m % 4], (pair0, pair1)[m % 2][:, :, 0:TN],
                              ACT.Gelu_apprx_tanh).then_inc(s_hid, 1)

            def copy_code(tile):
                wait(act, s_code, STEPS * (tile + 1))
                a_.copy(comb, banks[2][:, 0:TN]).then_inc(s_comb, 1)

            def gelu_out(tile):
                wait(act, s_f1, tile + 1)
                a_.activation(y1[0:G], banks[3][0:G, 0:TN], ACT.Gelu_apprx_tanh, bias=g1b[:]).then_inc(s_y1, 1)

            def tile_act(tile, first):
                for step in range(STEPS):
                    gelu(tile, 2 * step)
                    gelu(tile, 2 * step + 1)
                    if not first and step == 1:
                        copy_code(tile - 1)
                    if not first and step == 3:
                        gelu_out(tile - 1)

            tile_act(0, True)
            with act.Fori(1, TILES) as tile:
                tile_act(tile, False)
            copy_code(TILES - 1)
            gelu_out(TILES - 1)

        @block.vector
        def _(dve):
            v_ = nc.vector
            dve.wait_ge(s_const, 1)
            v_.tensor_copy(iota_f, iota_i).then_inc(s_cstd, 1)
            dve.wait_ge(s_tl, 16 * 7)
            v_.tensor_scalar(small_ids[0:2], small_ids[0:2], 0, None, ALU.is_gt).then_inc(s_cstd, 1)
            dve.wait_ge(s_cstd, 2)

            def onehots(jj, par):
                wait(dve, s_tps, jj - 1)
                v_.tensor_scalar(ohp[:, par].rearrange("p a b -> p (a b)"), pos_ids[:, bass.ds(jj * 448, 448)],
                                 iota_f, None, ALU.is_equal)
                v_.tensor_scalar(ohs[:, par].rearrange("p a b -> p (a b)"), small_ids[:, bass.ds(jj * 448, 448)],
                                 rowidx, None, ALU.is_equal).then_inc(s_oh, 1)

            def words(jj, par, base=0):
                wait(dve, s_tps, jj + 1)
                if isinstance(jj, int):
                    uses = jj // 2 + 1
                    wait(dve, s_word[par], 64 * uses + (16 if par == 0 else 0))
                else:
                    wait(dve, s_word[par], 32 * (jj - par) + 64 + (16 if par == 0 else 0))
                v_.tensor_tensor(emb[:, par].rearrange("p (a b) -> p a b", a=2),
                                 (pair0, pair1)[par][0:TT, :, 0:2 * D],
                                 word[:, par].rearrange("p (a b) d -> p a (b d)", a=2), ALU.add).then_inc(s_emb, 1)
                wait(dve, s_emb, jj + 1)
                for bb in range(4):
                    last = v_.bn_stats(tst[:, bb], emb[:, par, D * bb:D * bb + D])
                last.then_inc(s_tst, 1)
                wait_apart(dve, (s_tst, jj + 1))
                for bb in range(4):
                    last = v_.bn_aggr(tmv[:, bb], tst[:, bb])
                last.then_inc(s_tmv, 1)

            def normed(jj, par):
                wait(dve, s_trs, jj + 1)
                wait(dve, s_tmul, jj - 1)
                for bb in range(4):
                    last = v_.tensor_scalar(tnorm[:, par, bb], emb[:, par, D * bb:D * bb + D], tmv[:, bb, 0:1],
                                            trs[:, bb:bb + 1], ALU.subtract, ALU.mult)
                last.then_inc(s_tn, 1)

            onehots(0, 0)
            words(0, 0)
            normed(0, 0)
            dve.wait_ge(s_w1f, 32)
            v_.tensor_copy(w1h[:, 0], w1f)
            v_.tensor_copy(b1h[:, 0], b1f).then_inc(s_cstd, 1)
            for jj in (1, 2):
                onehots(jj, jj % 2)
                words(jj, jj % 2)
                normed(jj, jj % 2)
            with dve.Fori(0, 4) as pr:
                for k in range(2):
                    jj = 2 * pr + 3 + k
                    onehots(jj, 1 - k)
                    words(jj, 1 - k)
                    normed(jj, 1 - k)

            stage1_over(dve)
            v_.memset(tempc, 0.0)
            v_.memset(cbd, 0.0).then_inc(s_c2d, 1)
            v_.memset(sc[:, :, :, M:M + 8], SENTINEL)
            v_.memset(v4, SENTINEL).then_inc(s_c2d, 1)
            dve.wait_ge(s_c2, 7)
            dve.wait_ge(s_c2d, 2)
            dve.wait_ge(s_w2l, 16 * (6 + UB + S))

            def stats(k, u, src):
                for s in range(SUB):
                    last = v_.bn_stats(st[k][:, s], src[:, s])
                last.then_inc(s_st[k], 1)
                wait_apart(dve, (s_st[k], u + 1))
                for s in range(SUB):
                    last = v_.bn_aggr(mv[k][:, s], st[k][:, s])
                last.then_inc(s_mv[k], 1)

            def norm(k, u, src):
                wait(dve, s_rs[k], u + 1)
                wait(dve, s_tp[k], u)
                for s in range(SUB):
                    last = v_.tensor_scalar(xn[k][:, s], src[:, s], mv[k][:, s, 0:1], rs[k][:, s:s + 1],
                                            ALU.subtract, ALU.mult)
                last.then_inc(s_xn[k], 1)

            def top(u, s):
                n = SUB * u + s
                wait_apart(dve, (s_sc, n + 1), (s_sd, n - s))
                for g in range(S):
                    last = v_.max(v8[:, s, g], sc[:, s, g, 0:M])
                last.then_inc(s_v8, 1)
                wait(dve, s_v8, n + 1)
                v_.tensor_copy(v4[:, s, :, 0:4], v8[:, s, :, 0:4]).then_inc(s_v4, 1)
                wait_apart(dve, (s_v4, n + 1))
                for g in range(S):
                    last = v_.match_replace(mr[:, s, g], v4[:, s, g], sc[:, s, g], CHOSEN)
                last.then_inc(s_mr, 1)

            def raw(u, s):
                n = SUB * u + s
                wait(dve, s_se, n + 1)
                wait(dve, s_mr, n + 1)
                wait(dve, s_gg, n - s)
                v_.scalar_tensor_tensor(out=gu[:, s].rearrange("p (a b) -> p a b", a=S), in0=mr[:, s, :, 0:M],
                                        scalar=CHOSEN, in1=se[:, s].rearrange("p (a b) -> p a b", a=S),
                                        op0=ALU.is_equal, op1=ALU.mult).then_inc(s_gu, 1)
                wait(dve, s_gu, n + 1)
                v_.tensor_reduce(gs[:, s], gu[:, s].rearrange("p (a b) -> p a b", a=S), AX.X, ALU.add).then_inc(s_gs, 1)
                wait(dve, s_gs, n + 1)
                v_.reciprocal(gr[:, s], gs[:, s]).then_inc(s_gr, 1)

            def rest(u, s):
                n = SUB * u + s
                wait(dve, s_g1, n + 1)
                wait(dve, s_g3, n - s)
                v_.tensor_tensor(grr[:, s], pair1[:, 1, 0:4 * ST].rearrange("p (a b) -> p a b", a=4),
                                 gh[:, 0, :, ST * s:ST * s + ST], ALU.subtract).then_inc(s_grr, 1)

            def unit_dve(u, slot, do_a, do_g):
                if do_a:
                    wait(dve, s_x0, 16 * (u + 1))
                    stats("A", u, x0[:, slot])
                if do_g:
                    wait(dve, s_h1, u)
                    stats("G", u - 1, h1)
                if do_a:
                    norm("A", u, x0[:, slot])
                if do_g:
                    norm("G", u - 1, h1)
                if do_a:
                    for c in range(CH):
                        wait(dve, s_wsq, CH * u + c + 1)
                        v_.tensor_reduce(n2[:, c], wsq[:, c].rearrange("p (b n) -> p b n", b=UB), AX.X,
                                         ALU.add).then_inc(s_n2, 1)
                    wait(dve, s_n2, CH * (u + 1))
                    v_.tensor_scalar(n2m, n2, 1e-24, None, ALU.max).then_inc(s_nm, 1)
                    wait(dve, s_nm, u + 1)
                    v_.reciprocal(inv, n2m).then_inc(s_inv, 1)
                    wait(dve, s_inv, u + 1)
                    for b in range(UB):
                        last = v_.tensor_tensor(lsel[:, b, :, 0:HEADS], maskh,
                                                inv[:, :, b:b + 1].to_broadcast([128, CH, HEADS]), ALU.mult)
                    last.then_inc(s_L, 1)
                if do_g:
                    top(u - 1, 0)
                if do_a:
                    wait(dve, s_lg, u + 1)
                    v_.tensor_scalar(lg, pair1[:, 0, 0:N], tempc, None, ALU.mult).then_inc(s_lt, 1)
                    wait(dve, s_lt, u + 1)
                    v_.tensor_reduce(nmax, lg, AX.X, ALU.max, negate=True).then_inc(s_lm, 1)
                if do_g:
                    top(u - 1, 1)
                if do_a:
                    wait(dve, s_pe, u + 1)
                    v_.reciprocal(prc, psm).then_inc(s_pr, 1)
                    wait(dve, s_pr, u + 1)
                    v_.tensor_scalar(pi[:, 0:N], pe_, prc, None, ALU.mult).then_inc(s_pi, 1)
                    wait(dve, s_pi, u + 1)
                    v_.tensor_reduce(pss, pi[:, 0:N], AX.X, ALU.add).then_inc(s_ps, 1)
                    wait(dve, s_ps, u + 1)
                    v_.tensor_scalar(pse, pss, 1e-8, None, ALU.add).then_inc(s_pse, 1)
                    wait(dve, s_pse, u + 1)
                    v_.reciprocal(pi[:, N:N + 1], pse).then_inc(s_pix, 1)
                if do_g:
                    top(u - 1, 2)
                    raw(u - 1, 0)
                if do_a:
                    for c in range(CH):
                        wait(dve, s_pb, CH * u + c + 1)
                        pb = pair0[:, c % 2, 0:UB * (N + 1)].rearrange("p (b n) -> p b n", b=UB)
                        v_.tensor_tensor(wpi[:, c].rearrange("p (b n) -> p b n", b=UB),
                                         wv[:, c].rearrange("p (b n) -> p b n", b=UB), pb[:, :, 0:N],
                                         ALU.mult).then_inc(s_wpi, 1)
                        v_.tensor_copy(rsc[:, c], pb[:, :, N]).then_inc(s_rsc, 1)
                if do_g:
                    raw(u - 1, 1)
                    raw(u - 1, 2)
                if do_a:
                    for c in range(CH):
                        wait(dve, s_w2pi, CH * u + c + 1)
                        v_.tensor_reduce(dots[:, c], wsq[:, c].rearrange("p (b n) -> p b n", b=UB), AX.X,
                                         ALU.add).then_inc(s_dt, 1)
                    wait(dve, s_dt, CH * (u + 1))
                    wait(dve, s_rsc, CH * (u + 1))
                    v_.tensor_tensor(dsc, dots, rsc, ALU.mult).then_inc(s_ds, 1)
                    wait(dve, s_ds, u + 1)
                    v_.tensor_scalar(dmi, dsc, -1.0, -1.0, ALU.mult, ALU.add).then_inc(s_dm, 1)
                    wait(dve, s_dm, u + 1)
                    v_.reciprocal(natt, dmi).then_inc(s_na, 1)
                if do_g:
                    for s in range(SUB):
                        rest(u - 1, s)
                if do_a:
                    wait(dve, s_hp, u + 1)
                    wait(dve, s_h1d, 16 * u)
                    v_.tensor_tensor(h1[:, 0:2], banks[3][0:ST, 0:2 * D].rearrange("p (a b) -> p a b", a=2),
                                     x0[:, slot, 0:2], ALU.add)
                    v_.tensor_tensor(h1[:, 2], pair1[0:ST, 0, 128:128 + D], x0[:, slot, 2], ALU.add).then_inc(s_h1, 1)

            unit_dve(0, 0, True, False)
            unit_dve(1, 1, True, True)
            with dve.Fori(0, (UNITS - 2) // 2) as i:
                unit_dve(2 * i + 2, 0, True, True)
                unit_dve(2 * i + 3, 1, True, True)
            unit_dve(UNITS, 0, False, True)

            stage2_over(dve)

            def gate_chunk(tile, c):
                n = 128 * tile + c
                if c % 2 == 0:
                    wait(dve, s_hid, 64 * tile + c // 2 + 1)
                wait(dve, s_gb, n + 1)
                if c % 4 == 0:
                    wait(dve, s_code, STEPS * tile + c // 4 - 3)
                v_.tensor_tensor(gated[:, c // 4 % 4, c % 4], hid[:, c // 2 % 4, c % 2],
                                 banks[c % 2][:, 0:TN], ALU.mult).then_inc(s_gat, 1)

            def add_out(tile, half, par):
                wait(dve, s_f2, 2 * tile + half + 1)
                if half == 0:
                    wait(dve, s_h1l, 16 * (tile + 1))
                    if isinstance(tile, int):
                        wait(dve, s_od[par], 16 * (tile // 2 + 1))
                    else:
                        wait(dve, s_od[par], 8 * (tile - par) + 16)
                v_.tensor_tensor(outt[:, par, 2 * half:2 * half + 2],
                                 banks[3][0:ST, 0:2 * D].rearrange("p (a b) -> p a b", a=2),
                                 h1t[:, 2 * half:2 * half + 2], ALU.add).then_inc(s_out, 1)

            def tile_dve(tile, par, first):
                for step in range(STEPS):
                    for j in range(4):
                        gate_chunk(tile, 4 * step + j)
                    if not first and step == 5:
                        add_out(tile - 1, 0, 1 - par)
                    if not first and step == 7:
                        add_out(tile - 1, 1, 1 - par)

            tile_dve(0, 0, True)
            with dve.Fori(0, (TILES - 2) // 2) as i:
                for k in range(2):
                    tile_dve(2 * i + 1 + k, 1 - k, False)
            tile_dve(TILES - 1, 1, False)
            add_out(TILES - 1, 0, 1)
            add_out(TILES - 1, 1, 1)

        @block.tensor
        def _(pe):
            t_ = nc.tensor
            pe.wait_ge(s_xt, 48)
            pe.wait_ge(s_const, 5)
            for k in range(8):
                wait(pe, s_iev, k - 1)
                for c in range(KC):
                    t_.matmul(banks[k % 2][:, 0:D], xt[:, c, 128 * k:128 * k + 128], wtok[:, c],
                              start=(c == 0), stop=False)
                t_.matmul(banks[k % 2][:, 0:D], ones_row, tokb, start=False, stop=True).then_inc(s_ips, 1)

            pe.wait_ge(s_tl, 16 * 7)

            def tables(jj, par):
                wait(pe, s_oh, jj + 1)
                wait(pe, s_emb, jj - 1)
                for bb in range(4):
                    o = (pair0, pair1)[par][0:TT, bb // 2, D * (bb % 2):D * (bb % 2) + D]
                    t_.matmul(o, ohp[:, par, bb], wpos, start=True, stop=False)
                    last = t_.matmul(o, ohs[:, par, bb], wsmall, start=False, stop=True)
                last.then_inc(s_tps, 1)

            tables(0, 0)
            tables(1, 1)
            tables(2, 0)
            with pe.Fori(0, 4) as pr:
                tables(2 * pr + 3, 1)
                tables(2 * pr + 4, 0)

            stage1_over(pe)
            pe.wait_ge(s_c2, 7)
            pe.wait_ge(s_w2l, 16 * (6 + UB + S))

            def transposes(k, u, other_done):
                wait(pe, s_xn[k], u + 1)
                wait(pe, *other_done)
                for s in range(SUB):
                    t_.transpose(banks[0][:, ST * s:ST * s + ST], xn[k][:, s, 0:128], ident[0:ST, 0:ST])
                    last = t_.transpose(banks[1][0:D1, ST * s:ST * s + ST], xn[k][:, s, 128:D],
                                        ident[0:ST, 0:ST])
                last.then_inc(s_tp[k], 1)

            def w_product(u, c):
                if c == 0:
                    wait(pe, s_xt_["A"], u + 1)
                if c < 2:
                    wait(pe, s_rsc, CH * (u - 1) + 5 + c)
                else:
                    wait(pe, s_wsq, CH * u + c - 1)
                o = pair0[:, c % 2, 0:UT]
                t_.matmul(o, wq0[:, 128 * c:128 * c + 128], xt0["A"], start=True, stop=False)
                t_.matmul(o, wq1[:, 128 * c:128 * c + 128], xt1["A"], start=False, stop=True).then_inc(s_wp, 1)

            def unit_pe(u, do_a, do_g):
                if do_a:
                    transposes("A", u, (s_xt_["G"], u - 1))
                if do_g:
                    if do_a:
                        transposes("G", u - 1, (s_xt_["A"], u + 1))
                    else:
                        transposes("G", u - 1, (s_xt_["G"], u - 1))
                if do_a:
                    w_product(u, 0)
                    w_product(u, 1)
                if do_g:
                    wait(pe, s_xt_["G"], u)
                    wait(pe, s_grr, SUB * (u - 1))
                    t_.matmul(pair1[:, 1, 0:UT], pz0, xt0["G"], start=True, stop=False)
                    t_.matmul(pair1[:, 1, 0:UT], pz1, xt1["G"], start=False, stop=True).then_inc(s_z, 1)
                if do_a:
                    for c in range(2, CH):
                        w_product(u, c)
                if do_g:
                    wait(pe, s_zf, u)
                    for s in range(SUB):
                        wait(pe, s_sc, SUB * (u - 1) + s)
                        t_.matmul(banks[2][0:ST, :], zf[:, ST * s:ST * s + ST], cbd, start=True,
                                  stop=True).then_inc(s_sp, 1)
                if do_a:
                    wait(pe, s_L, u + 1)
                    wait(pe, s_h1, u)
                    for b in range(UB):
                        for c in range(CH):
                            last = t_.matmul(pair1[32 * b:32 * b + 32, 0, 0:N], lsel[:, b, c],
                                             wsq[:, c, N * b:N * b + N], start=(c == 0), stop=(c == CH - 1))
                    last.then_inc(s_lg, 1)
                    wait(pe, s_pix, u + 1)
                    for c in range(CH):
                        if c < 2:
                            wait(pe, s_wsq, CH * u + 5 + c)
                        else:
                            wait(pe, s_rsc, CH * u + c - 1)
                        for b in range(UB):
                            last = t_.matmul(pair0[:, c % 2, (N + 1) * b:(N + 1) * (b + 1)], headsel[:, b, c],
                                             pi, start=True, stop=True)
                        last.then_inc(s_pb, 1)
                if do_g:
                    wait(pe, s_z1, u)
                    for s in range(SUB):
                        n = SUB * (u - 1) + s
                        wait(pe, s_gg, n + 1)
                        wait(pe, s_grr, n)
                        for q in range(4):
                            last = t_.transpose(pair1[:, 1, ST * q:ST * q + ST], gg[:, s, 128 * q:128 * q + 128],
                                                ident[0:ST, 0:ST])
                        last.then_inc(s_gt, 1)
                if do_a:
                    wait(pe, s_o, CH * (u + 1))
                    wait(pe, s_lt, u + 1)
                    for s in range(SUB):
                        o = banks[3][0:ST, D * s:D * s + D] if s < 2 else pair1[0:ST, 0, 128:128 + D]
                        for c in range(CH):
                            t_.matmul(o, wv[:, c, ST * s:ST * s + ST], wout[:, c], start=(c == 0), stop=False)
                        last = t_.matmul(o, ones2, bout, start=False, stop=True)
                    last.then_inc(s_hp, 1)

            unit_pe(0, True, False)
            unit_pe(1, True, True)
            with pe.Fori(2, UNITS) as u:
                unit_pe(u, True, True)
            unit_pe(UNITS, False, True)

            stage2_over(pe)
            pe.wait_ge(s_ones, 2)
            pe.wait_ge(s_w, 64)

            def chunk_of(step, j):
                return 2 * j + step // 16, step % 16

            def hidden(tile, step):
                q = step // 8
                if step % 16 == 0:
                    wait(pe, s_zl[q // 2], 96 * (tile + 1))
                for j in range(4):
                    s, g = chunk_of(step, j)
                    if j % 2 == 0:
                        wait(pe, s_hid, 64 * tile + 2 * step + j // 2 - 1)
                    x = (16 * s + g) * 128
                    mm = t_.matmul((pair0, pair1)[j // 2][:, j % 2, 0:TN], w1s[:, x:x + 128],
                                   zst[:, q // 2, j], start=True, stop=True)
                    if j % 2 == 1:
                        mm.then_inc(s_hp1, 1)

            def spread(tile, step):
                q = step // 8
                if step % 8 == 0:
                    wait(pe, s_gl[q], 48 * (tile + 1))
                for j in range(4):
                    n = 128 * tile + 4 * step + j
                    wait(pe, s_gat, n - 1)
                    t_.matmul(banks[j % 2][:, 0:TN], sel[:, step % 8], gst[:, q, j],
                              start=True, stop=True).then_inc(s_gb, 1)

            def bias(tile, q):
                for j in range(4):
                    blk = (2 * j + q // 2) * 2 + q % 2
                    for part in range(3):
                        mm = t_.matmul(banks[2][32 * j:32 * j + 32, 0:TN], b2p[:, blk, part], gst[:, q, j],
                                       start=(q == 0 and part == 0), stop=False, skip_group_check=True)
                mm.then_inc(s_bp, 1)

            def decode(tile, step):
                wait(pe, s_gat, 128 * tile + 4 * step + 4)
                for j in range(4):
                    s, g = chunk_of(step, j)
                    mm = t_.matmul(banks[2][32 * j:32 * j + 32, 0:TN], w2p[:, 16 * s + g], gated[:, step % 4, j],
                                   start=False, stop=(step == STEPS - 1), skip_group_check=True)
                mm.then_inc(s_code, 1)

            def out1(tile):
                wait(pe, s_comb, tile + 1)
                wait(pe, s_out, 2 * tile)
                t_.matmul(banks[3][0:G, 0:TN], g1w[:], comb, start=True, stop=True).then_inc(s_f1, 1)

            def out2(tile, half):
                wait(pe, s_y1, tile + 1)
                if half == 1:
                    wait(pe, s_out, 2 * tile + 1)
                for k in range(2):
                    x = ST * (2 * half + k)
                    mm = t_.matmul(banks[3][0:ST, D * k:D * k + D], y1[:, x:x + ST], g2w[:], start=True, stop=True)
                mm.then_inc(s_f2, 1)

            def tile_pe(tile, first):
                for step in range(STEPS):
                    hidden(tile, step)
                    spread(tile, step)
                    if step < 2:
                        if not first:
                            decode(tile - 1, STEPS - 2 + step)
                    else:
                        if step == 2:
                            if not first:
                                wait(pe, s_comb, tile)
                            bias(tile, 0)
                        decode(tile, step - 2)
                        if step % 8 == 0:
                            bias(tile, step // 8)
                    if not first:
                        if step == 3:
                            out1(tile - 1)
                        if step == 5:
                            out2(tile - 1, 0)
                        if step == 7:
                            out2(tile - 1, 1)

            tile_pe(0, True)
            with pe.Fori(1, TILES) as tile:
                tile_pe(tile, False)
            decode(TILES - 1, STEPS - 2)
            decode(TILES - 1, STEPS - 1)
            out1(TILES - 1)
            out2(TILES - 1, 0)
            out2(TILES - 1, 1)


def kernel(**inputs):
    import concourse.bacc as bacc
    from concourse.bass_utils import run_bass_kernel_spmd as run

    a = {k: np.ascontiguousarray(v) for k, v in inputs.items()}

    def ids(x):
        return x.reshape(4, 16, 11, 7).transpose(2, 0, 1, 3)

    m10, m01 = a["mask_BS_i1_0"], a["mask_BS_i0_1"]
    i3, i9 = a["itok_BS_0_3"], a["itok_BS_0_9"]
    tables = [("L0_txt_W_type", m10), ("L0_txt_W_match_tok", m10), ("L0_txt_W_match_ent", m01),
              ("L0_txt_W_sf_tok", i3), ("L0_txt_W_sf_ent", i3), ("L0_txt_W_etype", i9),
              ("L0_txt_W_atype_ent", m10)]
    rows = [a[n].shape[0] for n, _ in tables]
    arrays = {
        "x": a["x"].reshape(64, 3, 4, 16, 4, 16).transpose(1, 3, 5, 0, 2, 4).reshape(768, 1024),
        "tok_w": a["L0_tok_W"].T,
        "tok_b": a["L0_tok_b"].reshape(1, -1),
        "word_ids": ids(a["x_txt"]).transpose(2, 3, 0, 1).reshape(112, 44),
        "pos_ids": ids(a["pos_BS"]).reshape(1, -1),
        "small_ids": np.concatenate([np.repeat(ids(i).reshape(1, -1), r, 0) for (_, i), r in zip(tables, rows)]),
        "row_index": np.concatenate([np.arange(r) for r in rows]).astype(np.float32).reshape(-1, 1),
        "w_word": a["L0_txt_W_word"],
        "w_pos": a["L0_txt_W_pos"],
        "w_small": np.concatenate([a[n] for n, _ in tables]),
        "gamma": a["L0_txt_ln_gamma"].reshape(1, -1),
        "beta": a["L0_txt_ln_beta"].reshape(1, -1),
        "w_qkv": a["L0_attn_w_qkv"],
        "temp": a["L0_attn_temp"],
        "w_out": a["L0_attn_w_out"],
        "b_out": a["L0_attn_b_out"].reshape(1, -1),
        "pz": a["L0_ffn_P"].transpose(1, 0, 2).reshape(192, 128),
        "ct": a["L0_ffn_C"].transpose(0, 2, 1).reshape(128, 64),
        "w1": a["L0_ffn_W1"].transpose(2, 0, 1, 3).reshape(128, 2048),
        "b1": a["L0_ffn_b1"].reshape(128, 128),
        "w2": a["L0_ffn_W2"].reshape(8, 16, 128, 16).transpose(2, 0, 1, 3).reshape(128, 2048),
        "b2": a["L0_ffn_b2"].reshape(8, 2, 32, 16).transpose(2, 0, 1, 3).reshape(32, 16, 16),
        "g1": a["L0_ffn_G1"],
        "g1b": a["L0_ffn_g1b"].reshape(-1, 1),
        "g2": a["L0_ffn_G2"],
        "g2b": a["L0_ffn_g2b"].reshape(1, -1),
    }
    nc = bacc.Bacc("TRN2", target_bir_lowering=False, num_devices=1)
    feed, t = {}, {}
    for name, v in arrays.items():
        v = np.ascontiguousarray(v)
        feed["in_" + name] = v
        t[name] = nc.dram_tensor("in_" + name, v.shape, mybir.dt.from_np(v.dtype), kind="ExternalInput").ap()
    t["out"] = nc.dram_tensor("out_h", (B, N, D), F32, kind="ExternalOutput").ap()
    build(nc, t)
    r = run(nc, [feed], core_ids=[0])
    return r.results[0]["out_h"]
```

```python
from contextlib import ExitStack

import numpy as np

import concourse.bass as bass
from concourse import mybir
from concourse.alu_op_type import AluOpType as ALU

ACT = mybir.ActivationFunctionType
AX = mybir.AxisListType
F32 = mybir.dt.float32
BF16 = mybir.dt.bfloat16
I32 = mybir.dt.int32

B = 64
NI, NT = 16, 77
N = NI + NT
TOK = B * N
D = 192
D1 = D - 128
KIN = 768
KC = KIN // 128
JJ = 11
TT = 112
SMALL = 26
HEADS, DH = 12, 64
INNER = HEADS * DH
CH = INNER // 128
UB = 4
UT = UB * N
ST = 124
SUB = UT // ST
UNITS = B // UB
S, R, M, H, G = 8, 16, 64, 32, 64
E = S * M
TN = 496
TILES = TOK // TN
TSUB = TN // ST
EB, KH = M // 16, H // 8
PAIRS = S // 2
BLOCKS = 2 * EB
QUADS = BLOCKS * PAIRS
ZP = [0, 0, 0, 1, 1, 2]
WP = [0, 1, 2, 0, 1, 0]
ZROWS = 6 * R + 3
SENTINEL = -3.0e38
ARENA = 38000
CHOSEN = 3.0e38
EPS_TXT, EPS_LN = 1e-12, 1e-5
OUT1_AT, OUT2_AT = 8, (11, 13)


def wait(eng, sem, value):
    if isinstance(value, int) and value <= 0:
        return
    eng.wait_ge(sem, value)


def build(nc, t):
    with ExitStack() as ctx:
        def sem(name):
            return ctx.enter_context(nc.semaphore(name))

        def sb(name, shape, dt=F32):
            return ctx.enter_context(nc.sbuf_tensor(name, shape, dt))

        h0 = nc.dram_tensor("h0_scratch", (TOK, D), F32, kind="Internal").ap()
        h1d = nc.dram_tensor("h1_scratch", (TOK, D), F32, kind="Internal").ap()
        zq = nc.dram_tensor("z_parts", (3, S * R, TOK), BF16, kind="Internal").ap()
        bq = nc.dram_tensor("bias_codes", (S * R, TOK), F32, kind="Internal").ap()
        gq = nc.dram_tensor("gate_parts", (3, E, TOK), BF16, kind="Internal").ap()

        ident = sb("ident", [128, 128])
        w1s = sb("w1_stack", [ZROWS, E * H], BF16)
        w2p = sb("w2_pad", [128, S * 16, 32])
        b2p = sb("b2_pad", [128, PAIRS, 3, 32], BF16)
        sel = sb("sel", [128, 128], BF16)
        g1w = sb("g1w", [128, G])
        g1b = sb("g1b", [G, 1])
        g2w = sb("g2w", [G + 1, D])
        arena = sb("arena", [128, ARENA])

        class Carver:
            def __init__(self):
                self.at = 0

            def __call__(self, rows, shape, dt=F32):
                words = int(np.prod(shape)) * (2 if dt == BF16 else 4)
                words = -(-words // 4)
                ap = arena[0:rows, self.at:self.at + words]
                self.at += words
                assert self.at <= ARENA, self.at
                if dt != F32:
                    ap = ap.bitcast(dt)
                if len(shape) > 1:
                    names = "abcd"[:len(shape)]
                    ap = ap.rearrange(f"p ({' '.join(names)}) -> p {' '.join(names)}",
                                      **{n: k for n, k in zip(names, shape)})
                return ap

        banks = [ctx.enter_context(nc.psum_tensor(f"bank{i}", [128, 512], F32)) for i in range(2)]
        pair0 = ctx.enter_context(nc.psum_tensor("pair0", [128, 2, 512], F32))
        pair1 = ctx.enter_context(nc.psum_tensor("pair1", [128, 2, 512], F32))
        banks += [ctx.enter_context(nc.psum_tensor(f"bank{i}", [128, 512], F32)) for i in range(6, 8)]

        c1 = Carver()
        xt = c1(128, [KC, B * NI])
        wtok = c1(128, [KC, D])
        tokb = c1(1, [D])
        ones_row = c1(1, [128])
        wpos = c1(128, [D])
        wsmall = c1(SMALL, [D])
        rowidx = c1(SMALL, [1])
        iota_i = c1(128, [1], I32)
        iota_f = c1(128, [1])
        widx = c1(TT, [JJ * 4], I32)
        wnow = c1(TT, [2, 4], I32)
        pos_ids = c1(128, [B * NT], I32)
        small_ids = c1(SMALL, [B * NT], I32)
        word = c1(TT, [2, 4, D])
        ohp = c1(128, [2, 4, TT])
        ohs = c1(SMALL, [2, 4, TT])
        emb = c1(TT, [2, 4 * D])
        tst = c1(TT, [4, 6])
        tmv = c1(TT, [4, 2])
        tve = c1(TT, [4])
        trs = c1(TT, [4])
        mhalf = c1(TT, [4])
        tnorm = c1(TT, [2, 4, D])
        tgam = c1(TT, [D])
        tbet = c1(TT, [D])
        tmul = c1(TT, [4, D])
        tout = c1(TT, [2, 4, D])
        img = c1(128, [2, D])
        w1f = c1(128, [2048])
        w1r = c1(128, [2048])
        w1h = c1(128, [3, 2048], BF16)
        b1f = c1(128, [128])
        b1r = c1(128, [128])
        b1h = c1(128, [3, 128], BF16)
        w2f = w1r
        b2f = c1(128, [PAIRS, R])
        b2r = c1(128, [PAIRS, R])

        c2 = Carver()
        wq0, wq1 = c2(128, [INNER]), c2(D1, [INNER])
        wout = c2(128, [CH, D])
        bout = c2(1, [D])
        ones2 = c2(1, [ST])
        tempc = c2(128, [1])
        maskh = c2(128, [CH, HEADS])
        headsel = c2(128, [UB, CH, 128])
        pz0, pz1 = c2(128, [128]), c2(D1, [128])
        cbd = c2(128, [E])
        mh2 = c2(ST, [SUB])
        x0 = c2(ST, [2, SUB, D])
        st = {k: c2(ST, [SUB, 6]) for k in "AG"}
        mv = {k: c2(ST, [SUB, 2]) for k in "AG"}
        ve = {k: c2(ST, [SUB]) for k in "AG"}
        rs = {k: c2(ST, [SUB]) for k in "AG"}
        xn = {k: c2(ST, [SUB, D]) for k in "AG"}
        xt0 = {k: c2(128, [UT]) for k in "AG"}
        xt1 = {k: c2(D1, [UT]) for k in "AG"}
        wv = c2(128, [CH, UT])
        wsq = c2(128, [CH, UT])
        wpi = c2(128, [CH, UT])
        n2 = c2(128, [CH, UB])
        n2m = c2(128, [CH, UB])
        inv = c2(128, [CH, UB])
        lsel = c2(128, [UB, CH, 32])
        lg = c2(128, [N])
        nmax = c2(128, [1])
        pe_ = c2(128, [N])
        psm = c2(128, [1])
        prc = c2(128, [1])
        pi = c2(128, [N + 1])
        pss = c2(128, [1])
        pse = c2(128, [1])
        rsc = c2(128, [CH, UB])
        dots = c2(128, [CH, UB])
        dsc = c2(128, [CH, UB])
        dmi = c2(128, [CH, UB])
        natt = c2(128, [CH, UB])
        h1 = c2(ST, [SUB, D])
        zf = c2(128, [UT])
        zr = c2(128, [UT])
        zh = c2(128, [3, UT], BF16)
        sc = c2(ST, [SUB, S, M + 8])
        v8 = c2(ST, [SUB, S, 8])
        v4 = c2(ST, [SUB, S, 8])
        mr = c2(ST, [SUB, S, M + 8])
        sd = c2(ST, [SUB, E])
        se = c2(ST, [SUB, E])
        gu = c2(ST, [SUB, E])
        gs = c2(ST, [SUB, S])
        gr = c2(ST, [SUB, S])
        gg = c2(ST, [SUB, E])
        grr = c2(128, [SUB, 4, ST])
        gh = c2(128, [3, 4, UT], BF16)
        bt = c2(128, [UT])

        c3 = Carver()
        gst = c3(128, [8, 2, TN], BF16)
        zst = c3(ZROWS, [2, PAIRS, TN], BF16)
        hid = c3(128, [4, KH, TN])
        gated = c3(128, [2, PAIRS, KH, TN])
        comb = c3(128, [TN])
        code = c3(128, [TN])
        y1 = c3(G + 1, [TN])
        bias_t = c3(128, [TN])
        h1t = c3(ST, [TSUB, D])
        outt = c3(ST, [2, TSUB, D])

        s_w = sem("weights_loaded")
        s_w1f, s_w2f, s_b2f = sem("w1_raw_loaded"), sem("w2_raw_loaded"), sem("b2_raw_loaded")
        s_const = sem("pool_constants")
        s_cstd = sem("dve_constants")
        s_split = sem("weight_split_steps")
        s_stack = sem("w1_stack_written")
        s_xt = sem("patches_loaded")
        s_tl = sem("text_tables_loaded")
        s_word = [sem("words_gathered0"), sem("words_gathered1")]
        s_oh, s_tps, s_emb, s_tst = sem("onehots_made"), sem("table_rows_summed"), sem("emb_summed"), sem("text_stats")
        s_tmv, s_tve, s_trs, s_tn = sem("text_moments"), sem("text_var_eps"), sem("text_rstd"), sem("text_normed")
        s_tmul, s_to = sem("text_scaled"), sem("text_ready")
        s_todma = [sem("text_stored0"), sem("text_stored1")]
        s_ips, s_iev = sem("image_summed"), sem("image_copied")
        s_idma = [sem("image_stored0"), sem("image_stored1")]
        s_w2l = sem("attention_weights_loaded")
        s_c2 = sem("attention_constants")
        s_c2d = sem("attention_constants_dve")

        s_x0 = sem("x0_loaded")
        s_st = {k: sem(f"stats_{k}") for k in "AG"}
        s_mv = {k: sem(f"moments_{k}") for k in "AG"}
        s_ve = {k: sem(f"var_eps_{k}") for k in "AG"}
        s_rs = {k: sem(f"rstd_{k}") for k in "AG"}
        s_xn = {k: sem(f"normed_{k}") for k in "AG"}
        s_tp = {k: sem(f"transposed_{k}") for k in "AG"}
        s_xt_ = {k: sem(f"xT_copied_{k}") for k in "AG"}
        s_wp = sem("w_product")
        s_wv, s_wsq = sem("w_copied"), sem("w_squared")
        s_n2, s_nm, s_inv, s_L = sem("norms_summed"), sem("norms_floored"), sem("norms_inverted"), sem("head_weights")
        s_lg, s_lt, s_lm, s_pe = sem("logits"), sem("logits_tempered"), sem("logits_max"), sem("logits_exp")
        s_pr, s_pi, s_ps, s_pse, s_pix = (sem("pi_recip"), sem("pi_made"), sem("pi_sum"), sem("pi_sum_eps"),
                                          sem("pi_complete"))
        s_pb = sem("pi_spread")
        s_wpi, s_rsc = sem("w_pi"), sem("pi_scale_copied")
        s_w2pi = sem("w2_pi")
        s_dt, s_ds, s_dm, s_na = sem("dots_summed"), sem("dots_scaled"), sem("dots_negated"), sem("neg_attn")
        s_o, s_hp, s_h1, s_h1d = sem("attended"), sem("out_product"), sem("h1_ready"), sem("h1_stored")
        s_z, s_zf, s_z1, s_zr, s_z2, s_z3, s_zd = (sem("z_product"), sem("z_copied"), sem("z_part1"), sem("z_rest"),
                                                   sem("z_part2"), sem("z_part3"), sem("z_stored"))
        s_sp, s_sc, s_v8, s_v4, s_mr = (sem("scores"), sem("scores_copied"), sem("top8"), sem("top4"),
                                        sem("chosen_marked"))
        s_sd, s_se, s_gu, s_gs, s_gr, s_gg = (sem("scores_shifted"), sem("scores_exp"), sem("gates_raw"),
                                              sem("gates_summed"), sem("gates_recip"), sem("gates_ready"))
        s_gt, s_g1, s_grr, s_g2, s_g3, s_gd = (sem("gates_transposed"), sem("gate_part1"), sem("gate_rest"),
                                               sem("gate_part2"), sem("gate_part3"), sem("gates_stored"))

        s_gl = [sem(f"gates_loaded{q}") for q in range(4)]
        s_zl = [sem(f"codes_loaded{q}") for q in range(2)]
        s_ones = sem("one_rows_set")
        s_hp1, s_hid = sem("hidden_product"), sem("hidden_gelu")
        s_gb, s_gat = sem("gates_spread"), sem("hidden_gated")
        s_code, s_comb = sem("chunk_decoded"), sem("code_copied")
        s_f1, s_y1, s_f2, s_out = sem("g1_product"), sem("g1_gelu"), sem("g2_product"), sem("out_added")
        s_h1l, s_od = sem("h1_loaded"), [sem("out_stored0"), sem("out_stored1")]

        def wait_apart(eng, *waits):
            held = [(sm, v if isinstance(v, int) else eng.to_reg(v)) for sm, v in waits]
            if any(not isinstance(v, int) for _, v in held):
                eng.wait_ge(s_const, 1)
            for sm, v in held:
                wait(eng, sm, v)

        gate_banks, code_bank, out_bank = banks[0:2], banks[3], banks[2]

        def chunk(s, block, k):
            return (s * EB + block) * KH + k

        h0_b = h0.rearrange("(b n) d -> b n d", b=B)
        h0_u = h0.rearrange("(u s p) d -> u p s d", s=SUB, p=ST)
        h1_u = h1d.rearrange("(u s p) d -> u p s d", s=SUB, p=ST)
        h1_t = h1d.rearrange("(u s p) d -> u p s d", s=TSUB, p=ST)
        out_t = t["out"].rearrange("b n d -> (b n) d").rearrange("(u s p) d -> u p s d", s=TSUB, p=ST)
        gq_w = gq.rearrange("p (q e) t -> p e q t", e=128)
        gq_r = gq.rearrange("p (j a o f b m) t -> p a o f b m j t", j=2, a=2, o=2, f=2, b=2)
        zq_r = zq.rearrange("p (j o r) t -> p o r j t", j=PAIRS, o=2)

        s_b2s = sem("b2_rest")
        s_wnow = sem("word_indices_placed")
        s_bp, s_bt, s_bd, s_bl = (sem("bias_product"), sem("bias_copied"), sem("bias_stored"),
                                  sem("bias_loaded"))
        s_cb = sem("bias_added")

        def stage1_over(eng):
            wait(eng, s_todma[0], 64 * 6)
            wait(eng, s_todma[1], 64 * 5)
            wait(eng, s_idma[0], 16 * 4)
            wait(eng, s_idma[1], 16 * 4)
            wait(eng, s_stack, 16 * 9)
            wait(eng, s_split, 5)
            wait(eng, s_b2s, 10)

        def stage2_over(eng):
            wait(eng, s_h1d, 16 * UNITS)
            wait(eng, s_zd, 48 * UNITS)
            wait(eng, s_gd, 48 * UNITS)
            wait(eng, s_bd, 16 * UNITS)

        block = ctx.enter_context(nc.Block())

        @block.sync
        def _(sp):
            sp.dma_start(wtok, t["tok_w"].rearrange("(c p) e -> p c e", p=128)).then_inc(s_xt, 16)
            sp.dma_start(xt, t["x"].rearrange("(c p) n -> p c n", p=128)).then_inc(s_xt, 16)
            sp.dma_start(tokb, t["tok_b"]).then_inc(s_xt, 16)
            sp.dma_start(pos_ids, t["pos_ids"][0:1, :].to_broadcast([128, B * NT])).then_inc(s_tl, 16)
            sp.dma_start(small_ids, t["small_ids"]).then_inc(s_tl, 16)
            sp.dma_start(rowidx, t["row_index"]).then_inc(s_tl, 16)
            sp.dma_start(wpos, t["w_pos"]).then_inc(s_tl, 16)
            sp.dma_start(wsmall, t["w_small"]).then_inc(s_tl, 16)
            sp.dma_start(tgam, t["gamma"][0:1, :].to_broadcast([TT, D])).then_inc(s_tl, 16)
            sp.dma_start(tbet, t["beta"][0:1, :].to_broadcast([TT, D])).then_inc(s_tl, 16)
            sp.dma_start(w1f, t["w1"]).then_inc(s_w1f, 16)
            sp.dma_start(b1f, t["b1"]).then_inc(s_w1f, 16)
            sp.dma_start(b2f, t["b2"]).then_inc(s_b2f, 16)
            sp.dma_start(g1w[:], t["g1"]).then_inc(s_w, 16)
            sp.dma_start(g1b[:], t["g1b"]).then_inc(s_w, 16)
            sp.dma_start(g2w[0:G], t["g2"]).then_inc(s_w, 16)
            sp.dma_start(g2w[G:G + 1], t["g2b"]).then_inc(s_w, 16)

            def store_text(jj, par):
                wait_apart(sp, (s_to, jj + 1))
                for bb in range(4):
                    dst = h0_b[16 * bb:16 * bb + 16, bass.ds(NI + 7 * jj, 7), :]
                    sp.dma_start(dst, tout[:, par, bb]).then_inc(s_todma[par], 16)

            store_text(0, 0)
            wait_apart(sp, (s_split, 4))
            for i in range(6):
                sp.dma_start(w1s[R * i:R * i + R].rearrange("r (s x) -> r s x", s=S),
                             w1h[:, WP[i]]).then_inc(s_stack, 16)
            for p in range(3):
                sp.dma_start(w1s[6 * R + p:6 * R + p + 1], b1h[:, p]).then_inc(s_stack, 16)
            sp.dma_start(w2f, t["w2"]).then_inc(s_w2f, 16)
            store_text(1, 1)
            store_text(2, 0)
            with sp.Fori(0, 4) as pr:
                store_text(2 * pr + 3, 1)
                store_text(2 * pr + 4, 0)

            stage1_over(sp)
            sp.dma_start(wq0, t["w_qkv"][0:128]).then_inc(s_w2l, 16)
            sp.dma_start(wq1, t["w_qkv"][128:D]).then_inc(s_w2l, 16)
            sp.dma_start(wout, t["w_out"].rearrange("(c p) e -> p c e", p=128)).then_inc(s_w2l, 16)
            sp.dma_start(bout, t["b_out"]).then_inc(s_w2l, 16)
            sp.dma_start(pz0, t["pz"][0:128]).then_inc(s_w2l, 16)
            sp.dma_start(pz1, t["pz"][128:D]).then_inc(s_w2l, 16)
            wait_apart(sp, (s_c2d, 1))
            for b in range(UB):
                sp.dma_start(tempc[32 * b:32 * b + HEADS], t["temp"]).then_inc(s_w2l, 16)
            for s in range(S):
                sp.dma_start(cbd[R * s:R * s + R, M * s:M * s + M], t["ct"][R * s:R * s + R]).then_inc(s_w2l, 16)

            def load_x0(u, slot):
                wait_apart(sp, (s_x0, 16 * u))
                wait_apart(sp, (s_h1, u - 1))
                sp.dma_start(x0[:, slot], h0_u[u]).then_inc(s_x0, 16)

            load_x0(0, 0)
            load_x0(1, 1)

            def store_h1(u):
                wait_apart(sp, (s_h1, u + 1))
                sp.dma_start(h1_u[u], h1).then_inc(s_h1d, 16)

            def store_codes(u):
                wait_apart(sp, (s_z3, u + 1))
                for p in range(3):
                    sp.dma_start(zq[p, :, bass.ds(u * UT, UT)], zh[:, p]).then_inc(s_zd, 16)

            def store_gates(u):
                wait_apart(sp, (s_g3, SUB * (u + 1)))
                for p in range(3):
                    sp.dma_start(gq_w[p, :, :, bass.ds(u * UT, UT)], gh[:, p]).then_inc(s_gd, 16)

            def store_bias(u):
                wait_apart(sp, (s_bt, u + 1))
                sp.dma_start(bq[:, bass.ds(u * UT, UT)], bt).then_inc(s_bd, 16)

            def unit_sp(u, slot):
                if not isinstance(u, int) or u >= 2:
                    store_bias(u - 2)
                load_x0(u + 1, slot)
                store_codes(u - 1)
                store_gates(u - 1)
                store_h1(u)

            store_h1(0)
            unit_sp(1, 0)
            with sp.Fori(0, (UNITS - 4) // 2) as i:
                unit_sp(2 * i + 2, 1)
                unit_sp(2 * i + 3, 0)
            unit_sp(UNITS - 2, 1)
            store_bias(UNITS - 3)
            store_codes(UNITS - 2)
            store_gates(UNITS - 2)
            store_h1(UNITS - 1)
            store_bias(UNITS - 2)
            store_codes(UNITS - 1)
            store_gates(UNITS - 1)
            store_bias(UNITS - 1)

            stage2_over(sp)

            def load_codes(tile, half):
                for i in range(6):
                    sp.dma_start(zst[R * i:R * i + R, half],
                                 zq_r[ZP[i], half, :, :, bass.ds(tile * TN, TN)]).then_inc(s_zl[half], 16)

            def load_gates(tile, q):
                for p in range(3):
                    for a in range(2):
                        for b in range(2):
                            r = 64 * a + 16 * p
                            sp.dma_start(gst[r:r + 16, 2 * q + b],
                                         gq_r[p, a, q // 2, q % 2, b, :, :, bass.ds(tile * TN, TN)]
                                         ).then_inc(s_gl[q], 16)

            def load_bias(tile):
                wait_apart(sp, (s_cb, tile))
                sp.dma_start(bias_t, bq[:, bass.ds(tile * TN, TN)]).then_inc(s_bl, 16)

            def load_h1(tile):
                wait_apart(sp, (s_out, TSUB // 2 * tile))
                sp.dma_start(h1t, h1_t[tile]).then_inc(s_h1l, 16)

            def store_out(tile, par):
                wait_apart(sp, (s_out, TSUB // 2 * (tile + 1)))
                sp.dma_start(out_t[tile], outt[:, par]).then_inc(s_od[par], 16)

            load_codes(0, 0)
            for q in range(4):
                load_gates(0, q)
                if q == 1:
                    load_codes(0, 1)
            load_h1(0)
            load_bias(0)
            for par in range(2):
                sp.sem_inc(s_od[par], 16)

            def refill(tile, q):
                wait_apart(sp, (s_gb, QUADS * (tile - 1) + 8 * (q + 1)),
                           (s_hp1, 2 * QUADS * (tile - 1) + 16 * (q + 1)))
                load_gates(tile, q)
                if q % 2 == 1:
                    load_codes(tile, q // 2)

            refill(1, 0)
            refill(1, 1)
            refill(1, 2)
            refill(1, 3)
            with sp.Fori(0, (TILES - 2) // 2) as i:
                for k in range(2):
                    tile = 2 * i + 1 + k
                    load_bias(tile)
                    store_out(tile - 1, k % 2)
                    load_h1(tile)
                    for q in range(4):
                        refill(tile + 1, q)
            load_bias(TILES - 1)
            store_out(TILES - 2, 0)
            load_h1(TILES - 1)
            store_out(TILES - 1, 1)
            for par in range(2):
                wait_apart(sp, (s_od[par], 16 * (TILES // 2 + 1)))

        @block.gpsimd
        def _(pool):
            p_ = nc.gpsimd
            pool.dma_start(widx, t["word_ids"]).then_inc(s_word[0], 16)
            p_.iota(iota_i, pattern=[[0, 1]], base=0, channel_multiplier=1).then_inc(s_const, 1)
            p_.memset(ident[:], 0.0).then_inc(s_const, 1)
            p_.memset(sel[:], 0.0).then_inc(s_const, 1)
            p_.memset(ones_row, 1.0)
            p_.memset(mhalf, -0.5).then_inc(s_const, 1)
            pool.wait_ge(s_const, 4)
            p_.affine_select(out=ident[:], in_=ident[:], compare_op=ALU.not_equal, fill=1.0, base=0,
                             pattern=[[-1, 128]], channel_multiplier=1).then_inc(s_const, 1)
            for i in range(6):
                a, p = divmod(i, 3)
                pool.wait_ge(s_const, 5 + i)
                v = sel[64 * a:64 * a + 48].rearrange("p (e h) -> p e h", e=16)
                p_.affine_select(out=v, in_=v, compare_op=ALU.not_equal, fill=1.0, base=-16 * p,
                                 pattern=[[-1, 16], [0, 8]], channel_multiplier=1).then_inc(s_const, 1)
            pool.wait_ge(s_const, 11)
            p_.memset(w2p[:], 0.0)
            p_.memset(b2p[:], 0.0).then_inc(s_const, 1)

            def gather(jj, par):
                wait_apart(pool, (s_emb, jj - 1))
                p_.tensor_copy(wnow[:, par], widx[:, bass.ds(4 * jj, 4)]).then_inc(s_wnow, 1)
                wait_apart(pool, (s_wnow, jj + 1))
                for bb in range(4):
                    p_.indirect_dma_start(
                        word[:, par, bb], None, t["w_word"],
                        bass.IndirectOffsetOnAxis(ap=wnow[:, par, bb:bb + 1], axis=0)).then_inc(s_word[par], 16)

            def text_rows(jj, par):
                wait_apart(pool, (s_tmv, jj + 1))
                p_.tensor_scalar_add(tve, tmv[:, :, 1], EPS_TXT).then_inc(s_tve, 1)
                wait(pool, s_tve, jj + 1)
                p_.tensor_tensor(trs, tve, mhalf, ALU.pow).then_inc(s_trs, 1)
                wait(pool, s_tn, jj + 1)
                p_.tensor_tensor(tmul, tnorm[:, par], tgam.unsqueeze(1).to_broadcast([TT, 4, D]),
                                 ALU.mult).then_inc(s_tmul, 1)
                wait(pool, s_tmul, jj + 1)
                wait(pool, s_todma[par], use_count(jj, par))
                p_.tensor_tensor(tout[:, par], tmul, tbet.unsqueeze(1).to_broadcast([TT, 4, D]),
                                 ALU.add).then_inc(s_to, 1)

            def use_count(jj, par):
                if isinstance(jj, int):
                    return 64 * (jj // 2)
                return 32 * (jj - par)

            pool.wait_ge(s_word[0], 16)
            gather(0, 0)
            gather(1, 1)
            pool.wait_ge(s_tl, 16 * 7)
            text_rows(0, 0)
            wait(pool, s_cstd, 3)
            p_.tensor_tensor(w1r, w1f, w1h[:, 0], ALU.subtract)
            p_.tensor_tensor(b1r, b1f, b1h[:, 0], ALU.subtract).then_inc(s_split, 1)
            pool.wait_ge(s_split, 1)
            p_.tensor_copy(w1h[:, 1], w1r)
            p_.tensor_copy(b1h[:, 1], b1r).then_inc(s_split, 1)
            pool.wait_ge(s_split, 2)
            p_.tensor_tensor(w1h[:, 2], w1r, w1h[:, 1], ALU.subtract)
            p_.tensor_tensor(b1h[:, 2], b1r, b1h[:, 1], ALU.subtract).then_inc(s_split, 2)
            gather(2, 0)
            for jj in (1, 2):
                text_rows(jj, jj % 2)
                gather(jj + 2, jj % 2)
            with pool.Fori(0, 3) as pr:
                for k in range(2):
                    jj = 2 * pr + 3 + k
                    text_rows(jj, 1 - k)
                    gather(jj + 2, 1 - k)
            text_rows(9, 1)
            text_rows(10, 0)
            pool.wait_ge(s_w2f, 16)
            w2v = w2f.rearrange("p (j o g r) -> p j o g r", j=PAIRS, o=2, g=16)
            w2o = w2p[:].rearrange("p (j o g) c -> p j o g c", j=PAIRS, o=2)
            pool.wait_ge(s_const, 12)
            for o in range(2):
                last = p_.tensor_copy(w2o[:, :, o, :, 16 * o:16 * o + 16], w2v[:, :, o])
            last.then_inc(s_split, 1)
            pool.wait_ge(s_b2f, 16)
            src = b2f
            done = 0
            for part in range(3):
                for o in range(2):
                    rows = slice(64 * o, 64 * o + 64)
                    p_.tensor_copy(b2p[rows, :, part, 16 * o:16 * o + 16], src[rows]).then_inc(s_b2s, 1)
                    done += 1
                    pool.wait_ge(s_b2s, done)
                    if part < 2:
                        p_.tensor_tensor(b2r[rows], src[rows], b2p[rows, :, part, 16 * o:16 * o + 16],
                                         ALU.subtract).then_inc(s_b2s, 1)
                        done += 1
                        pool.wait_ge(s_b2s, done)
                src = b2r

            stage1_over(pool)
            p_.memset(maskh, 0.0)
            p_.memset(headsel, 0.0)
            p_.memset(ones2, 1.0)
            p_.memset(lsel, 0.0)
            p_.memset(mh2, -0.5).then_inc(s_c2, 1)
            for o in range(2):
                pool.wait_ge(s_c2, 1 + o)
                v = maskh[64 * o:64 * o + 64]
                p_.affine_select(out=v, in_=v, compare_op=ALU.not_equal, fill=1.0, base=-o,
                                 pattern=[[-2, CH], [1, HEADS]], channel_multiplier=0).then_inc(s_c2, 1)
            for b in range(UB):
                pool.wait_ge(s_c2, 3 + b)
                v = headsel[32 * b:32 * b + 32, b].rearrange("p c (o d) -> p c o d", o=2)
                p_.affine_select(out=v, in_=v, compare_op=ALU.not_equal, fill=1.0, base=0,
                                 pattern=[[-2, CH], [-1, 2], [0, DH]], channel_multiplier=1).then_inc(s_c2, 1)
            pool.wait_ge(s_c2, 7)

            def rstd(k, u, eps):
                wait_apart(pool, (s_mv[k], u + 1), (s_xn[k], u))
                p_.tensor_scalar_add(ve[k], mv[k][:, :, 1], eps).then_inc(s_ve[k], 1)
                wait(pool, s_ve[k], u + 1)
                p_.tensor_tensor(rs[k], ve[k], mh2, ALU.pow).then_inc(s_rs[k], 1)

            def z_parts(u):
                wait(pool, s_z1, u + 1)
                wait(pool, s_zd, 48 * u)
                p_.tensor_tensor(zr, zf, zh[:, 0], ALU.subtract).then_inc(s_zr, 1)
                wait_apart(pool, (s_zr, u + 1))
                p_.tensor_copy(zh[:, 1], zr).then_inc(s_z2, 1)
                wait(pool, s_z2, u + 1)
                p_.tensor_tensor(zh[:, 2], zr, zh[:, 1], ALU.subtract).then_inc(s_z3, 1)

            def shift(u, s):
                wait(pool, s_v8, SUB * u + s + 1)
                wait(pool, s_se, SUB * u)
                p_.tensor_tensor(sd[:, s].rearrange("p (a b) -> p a b", a=S), sc[:, s, :, 0:M],
                                 v8[:, s, :, 0:1].to_broadcast([ST, S, M]), ALU.subtract).then_inc(s_sd, 1)

            def gates(u, s):
                wait(pool, s_gr, SUB * u + s + 1)
                wait(pool, s_gt, SUB * u)
                p_.tensor_tensor(gg[:, s].rearrange("p (a b) -> p a b", a=S),
                                 gu[:, s].rearrange("p (a b) -> p a b", a=S),
                                 gr[:, s].unsqueeze(2).to_broadcast([ST, S, M]), ALU.mult).then_inc(s_gg, 1)

            def gate_parts(u, s):
                n = SUB * u + s
                wait_apart(pool, (s_grr, n + 1))
                p_.tensor_copy(gh[:, 1, :, ST * s:ST * s + ST], grr[:, s]).then_inc(s_g2, 1)
                wait_apart(pool, (s_g2, n + 1))
                p_.tensor_tensor(gh[:, 2, :, ST * s:ST * s + ST], grr[:, s],
                                 gh[:, 1, :, ST * s:ST * s + ST], ALU.subtract).then_inc(s_g3, 1)

            def unit_pool(u, do_a, do_g):
                if do_a:
                    rstd("A", u, EPS_LN)
                if do_g:
                    rstd("G", u - 1, EPS_LN)
                    z_parts(u - 1)
                    for s in range(SUB):
                        shift(u - 1, s)
                    gates(u - 1, 0)
                if do_a:
                    wait(pool, s_lg, u + 1)
                    for c in range(CH):
                        wait(pool, s_wpi, CH * u + c + 1)
                        p_.tensor_tensor(wsq[:, c], wpi[:, c], wv[:, c], ALU.mult).then_inc(s_w2pi, 1)
                if do_g:
                    gates(u - 1, 1)
                    gates(u - 1, 2)
                if do_a:
                    wait(pool, s_na, u + 1)
                    wait(pool, s_w2pi, CH * (u + 1))
                    for c in range(CH):
                        p_.tensor_tensor(wv[:, c].rearrange("p (b n) -> p b n", b=UB),
                                         wpi[:, c].rearrange("p (b n) -> p b n", b=UB),
                                         natt[:, c].unsqueeze(2).to_broadcast([128, UB, N]),
                                         ALU.mult).then_inc(s_o, 1)
                if do_g:
                    for s in range(SUB):
                        gate_parts(u - 1, s)

            unit_pool(0, True, False)
            unit_pool(1, True, True)
            with pool.Fori(2, UNITS) as u:
                unit_pool(u, True, True)
            unit_pool(UNITS, False, True)
            stage2_over(pool)
            p_.memset(zst[96:ZROWS], 1.0).then_inc(s_ones, 1)
            pool.wait_ge(s_ones, 1)
            p_.memset(y1[G:G + 1], 1.0).then_inc(s_ones, 1)
            with pool.Fori(0, TILES) as tile:
                wait_apart(pool, (s_comb, tile + 1), (s_bl, 16 * (tile + 1)))
                p_.tensor_tensor(code, comb, bias_t, ALU.add).then_inc(s_cb, 1)

        @block.scalar
        def _(act):
            a_ = nc.scalar
            for k in range(8):
                wait(act, s_ips, k + 1)
                wait(act, s_idma[k % 2], 16 * (k // 2))
                a_.copy(img[:, k % 2], banks[k % 2][:, 0:D]).then_inc(s_iev, 1)
                wait(act, s_iev, k + 1)
                act.dma_start(h0_b[8 * k:8 * k + 8, 0:NI, :], img[:, k % 2]).then_inc(s_idma[k % 2], 16)

            stage1_over(act)

            def xT(k, u):
                wait(act, s_tp[k], u + 1)
                a_.copy(xt0[k], banks[0][:, 0:UT])
                a_.copy(xt1[k], banks[1][0:D1, 0:UT]).then_inc(s_xt_[k], 1)

            def w_copy(u, c):
                wait(act, s_wp, CH * u + c + 1)
                if c == 0:
                    wait(act, s_hp, u)
                    wait(act, s_dt, CH * u)
                src = pair0[:, c % 2, 0:UT]
                a_.copy(wv[:, c], src).then_inc(s_wv, 1)
                a_.activation(wsq[:, c], src, ACT.Square).then_inc(s_wsq, 1)

            def copy_bias(u):
                wait(act, s_bp, u + 1)
                wait(act, s_bd, 16 * u)
                a_.copy(bt, pair1[:, 1, 0:UT]).then_inc(s_bt, 1)

            def unit_act(u, do_a, do_g):
                if do_a:
                    xT("A", u)
                if do_g:
                    xT("G", u - 1)
                if do_a:
                    w_copy(u, 0)
                    w_copy(u, 1)
                if do_g and (not isinstance(u, int) or u >= 2):
                    copy_bias(u - 2)
                if do_g:
                    wait(act, s_z, u)
                    wait(act, s_zd, 48 * (u - 1))
                    wait(act, s_z3, u - 1)
                    a_.copy(zf, pair1[:, 1, 0:UT]).then_inc(s_zf, 1)
                    a_.copy(zh[:, 0], pair1[:, 1, 0:UT]).then_inc(s_z1, 1)
                if do_a:
                    for c in range(2, CH):
                        w_copy(u, c)
                if do_g:
                    for s in range(SUB):
                        n = SUB * (u - 1) + s
                        wait(act, s_sp, n + 1)
                        wait(act, s_mr, n - s)
                        wait(act, s_sd, n - s)
                        a_.copy(sc[:, s, :, 0:M],
                                banks[2][0:ST, :].rearrange("p (a b) -> p a b", a=S)).then_inc(s_sc, 1)
                if do_a:
                    wait(act, s_lm, u + 1)
                    a_.activation(pe_, lg, ACT.Exp, bias=nmax, accum_out=psm).then_inc(s_pe, 1)
                if do_g:
                    for s in range(SUB):
                        n = SUB * (u - 1) + s
                        wait(act, s_sd, n + 1)
                        wait(act, s_gu, n - s)
                        a_.activation(se[:, s], sd[:, s], ACT.Exp).then_inc(s_se, 1)
                    for s in range(SUB):
                        n = SUB * (u - 1) + s
                        wait(act, s_gt, n + 1)
                        if s == 0:
                            wait(act, s_gd, 48 * (u - 1))
                            wait(act, s_bp, u - 1)
                        a_.copy(gh[:, 0, :, ST * s:ST * s + ST],
                                pair1[:, 1, 0:4 * ST].rearrange("p (a b) -> p a b", a=4)).then_inc(s_g1, 1)

            unit_act(0, True, False)
            unit_act(1, True, True)
            unit_act(2, True, True)
            with act.Fori(3, UNITS) as u:
                unit_act(u, True, True)
            unit_act(UNITS, False, True)
            copy_bias(UNITS - 1)

            stage2_over(act)
            wait(act, s_ones, 2)
            wait(act, s_w, 64)

            def gelu(tile, pair):
                quad = pair // 2
                wait(act, s_hp1, 2 * QUADS * tile + pair + 1)
                if pair % 2 == 0:
                    wait(act, s_gat, QUADS * tile + quad - 3)
                a_.activation(hid[:, quad % 4, 2 * (pair % 2):2 * (pair % 2) + 2], (pair0, pair1)[pair % 2][:, :, 0:TN],
                              ACT.Gelu_apprx_tanh).then_inc(s_hid, 1)

            def copy_code(tile):
                wait(act, s_code, QUADS * (tile + 1))
                a_.copy(comb, code_bank[:, 0:TN]).then_inc(s_comb, 1)

            def gelu_out(tile):
                wait(act, s_f1, tile + 1)
                a_.activation(y1[0:G], out_bank[0:G, 0:TN], ACT.Gelu_apprx_tanh,
                              bias=g1b[:]).then_inc(s_y1, 1)

            def tile_act(tile, first):
                for pair in range(2 * QUADS):
                    gelu(tile, pair)
                    if not first:
                        if pair == 9:
                            copy_code(tile - 1)
                        if pair == 2 * OUT1_AT + 5:
                            gelu_out(tile - 1)

            tile_act(0, True)
            with act.Fori(1, TILES) as tile:
                tile_act(tile, False)
            copy_code(TILES - 1)
            gelu_out(TILES - 1)

        @block.vector
        def _(dve):
            v_ = nc.vector
            dve.wait_ge(s_const, 1)
            v_.tensor_copy(iota_f, iota_i).then_inc(s_cstd, 1)
            dve.wait_ge(s_tl, 16 * 7)
            v_.tensor_scalar(small_ids[0:2], small_ids[0:2], 0, None, ALU.is_gt).then_inc(s_cstd, 1)
            dve.wait_ge(s_cstd, 2)

            def onehots(jj, par):
                wait(dve, s_tps, jj - 1)
                v_.tensor_scalar(ohp[:, par].rearrange("p a b -> p (a b)"), pos_ids[:, bass.ds(jj * 448, 448)],
                                 iota_f, None, ALU.is_equal)
                v_.tensor_scalar(ohs[:, par].rearrange("p a b -> p (a b)"), small_ids[:, bass.ds(jj * 448, 448)],
                                 rowidx, None, ALU.is_equal).then_inc(s_oh, 1)

            def words(jj, par, base=0):
                wait(dve, s_tps, jj + 1)
                if isinstance(jj, int):
                    uses = jj // 2 + 1
                    wait(dve, s_word[par], 64 * uses + (16 if par == 0 else 0))
                else:
                    wait(dve, s_word[par], 32 * (jj - par) + 64 + (16 if par == 0 else 0))
                v_.tensor_tensor(emb[:, par].rearrange("p (a b) -> p a b", a=2),
                                 (pair0, pair1)[par][0:TT, :, 0:2 * D],
                                 word[:, par].rearrange("p (a b) d -> p a (b d)", a=2), ALU.add).then_inc(s_emb, 1)
                wait(dve, s_emb, jj + 1)
                for bb in range(4):
                    last = v_.bn_stats(tst[:, bb], emb[:, par, D * bb:D * bb + D])
                last.then_inc(s_tst, 1)
                wait_apart(dve, (s_tst, jj + 1))
                for bb in range(4):
                    last = v_.bn_aggr(tmv[:, bb], tst[:, bb])
                last.then_inc(s_tmv, 1)

            def normed(jj, par):
                wait(dve, s_trs, jj + 1)
                wait(dve, s_tmul, jj - 1)
                for bb in range(4):
                    last = v_.tensor_scalar(tnorm[:, par, bb], emb[:, par, D * bb:D * bb + D], tmv[:, bb, 0:1],
                                            trs[:, bb:bb + 1], ALU.subtract, ALU.mult)
                last.then_inc(s_tn, 1)

            onehots(0, 0)
            words(0, 0)
            normed(0, 0)
            dve.wait_ge(s_w1f, 32)
            v_.tensor_copy(w1h[:, 0], w1f)
            v_.tensor_copy(b1h[:, 0], b1f).then_inc(s_cstd, 1)
            for jj in (1, 2):
                onehots(jj, jj % 2)
                words(jj, jj % 2)
                normed(jj, jj % 2)
            with dve.Fori(0, 4) as pr:
                for k in range(2):
                    jj = 2 * pr + 3 + k
                    onehots(jj, 1 - k)
                    words(jj, 1 - k)
                    normed(jj, 1 - k)

            stage1_over(dve)
            v_.memset(tempc, 0.0)
            v_.memset(cbd, 0.0).then_inc(s_c2d, 1)
            v_.memset(sc[:, :, :, M:M + 8], SENTINEL)
            v_.memset(v4, SENTINEL).then_inc(s_c2d, 1)
            dve.wait_ge(s_c2, 7)
            dve.wait_ge(s_c2d, 2)
            dve.wait_ge(s_w2l, 16 * (6 + UB + S))

            def stats(k, u, src):
                for s in range(SUB):
                    last = v_.bn_stats(st[k][:, s], src[:, s])
                last.then_inc(s_st[k], 1)
                wait_apart(dve, (s_st[k], u + 1))
                for s in range(SUB):
                    last = v_.bn_aggr(mv[k][:, s], st[k][:, s])
                last.then_inc(s_mv[k], 1)

            def norm(k, u, src):
                wait(dve, s_rs[k], u + 1)
                wait(dve, s_tp[k], u)
                for s in range(SUB):
                    last = v_.tensor_scalar(xn[k][:, s], src[:, s], mv[k][:, s, 0:1], rs[k][:, s:s + 1],
                                            ALU.subtract, ALU.mult)
                last.then_inc(s_xn[k], 1)

            def top(u, s):
                n = SUB * u + s
                wait_apart(dve, (s_sc, n + 1), (s_sd, n - s))
                for g in range(S):
                    last = v_.max(v8[:, s, g], sc[:, s, g, 0:M])
                last.then_inc(s_v8, 1)
                wait(dve, s_v8, n + 1)
                v_.tensor_copy(v4[:, s, :, 0:4], v8[:, s, :, 0:4]).then_inc(s_v4, 1)
                wait_apart(dve, (s_v4, n + 1))
                for g in range(S):
                    last = v_.match_replace(mr[:, s, g], v4[:, s, g], sc[:, s, g], CHOSEN)
                last.then_inc(s_mr, 1)

            def raw(u, s):
                n = SUB * u + s
                wait(dve, s_se, n + 1)
                wait(dve, s_mr, n + 1)
                wait(dve, s_gg, n - s)
                v_.scalar_tensor_tensor(out=gu[:, s].rearrange("p (a b) -> p a b", a=S), in0=mr[:, s, :, 0:M],
                                        scalar=CHOSEN, in1=se[:, s].rearrange("p (a b) -> p a b", a=S),
                                        op0=ALU.is_equal, op1=ALU.mult).then_inc(s_gu, 1)
                wait(dve, s_gu, n + 1)
                v_.tensor_reduce(gs[:, s], gu[:, s].rearrange("p (a b) -> p a b", a=S), AX.X, ALU.add).then_inc(s_gs, 1)
                wait(dve, s_gs, n + 1)
                v_.reciprocal(gr[:, s], gs[:, s]).then_inc(s_gr, 1)

            def rest(u, s):
                n = SUB * u + s
                wait(dve, s_g1, n + 1)
                wait(dve, s_g3, n - s)
                v_.tensor_tensor(grr[:, s], pair1[:, 1, 0:4 * ST].rearrange("p (a b) -> p a b", a=4),
                                 gh[:, 0, :, ST * s:ST * s + ST], ALU.subtract).then_inc(s_grr, 1)

            def unit_dve(u, slot, do_a, do_g):
                if do_a:
                    wait(dve, s_x0, 16 * (u + 1))
                    stats("A", u, x0[:, slot])
                if do_g:
                    wait(dve, s_h1, u)
                    stats("G", u - 1, h1)
                if do_a:
                    norm("A", u, x0[:, slot])
                if do_g:
                    norm("G", u - 1, h1)
                if do_a:
                    for c in range(CH):
                        wait(dve, s_wsq, CH * u + c + 1)
                        v_.tensor_reduce(n2[:, c], wsq[:, c].rearrange("p (b n) -> p b n", b=UB), AX.X,
                                         ALU.add).then_inc(s_n2, 1)
                    wait(dve, s_n2, CH * (u + 1))
                    v_.tensor_scalar(n2m, n2, 1e-24, None, ALU.max).then_inc(s_nm, 1)
                    wait(dve, s_nm, u + 1)
                    v_.reciprocal(inv, n2m).then_inc(s_inv, 1)
                    wait(dve, s_inv, u + 1)
                    for b in range(UB):
                        last = v_.tensor_tensor(lsel[:, b, :, 0:HEADS], maskh,
                                                inv[:, :, b:b + 1].to_broadcast([128, CH, HEADS]), ALU.mult)
                    last.then_inc(s_L, 1)
                if do_g:
                    top(u - 1, 0)
                if do_a:
                    wait(dve, s_lg, u + 1)
                    v_.tensor_scalar(lg, pair1[:, 0, 0:N], tempc, None, ALU.mult).then_inc(s_lt, 1)
                    wait(dve, s_lt, u + 1)
                    v_.tensor_reduce(nmax, lg, AX.X, ALU.max, negate=True).then_inc(s_lm, 1)
                if do_g:
                    top(u - 1, 1)
                if do_a:
                    wait(dve, s_pe, u + 1)
                    v_.reciprocal(prc, psm).then_inc(s_pr, 1)
                    wait(dve, s_pr, u + 1)
                    v_.tensor_scalar(pi[:, 0:N], pe_, prc, None, ALU.mult).then_inc(s_pi, 1)
                    wait(dve, s_pi, u + 1)
                    v_.tensor_reduce(pss, pi[:, 0:N], AX.X, ALU.add).then_inc(s_ps, 1)
                    wait(dve, s_ps, u + 1)
                    v_.tensor_scalar(pse, pss, 1e-8, None, ALU.add).then_inc(s_pse, 1)
                    wait(dve, s_pse, u + 1)
                    v_.reciprocal(pi[:, N:N + 1], pse).then_inc(s_pix, 1)
                if do_g:
                    top(u - 1, 2)
                    raw(u - 1, 0)
                if do_a:
                    for c in range(CH):
                        wait(dve, s_pb, CH * u + c + 1)
                        pb = pair0[:, c % 2, 0:UB * (N + 1)].rearrange("p (b n) -> p b n", b=UB)
                        v_.tensor_tensor(wpi[:, c].rearrange("p (b n) -> p b n", b=UB),
                                         wv[:, c].rearrange("p (b n) -> p b n", b=UB), pb[:, :, 0:N],
                                         ALU.mult).then_inc(s_wpi, 1)
                        v_.tensor_copy(rsc[:, c], pb[:, :, N]).then_inc(s_rsc, 1)
                if do_g:
                    raw(u - 1, 1)
                    raw(u - 1, 2)
                if do_a:
                    for c in range(CH):
                        wait(dve, s_w2pi, CH * u + c + 1)
                        v_.tensor_reduce(dots[:, c], wsq[:, c].rearrange("p (b n) -> p b n", b=UB), AX.X,
                                         ALU.add).then_inc(s_dt, 1)
                    wait(dve, s_dt, CH * (u + 1))
                    wait(dve, s_rsc, CH * (u + 1))
                    v_.tensor_tensor(dsc, dots, rsc, ALU.mult).then_inc(s_ds, 1)
                    wait(dve, s_ds, u + 1)
                    v_.tensor_scalar(dmi, dsc, -1.0, -1.0, ALU.mult, ALU.add).then_inc(s_dm, 1)
                    wait(dve, s_dm, u + 1)
                    v_.reciprocal(natt, dmi).then_inc(s_na, 1)
                if do_g:
                    for s in range(SUB):
                        rest(u - 1, s)
                if do_a:
                    wait(dve, s_hp, u + 1)
                    wait(dve, s_h1d, 16 * u)
                    v_.tensor_tensor(h1[:, 0:2], banks[3][0:ST, 0:2 * D].rearrange("p (a b) -> p a b", a=2),
                                     x0[:, slot, 0:2], ALU.add)
                    v_.tensor_tensor(h1[:, 2], pair1[0:ST, 0, 128:128 + D], x0[:, slot, 2], ALU.add).then_inc(s_h1, 1)

            unit_dve(0, 0, True, False)
            unit_dve(1, 1, True, True)
            with dve.Fori(0, (UNITS - 2) // 2) as i:
                unit_dve(2 * i + 2, 0, True, True)
                unit_dve(2 * i + 3, 1, True, True)
            unit_dve(UNITS, 0, False, True)

            stage2_over(dve)

            def gate_quad(tile, quad):
                wait(dve, s_hid, 2 * QUADS * tile + 2 * quad + 2)
                wait(dve, s_gb, QUADS * tile + quad + 1)
                block, j = divmod(quad, PAIRS)
                if j == 0:
                    wait(dve, s_code, QUADS * tile + PAIRS * (block - 1))
                v_.tensor_tensor(gated[:, block % 2, j], hid[:, quad % 4],
                                 gate_banks[quad % 2][:, 0:TN].unsqueeze(1).to_broadcast([128, KH, TN]),
                                 ALU.mult).then_inc(s_gat, 1)

            def add_out(tile, half, par):
                wait(dve, s_f2, 2 * tile + half + 1)
                if half == 0:
                    wait(dve, s_h1l, 16 * (tile + 1))
                    if isinstance(tile, int):
                        wait(dve, s_od[par], 16 * (tile // 2 + 1))
                    else:
                        wait(dve, s_od[par], 8 * (tile - par) + 16)
                v_.tensor_tensor(outt[:, par, 2 * half:2 * half + 2],
                                 out_bank[0:ST, 0:2 * D].rearrange("p (a b) -> p a b", a=2),
                                 h1t[:, 2 * half:2 * half + 2], ALU.add).then_inc(s_out, 1)

            def tile_dve(tile, par, first):
                for quad in range(QUADS):
                    gate_quad(tile, quad)
                    if not first:
                        for half in range(2):
                            if quad == OUT2_AT[half] + 1:
                                add_out(tile - 1, half, 1 - par)

            tile_dve(0, 0, True)
            with dve.Fori(0, (TILES - 2) // 2) as i:
                for k in range(2):
                    tile_dve(2 * i + 1 + k, 1 - k, False)
            tile_dve(TILES - 1, 1, False)
            add_out(TILES - 1, 0, 1)
            add_out(TILES - 1, 1, 1)

        @block.tensor
        def _(pe):
            t_ = nc.tensor
            pe.wait_ge(s_xt, 48)
            pe.wait_ge(s_const, 5)
            for k in range(8):
                wait(pe, s_iev, k - 1)
                for c in range(KC):
                    t_.matmul(banks[k % 2][:, 0:D], xt[:, c, 128 * k:128 * k + 128], wtok[:, c],
                              start=(c == 0), stop=False)
                t_.matmul(banks[k % 2][:, 0:D], ones_row, tokb, start=False, stop=True).then_inc(s_ips, 1)

            pe.wait_ge(s_tl, 16 * 7)

            def tables(jj, par):
                wait(pe, s_oh, jj + 1)
                wait(pe, s_emb, jj - 1)
                for bb in range(4):
                    o = (pair0, pair1)[par][0:TT, bb // 2, D * (bb % 2):D * (bb % 2) + D]
                    t_.matmul(o, ohp[:, par, bb], wpos, start=True, stop=False)
                    last = t_.matmul(o, ohs[:, par, bb], wsmall, start=False, stop=True)
                last.then_inc(s_tps, 1)

            tables(0, 0)
            tables(1, 1)
            tables(2, 0)
            with pe.Fori(0, 4) as pr:
                tables(2 * pr + 3, 1)
                tables(2 * pr + 4, 0)

            stage1_over(pe)
            pe.wait_ge(s_c2, 7)
            pe.wait_ge(s_w2l, 16 * (6 + UB + S))

            def transposes(k, u, other_done):
                wait(pe, s_xn[k], u + 1)
                wait(pe, *other_done)
                for s in range(SUB):
                    t_.transpose(banks[0][:, ST * s:ST * s + ST], xn[k][:, s, 0:128], ident[0:ST, 0:ST])
                    last = t_.transpose(banks[1][0:D1, ST * s:ST * s + ST], xn[k][:, s, 128:D],
                                        ident[0:ST, 0:ST])
                last.then_inc(s_tp[k], 1)

            def w_product(u, c):
                if c == 0:
                    wait(pe, s_xt_["A"], u + 1)
                if c < 2:
                    wait(pe, s_rsc, CH * (u - 1) + 5 + c)
                else:
                    wait(pe, s_wsq, CH * u + c - 1)
                o = pair0[:, c % 2, 0:UT]
                t_.matmul(o, wq0[:, 128 * c:128 * c + 128], xt0["A"], start=True, stop=False)
                t_.matmul(o, wq1[:, 128 * c:128 * c + 128], xt1["A"], start=False, stop=True).then_inc(s_wp, 1)

            def bias(u):
                wait(pe, s_g3, SUB * (u + 1))
                for i in range(6):
                    for j in range(PAIRS):
                        mm = t_.matmul(pair1[32 * j:32 * j + 32, 1, 0:UT], b2p[:, j, WP[i]], gh[:, ZP[i], j],
                                       start=(i == 0), stop=(i == 5), skip_group_check=True)
                mm.then_inc(s_bp, 1)

            def unit_pe(u, do_a, do_g):
                if do_a:
                    transposes("A", u, (s_xt_["G"], u - 1))
                if do_g:
                    if do_a:
                        transposes("G", u - 1, (s_xt_["A"], u + 1))
                    else:
                        transposes("G", u - 1, (s_xt_["G"], u - 1))
                if do_a:
                    w_product(u, 0)
                    w_product(u, 1)
                if do_g and (not isinstance(u, int) or u >= 2):
                    bias(u - 2)
                if do_g:
                    wait(pe, s_xt_["G"], u)
                    wait(pe, s_grr, SUB * (u - 1))
                    wait(pe, s_bt, u - 1)
                    t_.matmul(pair1[:, 1, 0:UT], pz0, xt0["G"], start=True, stop=False)
                    t_.matmul(pair1[:, 1, 0:UT], pz1, xt1["G"], start=False, stop=True).then_inc(s_z, 1)
                if do_a:
                    for c in range(2, CH):
                        w_product(u, c)
                if do_g:
                    wait(pe, s_zf, u)
                    for s in range(SUB):
                        wait(pe, s_sc, SUB * (u - 1) + s)
                        t_.matmul(banks[2][0:ST, :], zf[:, ST * s:ST * s + ST], cbd, start=True,
                                  stop=True).then_inc(s_sp, 1)
                if do_a:
                    wait(pe, s_L, u + 1)
                    wait(pe, s_h1, u)
                    for b in range(UB):
                        for c in range(CH):
                            last = t_.matmul(pair1[32 * b:32 * b + 32, 0, 0:N], lsel[:, b, c],
                                             wsq[:, c, N * b:N * b + N], start=(c == 0), stop=(c == CH - 1))
                    last.then_inc(s_lg, 1)
                    wait(pe, s_pix, u + 1)
                    for c in range(CH):
                        if c < 2:
                            wait(pe, s_wsq, CH * u + 5 + c)
                        else:
                            wait(pe, s_rsc, CH * u + c - 1)
                        for b in range(UB):
                            last = t_.matmul(pair0[:, c % 2, (N + 1) * b:(N + 1) * (b + 1)], headsel[:, b, c],
                                             pi, start=True, stop=True)
                        last.then_inc(s_pb, 1)
                if do_g:
                    wait(pe, s_z1, u)
                    for s in range(SUB):
                        n = SUB * (u - 1) + s
                        wait(pe, s_gg, n + 1)
                        wait(pe, s_grr, n)
                        for q in range(4):
                            last = t_.transpose(pair1[:, 1, ST * q:ST * q + ST], gg[:, s, 128 * q:128 * q + 128],
                                                ident[0:ST, 0:ST])
                        last.then_inc(s_gt, 1)
                if do_a:
                    wait(pe, s_o, CH * (u + 1))
                    wait(pe, s_lt, u + 1)
                    for s in range(SUB):
                        o = banks[3][0:ST, D * s:D * s + D] if s < 2 else pair1[0:ST, 0, 128:128 + D]
                        for c in range(CH):
                            t_.matmul(o, wv[:, c, ST * s:ST * s + ST], wout[:, c], start=(c == 0), stop=False)
                        last = t_.matmul(o, ones2, bout, start=False, stop=True)
                    last.then_inc(s_hp, 1)

            unit_pe(0, True, False)
            unit_pe(1, True, True)
            with pe.Fori(2, UNITS) as u:
                unit_pe(u, True, True)
            unit_pe(UNITS, False, True)
            bias(UNITS - 1)

            stage2_over(pe)
            pe.wait_ge(s_ones, 2)
            pe.wait_ge(s_w, 64)

            def hidden(tile, pair):
                block, j = divmod(pair // 2, PAIRS)
                o, eb = divmod(block, EB)
                if pair % QUADS == 0:
                    wait(pe, s_zl[o], 96 * (tile + 1))
                wait(pe, s_hid, 2 * QUADS * tile + pair - 1)
                for a in range(2):
                    x = chunk(2 * j + o, eb, 2 * (pair % 2) + a) * 128
                    mm = t_.matmul((pair0, pair1)[pair % 2][:, a, 0:TN], w1s[:, x:x + 128], zst[:, o, j],
                                   start=True, stop=True)
                mm.then_inc(s_hp1, 1)

            def spread(tile, quad):
                block, j = divmod(quad, PAIRS)
                if quad % (QUADS // 4) == 0:
                    wait(pe, s_gl[block // 2], 192 * (tile + 1))
                wait(pe, s_gat, QUADS * tile + quad - 1)
                rows = slice(64 * (j % 2), 64 * (j % 2) + 48)
                t_.matmul(gate_banks[quad % 2][:, 0:TN], sel[rows], gst[rows, block, j // 2],
                          start=True, stop=True).then_inc(s_gb, 1)

            def decode(tile, block, k):
                if k == 0:
                    wait(pe, s_gat, QUADS * tile + PAIRS * (block + 1))
                    if block == 0:
                        wait(pe, s_comb, tile)
                o, eb = divmod(block, EB)
                for j in range(PAIRS):
                    mm = t_.matmul(code_bank[32 * j:32 * j + 32, 0:TN], w2p[:, chunk(2 * j + o, eb, k)],
                                   gated[:, block % 2, j, k], start=(block == 0 and k == 0),
                                   stop=(block == BLOCKS - 1 and k == KH - 1), skip_group_check=True)
                mm.then_inc(s_code, 1)

            def out1(tile):
                wait(pe, s_cb, tile + 1)
                wait(pe, s_h1l, 16 * (tile + 1))
                t_.matmul(out_bank[0:G, 0:TN], g1w[:], code, start=True, stop=True).then_inc(s_f1, 1)

            def out2(tile, half):
                wait(pe, s_y1, tile + 1)
                if half == 1:
                    wait(pe, s_out, 2 * tile + 1)
                for k in range(2):
                    x = ST * (2 * half + k)
                    mm = t_.matmul(out_bank[0:ST, D * k:D * k + D], y1[:, x:x + ST], g2w[:],
                                   start=True, stop=True)
                mm.then_inc(s_f2, 1)

            def tile_pe(tile, first, last):
                for quad in range(QUADS):
                    if quad + 1 < QUADS:
                        spread(tile, quad + 1)
                    elif not last:
                        spread(tile + 1, 0)
                    for ahead in (3, 4):
                        pair = 2 * quad + ahead
                        if pair < 2 * QUADS:
                            hidden(tile, pair)
                        elif not last:
                            hidden(tile + 1, pair - 2 * QUADS)
                        if ahead == 3:
                            block, k = divmod(quad - PAIRS, KH)
                            if block >= 0:
                                decode(tile, block, k)
                            elif not first:
                                decode(tile - 1, BLOCKS - 1, k)
                    if not first:
                        if quad == OUT1_AT:
                            out1(tile - 1)
                        for half in range(2):
                            if quad == OUT2_AT[half]:
                                out2(tile - 1, half)

            spread(0, 0)
            for pair in range(3):
                hidden(0, pair)
            tile_pe(0, True, False)
            with pe.Fori(1, TILES - 1) as tile:
                tile_pe(tile, False, False)
            tile_pe(TILES - 1, False, True)
            for k in range(KH):
                decode(TILES - 1, BLOCKS - 1, k)
            out1(TILES - 1)
            out2(TILES - 1, 0)
            out2(TILES - 1, 1)


def kernel(**inputs):
    import concourse.bacc as bacc
    from concourse.bass_utils import run_bass_kernel_spmd as run

    a = {k: np.ascontiguousarray(v) for k, v in inputs.items()}

    def ids(x):
        return x.reshape(4, 16, 11, 7).transpose(2, 0, 1, 3)

    m10, m01 = a["mask_BS_i1_0"], a["mask_BS_i0_1"]
    i3, i9 = a["itok_BS_0_3"], a["itok_BS_0_9"]
    tables = [("L0_txt_W_type", m10), ("L0_txt_W_match_tok", m10), ("L0_txt_W_match_ent", m01),
              ("L0_txt_W_sf_tok", i3), ("L0_txt_W_sf_ent", i3), ("L0_txt_W_etype", i9),
              ("L0_txt_W_atype_ent", m10)]
    rows = [a[n].shape[0] for n, _ in tables]
    arrays = {
        "x": a["x"].reshape(64, 3, 4, 16, 4, 16).transpose(1, 3, 5, 0, 2, 4).reshape(768, 1024),
        "tok_w": a["L0_tok_W"].T,
        "tok_b": a["L0_tok_b"].reshape(1, -1),
        "word_ids": ids(a["x_txt"]).transpose(2, 3, 0, 1).reshape(112, 44),
        "pos_ids": ids(a["pos_BS"]).reshape(1, -1),
        "small_ids": np.concatenate([np.repeat(ids(i).reshape(1, -1), r, 0) for (_, i), r in zip(tables, rows)]),
        "row_index": np.concatenate([np.arange(r) for r in rows]).astype(np.float32).reshape(-1, 1),
        "w_word": a["L0_txt_W_word"],
        "w_pos": a["L0_txt_W_pos"],
        "w_small": np.concatenate([a[n] for n, _ in tables]),
        "gamma": a["L0_txt_ln_gamma"].reshape(1, -1),
        "beta": a["L0_txt_ln_beta"].reshape(1, -1),
        "w_qkv": a["L0_attn_w_qkv"],
        "temp": a["L0_attn_temp"],
        "w_out": a["L0_attn_w_out"],
        "b_out": a["L0_attn_b_out"].reshape(1, -1),
        "pz": a["L0_ffn_P"].transpose(1, 0, 2).reshape(192, 128),
        "ct": a["L0_ffn_C"].transpose(0, 2, 1).reshape(128, 64),
        "w1": a["L0_ffn_W1"].reshape(8, 4, 16, 16, 4, 8).transpose(3, 0, 1, 4, 2, 5).reshape(128, 2048),
        "b1": a["L0_ffn_b1"].reshape(8, 4, 16, 4, 8).transpose(0, 1, 3, 2, 4).reshape(128, 128),
        "w2": a["L0_ffn_W2"].reshape(8, 4, 16, 4, 8, 16).transpose(2, 4, 0, 1, 3, 5).reshape(128, 2048),
        "b2": a["L0_ffn_b2"].reshape(4, 2, 64, 16).transpose(1, 2, 0, 3).reshape(128, 4, 16),
        "g1": a["L0_ffn_G1"],
        "g1b": a["L0_ffn_g1b"].reshape(-1, 1),
        "g2": a["L0_ffn_G2"],
        "g2b": a["L0_ffn_g2b"].reshape(1, -1),
    }
    nc = bacc.Bacc("TRN2", target_bir_lowering=False, num_devices=1)
    feed, t = {}, {}
    for name, v in arrays.items():
        v = np.ascontiguousarray(v)
        feed["in_" + name] = v
        t[name] = nc.dram_tensor("in_" + name, v.shape, mybir.dt.from_np(v.dtype), kind="ExternalInput").ap()
    t["out"] = nc.dram_tensor("out_h", (B, N, D), F32, kind="ExternalOutput").ap()
    build(nc, t)
    r = run(nc, [feed], core_ids=[0])
    return r.results[0]["out_h"]
```

```python
from contextlib import ExitStack

import numpy as np

import concourse.bass as bass
from concourse import mybir
from concourse.alu_op_type import AluOpType as ALU

ACT = mybir.ActivationFunctionType
AX = mybir.AxisListType
F32 = mybir.dt.float32
BF16 = mybir.dt.bfloat16
I32 = mybir.dt.int32

B = 64
NI, NT = 16, 77
N = NI + NT
TOK = B * N
D = 192
D1 = D - 128
KIN = 768
KC = KIN // 128
JJ = 11
TT = 112
SMALL = 26
HEADS, DH = 12, 64
INNER = HEADS * DH
CH = INNER // 128
UB = 4
UT = UB * N
ST = 124
SUB = UT // ST
UNITS = B // UB
S, R, M, H, G = 8, 16, 64, 32, 64
E = S * M
TN = 496
TILES = TOK // TN
TSUB = TN // ST
EB, KH = M // 16, H // 8
PAIRS = S // 2
BLOCKS = 2 * EB
QUADS = BLOCKS * PAIRS
ZP = [0, 0, 0, 1, 1, 2]
WP = [0, 1, 2, 0, 1, 0]
ZROWS = 6 * R + 3
SENTINEL = -3.0e38
LATE = 28200
ARENA = 38300
CHOSEN = 3.0e38
EPS_TXT, EPS_LN = 1e-12, 1e-5
POOL_QUADS = [q for q in range(QUADS) if q % 8 == 4]
DVE_QUADS = QUADS - len(POOL_QUADS)
AHEAD = 4
OUT1_AT, OUT2_AT = 8, (11, 13)


def wait(eng, sem, value):
    if isinstance(value, int) and value <= 0:
        return
    eng.wait_ge(sem, value)


def dve_gated(tile, quad):
    return DVE_QUADS * tile + sum(q not in POOL_QUADS for q in range(quad + 1))


def pool_quads(tile, quad):
    return len(POOL_QUADS) * tile + sum(q <= quad for q in POOL_QUADS)


def build(nc, t):
    with ExitStack() as ctx:
        def sem(name):
            return ctx.enter_context(nc.semaphore(name))

        def sb(name, shape, dt=F32):
            return ctx.enter_context(nc.sbuf_tensor(name, shape, dt))

        h0 = nc.dram_tensor("h0_scratch", (TOK, D), F32, kind="Internal").ap()
        h1d = nc.dram_tensor("h1_scratch", (TOK, D), F32, kind="Internal").ap()
        zq = nc.dram_tensor("z_parts", (3, S * R, TOK), BF16, kind="Internal").ap()
        bq = nc.dram_tensor("bias_codes", (S * R, TOK), F32, kind="Internal").ap()
        gq = nc.dram_tensor("gate_parts", (3, E, TOK), BF16, kind="Internal").ap()

        ident = sb("ident", [128, 128])
        w1s = sb("w1_stack", [ZROWS, E * H], BF16)
        w2p = sb("w2_pad", [128, S * 16, 32])
        b2p = sb("b2_pad", [128, PAIRS, 3, 32], BF16)
        sel = sb("sel", [128, 128], BF16)
        g1w = sb("g1w", [128, G])
        g1b = sb("g1b", [G, 1])
        g2w = sb("g2w", [G + 1, D])
        arena = sb("arena", [128, ARENA])

        class Carver:
            def __init__(self, start=0, end=ARENA):
                self.at, self.end = start, end

            def __call__(self, rows, shape, dt=F32):
                words = int(np.prod(shape)) * (2 if dt == BF16 else 4)
                words = -(-words // 4)
                ap = arena[0:rows, self.at:self.at + words]
                self.at += words
                assert self.at <= self.end, self.at
                if dt != F32:
                    ap = ap.bitcast(dt)
                if len(shape) > 1:
                    names = "abcd"[:len(shape)]
                    ap = ap.rearrange(f"p ({' '.join(names)}) -> p {' '.join(names)}",
                                      **{n: k for n, k in zip(names, shape)})
                return ap

        banks = [ctx.enter_context(nc.psum_tensor(f"bank{i}", [128, 512], F32)) for i in range(2)]
        pair0 = ctx.enter_context(nc.psum_tensor("pair0", [128, 2, 512], F32))
        pair1 = ctx.enter_context(nc.psum_tensor("pair1", [128, 2, 512], F32))
        banks += [ctx.enter_context(nc.psum_tensor(f"bank{i}", [128, 512], F32)) for i in range(6, 8)]

        c1 = Carver(0, LATE)
        xt = c1(128, [KC, B * NI])
        cr = Carver(c1.at - KC * B * NI, c1.at)
        w1f = cr(128, [2048])
        w1r = cr(128, [2048])
        w2f = cr(128, [2048])
        wtok = c1(128, [KC, D])
        tokb = c1(1, [D])
        ones_row = c1(1, [128])
        wpos = c1(128, [D])
        wsmall = c1(SMALL, [D])
        rowidx = c1(SMALL, [1])
        iota_i = c1(128, [1], I32)
        iota_f = c1(128, [1])
        widx = c1(TT, [JJ * 4], I32)
        wnow = c1(TT, [2, 4], I32)
        pos_ids = c1(128, [B * NT], I32)
        small_ids = c1(SMALL, [B * NT], I32)
        word = c1(TT, [2, 4, D])
        ohp = c1(128, [2, 4, TT])
        ohs = c1(SMALL, [2, 4, TT])
        emb = c1(TT, [2, 4 * D])
        tst = c1(TT, [4, 6])
        tmv = c1(TT, [4, 2])
        tve = c1(TT, [4])
        trs = c1(TT, [4])
        tneg = c1(TT, [4])
        mhalf = c1(TT, [4])
        tnorm = c1(TT, [2, 4, D])
        tgam = c1(TT, [D])
        tbet = c1(TT, [D])
        tmul = c1(TT, [4, D])
        tout = c1(TT, [2, 4, D])
        img = c1(128, [2, D])
        b1f = c1(128, [128])
        b1r = c1(128, [128])
        b2f = c1(128, [PAIRS, R])
        b2r = c1(128, [PAIRS, R])

        cl = Carver(LATE)
        w1h = cl(128, [3, 2048], BF16)
        b1h = cl(128, [3, 128], BF16)
        wq0, wq1 = cl(128, [INNER]), cl(D1, [INNER])
        wout = cl(128, [CH, D])
        bout = cl(ST, [D])
        tempc = cl(128, [1])
        maskh = cl(128, [CH, HEADS])
        headsel = cl(128, [UB, CH, 128])
        pz0, pz1 = cl(128, [128]), cl(D1, [128])
        cbd = cl(128, [E])

        c2 = Carver(0, LATE)
        wv = c2(128, [CH, UT])
        wsq = c2(128, [CH, UT])
        wpi = c2(128, [CH, UT])
        attended_end = c2.at
        mh2 = c2(ST, [SUB])
        x0 = c2(ST, [SUB, D])
        xr = c2(ST, [SUB, D])
        xb = c2(ST, [SUB, D])
        st = {k: c2(ST, [SUB, 6]) for k in "AG"}
        mv = {k: c2(ST, [SUB, 2]) for k in "AG"}
        ve = {k: c2(ST, [SUB]) for k in "AG"}
        rs = {k: c2(ST, [SUB]) for k in "AG"}
        xn = {k: c2(ST, [SUB, D]) for k in "AG"}
        xt0 = {k: c2(128, [UT]) for k in "AG"}
        xt1 = {k: c2(D1, [UT]) for k in "AG"}
        w2pi = c2(128, [CH, UT])
        n2 = c2(128, [CH, UB])
        n2m = c2(128, [CH, UB])
        inv = c2(128, [CH, UB])
        lsel = c2(128, [UB, CH, 32])
        lg = c2(128, [N])
        nmax = c2(128, [1])
        pe_ = c2(128, [N])
        psm = c2(128, [1])
        prc = c2(128, [1])
        pi = c2(128, [N + 1])
        pss = c2(128, [1])
        pse = c2(128, [1])
        rsc = c2(128, [CH, UB])
        dots = c2(128, [CH, UB])
        dsc = c2(128, [CH, UB])
        dmi = c2(128, [CH, UB])
        natt = c2(128, [CH, UB])
        h1 = c2(ST, [SUB, D])
        zf = c2(128, [UT])
        zr = c2(128, [UT])
        zh = c2(128, [3, UT], BF16)
        sc = c2(ST, [SUB, S, M + 8])
        v8 = c2(ST, [SUB, S, 8])
        v4 = c2(ST, [SUB, S, 8])
        mr = c2(ST, [SUB, S, M + 8])
        sd = c2(ST, [SUB, E])
        se = c2(ST, [SUB, E])
        gu = c2(ST, [SUB, E])
        gs = c2(ST, [SUB, S])
        gr = c2(ST, [SUB, S])
        gg = c2(ST, [SUB, E])
        grr = c2(128, [SUB, 4, ST])
        ct = Carver(LATE, LATE + 3 * 1024 + 3 * 64)
        gh = ct(128, [3, 4, UT], BF16)
        bt = ct(128, [UT])

        c3 = Carver()
        gst = c3(128, [8, 2, TN], BF16)
        zst = c3(ZROWS, [2, PAIRS, TN], BF16)
        assert c3.at <= attended_end
        hid = c3(128, [4, KH, TN])
        gated = c3(128, [2, PAIRS, KH, TN])
        comb = c3(128, [TN])
        gcopy = c3(128, [TN])
        code = c3(128, [TN])
        y1 = c3(G + 1, [TN])
        bias_t = c3(128, [TN])
        h1t = c3(ST, [TSUB, D])
        outt = c3(ST, [2, TSUB, D])

        s_w = sem("weights_loaded")
        s_w1f, s_w2f, s_b2f = sem("w1_raw_loaded"), sem("w2_raw_loaded"), sem("b2_raw_loaded")
        s_const = sem("pool_constants")
        s_cstd = sem("dve_constants")
        s_zero = sem("constants_zeroed")
        s_wc, s_ws = sem("w1_cast_to_part"), sem("w1_rest_taken")
        s_bc, s_br = sem("b2_cast_to_part"), sem("b2_rest_taken")
        s_w2c = sem("w2_placed")
        s_stack = sem("w1_stack_written")
        s_xt = sem("patches_loaded")
        s_tl = sem("text_tables_loaded")
        s_ix = sem("word_ids_loaded")
        s_tneg, s_xm = sem("means_negated"), sem("mean_taken_off")
        s_word = [sem("words_gathered0"), sem("words_gathered1")]
        s_oh, s_tps, s_emb, s_tst = sem("onehots_made"), sem("table_rows_summed"), sem("emb_summed"), sem("text_stats")
        s_tmv, s_tve, s_trs, s_tn = sem("text_moments"), sem("text_var_eps"), sem("text_rstd"), sem("text_normed")
        s_tmul, s_to = sem("text_scaled"), sem("text_ready")
        s_todma = [sem("text_stored0"), sem("text_stored1")]
        s_ips, s_iev = sem("image_summed"), sem("image_copied")
        s_idma = [sem("image_stored0"), sem("image_stored1")]
        s_w2l = sem("attention_weights_loaded")
        s_c2 = sem("attention_constants")
        s_c2d = sem("attention_constants_dve")

        s_x0, s_xr, s_xb = sem("x0_loaded"), sem("residual_loaded"), sem("residual_biased")
        s_st = {k: sem(f"stats_{k}") for k in "AG"}
        s_mv = {k: sem(f"moments_{k}") for k in "AG"}
        s_ve = {k: sem(f"var_eps_{k}") for k in "AG"}
        s_rs = {k: sem(f"rstd_{k}") for k in "AG"}
        s_xn = {k: sem(f"normed_{k}") for k in "AG"}
        s_tp = {k: sem(f"transposed_{k}") for k in "AG"}
        s_xt_ = {k: sem(f"xT_copied_{k}") for k in "AG"}
        s_wp = sem("w_product")
        s_wv, s_wsq = sem("w_copied"), sem("w_squared")
        s_nm, s_inv, s_L = sem("norms_floored"), sem("norms_inverted"), sem("head_weights")
        s_lg, s_lt, s_lm, s_pe = sem("logits"), sem("logits_tempered"), sem("logits_max"), sem("logits_exp")
        s_pr, s_pi, s_ps, s_pse, s_pix = (sem("pi_recip"), sem("pi_made"), sem("pi_sum"), sem("pi_sum_eps"),
                                          sem("pi_complete"))
        s_pb = sem("pi_spread")
        s_wpi, s_rsc = sem("w_pi"), sem("pi_scale_copied")
        s_w2pi = sem("w2_pi")
        s_dt, s_ds, s_dm, s_na = sem("dots_summed"), sem("dots_scaled"), sem("dots_negated"), sem("neg_attn")
        s_o, s_hp, s_h1, s_h1d = sem("attended"), sem("out_product"), sem("h1_ready"), sem("h1_stored")
        s_z, s_zf, s_z1, s_zr, s_z2, s_z3, s_zd = (sem("z_product"), sem("z_copied"), sem("z_part1"), sem("z_rest"),
                                                   sem("z_part2"), sem("z_part3"), sem("z_stored"))
        s_sp, s_sc, s_v8, s_v4, s_mr = (sem("scores"), sem("scores_copied"), sem("top8"), sem("top4"),
                                        sem("chosen_marked"))
        s_sd, s_se, s_gu, s_gs, s_gr, s_gg = (sem("scores_shifted"), sem("scores_exp"), sem("gates_raw"),
                                              sem("gates_summed"), sem("gates_recip"), sem("gates_ready"))
        s_gt, s_g1, s_grr, s_g2, s_g3, s_gd = (sem("gates_transposed"), sem("gate_part1"), sem("gate_rest"),
                                               sem("gate_part2"), sem("gate_part3"), sem("gates_stored"))

        s_gl = [sem(f"gates_loaded{q}") for q in range(4)]
        s_zl = [sem(f"codes_loaded{q}") for q in range(2)]
        s_ones = sem("one_rows_set")
        s_hp1, s_hid = sem("hidden_product"), sem("hidden_gelu")
        s_gb, s_gat = sem("gates_spread"), sem("hidden_gated")
        s_code, s_comb = sem("chunk_decoded"), sem("code_copied")
        s_f1, s_y1, s_f2, s_out = sem("g1_product"), sem("g1_gelu"), sem("g2_product"), sem("out_added")
        s_h1l, s_od = sem("h1_loaded"), [sem("out_stored0"), sem("out_stored1")]

        def wait_apart(eng, *waits):
            held = [(sm, v if isinstance(v, int) else eng.to_reg(v)) for sm, v in waits]
            if any(not isinstance(v, int) for _, v in held):
                eng.wait_ge(s_const, 1)
            for sm, v in held:
                wait(eng, sm, v)

        gate_banks, code_bank, out_bank = banks[0:2], banks[3], banks[2]

        def gt_bank(s):
            return (banks[0], banks[1], pair1[:, 1])[s]

        def chunk(s, block, k):
            return (s * EB + block) * KH + k

        h0_b = h0.rearrange("(b n) d -> b n d", b=B)
        h0_u = h0.rearrange("(u s p) d -> u p s d", s=SUB, p=ST)
        h1_u = h1d.rearrange("(u s p) d -> u p s d", s=SUB, p=ST)
        h1_t = h1d.rearrange("(u s p) d -> u p s d", s=TSUB, p=ST)
        out_t = t["out"].rearrange("b n d -> (b n) d").rearrange("(u s p) d -> u p s d", s=TSUB, p=ST)
        gq_w = gq.rearrange("p (q e) t -> p e q t", e=128)
        gq_r = gq.rearrange("p (j a o f b m) t -> p a o f b m j t", j=2, a=2, o=2, f=2, b=2)
        zq_r = zq.rearrange("p (j o r) t -> p o r j t", j=PAIRS, o=2)

        s_wnow = sem("word_indices_placed")
        s_bp, s_bt, s_bd, s_bl = (sem("bias_product"), sem("bias_copied"), sem("bias_stored"),
                                  sem("bias_loaded"))
        s_cb = sem("bias_added")
        s_gc, s_pg = sem("gates_copied"), sem("hidden_gated_by_pool")

        def stage1_over(eng):
            eng.wait_ge(s_todma[0], 64 * 6)
            eng.wait_ge(s_todma[1], 64 * 5)
            eng.wait_ge(s_idma[0], 16 * 4)
            eng.wait_ge(s_idma[1], 16 * 4)
            eng.wait_ge(s_ws, 2)
            eng.wait_ge(s_bc, 3)
            eng.wait_ge(s_w2c, 1)

        def has(u):
            return not isinstance(u, int) or 0 <= u < UNITS

        def stage2_over(eng):
            eng.wait_ge(s_stack, 16 * 9)
            wait(eng, s_h1d, 16 * UNITS)
            wait(eng, s_zd, 48 * UNITS)
            wait(eng, s_gd, 48 * UNITS)
            wait(eng, s_bd, 16 * UNITS)

        block = ctx.enter_context(nc.Block())

        @block.sync
        def _(sp):
            sp.dma_start(widx, t["word_ids"]).then_inc(s_ix, 16)
            sp.dma_start(rowidx, t["row_index"]).then_inc(s_tl, 16)
            sp.dma_start(small_ids, t["small_ids"]).then_inc(s_tl, 16)
            sp.dma_start(pos_ids, t["pos_ids"][0:1, :].to_broadcast([128, B * NT])).then_inc(s_tl, 16)
            sp.dma_start(wpos, t["w_pos"]).then_inc(s_tl, 16)
            sp.dma_start(wsmall, t["w_small"]).then_inc(s_tl, 16)
            sp.dma_start(tgam, t["gamma"][0:1, :].to_broadcast([TT, D])).then_inc(s_tl, 16)
            sp.dma_start(tbet, t["beta"][0:1, :].to_broadcast([TT, D])).then_inc(s_tl, 16)
            sp.dma_start(wtok, t["tok_w"].rearrange("(c p) e -> p c e", p=128)).then_inc(s_xt, 16)
            sp.dma_start(tokb, t["tok_b"]).then_inc(s_xt, 16)
            sp.dma_start(xt, t["x"].rearrange("(c p) n -> p c n", p=128)).then_inc(s_xt, 16)
            sp.dma_start(b1f, t["b1"]).then_inc(s_w1f, 16)
            sp.dma_start(b2f, t["b2"]).then_inc(s_b2f, 16)
            sp.dma_start(g1w[:], t["g1"]).then_inc(s_w, 16)
            sp.dma_start(g1b[:], t["g1b"]).then_inc(s_w, 16)
            sp.dma_start(g2w[0:G], t["g2"]).then_inc(s_w, 16)
            sp.dma_start(g2w[G:G + 1], t["g2b"]).then_inc(s_w, 16)
            sp.dma_start(wq0, t["w_qkv"][0:128]).then_inc(s_w2l, 16)
            sp.dma_start(wq1, t["w_qkv"][128:D]).then_inc(s_w2l, 16)
            sp.dma_start(wout, t["w_out"].rearrange("(c p) e -> p c e", p=128)).then_inc(s_w2l, 16)
            sp.dma_start(bout, t["b_out"][0:1, :].to_broadcast([ST, D])).then_inc(s_w2l, 16)
            sp.dma_start(pz0, t["pz"][0:128]).then_inc(s_w2l, 16)
            sp.dma_start(pz1, t["pz"][128:D]).then_inc(s_w2l, 16)
            sp.wait_ge(s_zero, 1)
            for b in range(UB):
                sp.dma_start(tempc[32 * b:32 * b + HEADS], t["temp"]).then_inc(s_w2l, 16)
            for s in range(S):
                sp.dma_start(cbd[R * s:R * s + R, M * s:M * s + M], t["ct"][R * s:R * s + R]).then_inc(s_w2l, 16)

            def store_text(jj, par):
                wait_apart(sp, (s_to, jj + 1))
                for bb in range(4):
                    dst = h0_b[16 * bb:16 * bb + 16, bass.ds(NI + 7 * jj, 7), :]
                    sp.dma_start(dst, tout[:, par, bb]).then_inc(s_todma[par], 16)

            store_text(0, 0)
            store_text(1, 1)
            store_text(2, 0)
            with sp.Fori(0, 4) as pr:
                store_text(2 * pr + 3, 1)
                store_text(2 * pr + 4, 0)
            stage1_over(sp)

            def load_x0(u):
                wait_apart(sp, (s_xn["A"], u))
                sp.dma_start(x0, h0_u[u]).then_inc(s_x0, 16)

            def load_xr(u):
                wait_apart(sp, (s_xb, u))
                sp.dma_start(xr, h0_u[u]).then_inc(s_xr, 16)

            def store_h1(u):
                wait_apart(sp, (s_h1, u + 1))
                sp.dma_start(h1_u[u], h1).then_inc(s_h1d, 16)

            def store_codes(u):
                wait_apart(sp, (s_z3, u + 1))
                for p in range(3):
                    sp.dma_start(zq[p, :, bass.ds(u * UT, UT)], zh[:, p]).then_inc(s_zd, 16)

            def store_gates(u):
                wait_apart(sp, (s_g3, SUB * (u + 1)))
                for p in range(3):
                    sp.dma_start(gq_w[p, :, :, bass.ds(u * UT, UT)], gh[:, p]).then_inc(s_gd, 16)

            def store_bias(u):
                wait_apart(sp, (s_bt, u + 1))
                sp.dma_start(bq[:, bass.ds(u * UT, UT)], bt).then_inc(s_bd, 16)

            def pass_sp(i):
                if has(i - 1):
                    load_xr(i - 1)
                if has(i + 1):
                    load_x0(i + 1)
                if has(i - 3):
                    store_gates(i - 3)
                if has(i - 2):
                    store_codes(i - 2)
                if has(i - 3):
                    store_bias(i - 3)
                if has(i - 1):
                    store_h1(i - 1)

            load_x0(0)
            for i in range(6):
                sp.dma_start(w1s[R * i:R * i + R].rearrange("r (s x) -> r s x", s=S),
                             w1h[:, WP[i]]).then_inc(s_stack, 16)
            for p in range(3):
                sp.dma_start(w1s[6 * R + p:6 * R + p + 1], b1h[:, p]).then_inc(s_stack, 16)
            for i in range(4):
                pass_sp(i)
            with sp.Fori(4, UNITS - 1) as i:
                pass_sp(i)
            pass_sp(UNITS - 1)
            pass_sp(UNITS)

            def load_codes(tile, half):
                for i in range(6):
                    sp.dma_start(zst[R * i:R * i + R, half],
                                 zq_r[ZP[i], half, :, :, bass.ds(tile * TN, TN)]).then_inc(s_zl[half], 16)

            def load_gates(tile, q):
                for p in range(3):
                    for a in range(2):
                        for b in range(2):
                            r = 64 * a + 16 * p
                            sp.dma_start(gst[r:r + 16, 2 * q + b],
                                         gq_r[p, a, q // 2, q % 2, b, :, :, bass.ds(tile * TN, TN)]
                                         ).then_inc(s_gl[q], 16)

            sp.wait_ge(s_h1, UNITS)
            sp.wait_ge(s_zd, 48 * (UNITS - 1))
            sp.wait_ge(s_gd, 48 * (UNITS - 2))
            load_codes(0, 0)
            load_gates(0, 0)
            pass_sp(UNITS + 1)
            load_gates(0, 1)
            pass_sp(UNITS + 2)
            load_codes(0, 1)
            load_gates(0, 2)
            load_gates(0, 3)


            stage2_over(sp)

            def load_bias(tile):
                wait_apart(sp, (s_cb, tile))
                sp.dma_start(bias_t, bq[:, bass.ds(tile * TN, TN)]).then_inc(s_bl, 16)

            def load_h1(tile):
                wait_apart(sp, (s_out, TSUB // 2 * tile))
                sp.dma_start(h1t, h1_t[tile]).then_inc(s_h1l, 16)

            def store_out(tile, par):
                wait_apart(sp, (s_out, TSUB // 2 * (tile + 1)))
                sp.dma_start(out_t[tile], outt[:, par]).then_inc(s_od[par], 16)

            load_h1(0)
            load_bias(0)
            for par in range(2):
                sp.sem_inc(s_od[par], 16)

            def refill(tile, q):
                wait_apart(sp, (s_gb, QUADS * (tile - 1) + 8 * (q + 1)),
                           (s_hp1, 2 * QUADS * (tile - 1) + 16 * (q + 1)))
                load_gates(tile, q)
                if q % 2 == 1:
                    load_codes(tile, q // 2)

            refill(1, 0)
            refill(1, 1)
            refill(1, 2)
            refill(1, 3)
            with sp.Fori(0, (TILES - 2) // 2) as i:
                for k in range(2):
                    tile = 2 * i + 1 + k
                    load_bias(tile)
                    store_out(tile - 1, k % 2)
                    load_h1(tile)
                    for q in range(4):
                        refill(tile + 1, q)
            load_bias(TILES - 1)
            store_out(TILES - 2, 0)
            load_h1(TILES - 1)
            store_out(TILES - 1, 1)
            for par in range(2):
                wait_apart(sp, (s_od[par], 16 * (TILES // 2 + 1)))

        @block.gpsimd
        def _(pool):
            p_ = nc.gpsimd
            p_.iota(iota_i, pattern=[[0, 1]], base=0, channel_multiplier=1).then_inc(s_const, 1)
            p_.memset(ones_row, 1.0)
            p_.memset(mhalf, -0.5).then_inc(s_const, 1)

            def gather(jj, par):
                wait_apart(pool, (s_emb, jj - 1))
                p_.tensor_copy(wnow[:, par], widx[:, bass.ds(4 * jj, 4)]).then_inc(s_wnow, 1)
                wait_apart(pool, (s_wnow, jj + 1))
                for bb in range(4):
                    p_.indirect_dma_start(
                        word[:, par, bb], None, t["w_word"],
                        bass.IndirectOffsetOnAxis(ap=wnow[:, par, bb:bb + 1], axis=0)).then_inc(s_word[par], 16)

            def text_rstd(jj):
                wait_apart(pool, (s_tmv, jj + 1))
                p_.tensor_scalar_add(tve, tmv[:, :, 1], EPS_TXT).then_inc(s_tve, 1)
                pool.wait_ge(s_tve, jj + 1)
                p_.tensor_tensor(trs, tve, mhalf, ALU.pow).then_inc(s_trs, 1)

            pool.wait_ge(s_ix, 16)
            gather(0, 0)
            gather(1, 1)
            pool.wait_ge(s_zero, 1)
            p_.affine_select(out=ident[:], in_=ident[:], compare_op=ALU.not_equal, fill=1.0, base=0,
                             pattern=[[-1, 128]], channel_multiplier=1).then_inc(s_const, 1)
            for i in range(6):
                a, p = divmod(i, 3)
                pool.wait_ge(s_const, 3 + i)
                v = sel[:].rearrange("p (e h) -> p e h", e=16)
                p_.affine_select(out=v, in_=v, compare_op=ALU.not_equal, fill=1.0, base=-64 * a - 16 * p,
                                 pattern=[[-1, 16], [0, 8]], channel_multiplier=1).then_inc(s_const, 1)
            text_rstd(0)
            gather(2, 0)
            p_.affine_select(out=maskh, in_=maskh, compare_op=ALU.is_ge, fill=0.0, base=0,
                             pattern=[[128, CH], [-64, HEADS]], channel_multiplier=1).then_inc(s_c2, 1)
            pool.wait_ge(s_c2, 1)
            p_.affine_select(out=maskh, in_=maskh, compare_op=ALU.is_ge, fill=0.0, base=63,
                             pattern=[[-128, CH], [64, HEADS]], channel_multiplier=-1).then_inc(s_c2, 1)
            text_rstd(1)
            gather(3, 1)
            for b in range(UB):
                v = headsel[:, b].rearrange("p c (o d) -> p c o d", o=2)
                p_.affine_select(out=v, in_=v, compare_op=ALU.not_equal, fill=1.0, base=-32 * b,
                                 pattern=[[-2, CH], [-1, 2], [0, DH]], channel_multiplier=1).then_inc(s_c2, 1)
            text_rstd(2)
            gather(4, 0)
            with pool.Fori(0, 3) as pr:
                for k in range(2):
                    jj = 2 * pr + 3 + k
                    text_rstd(jj)
                    gather(jj + 2, 1 - k)
            text_rstd(9)
            text_rstd(10)

            stage1_over(pool)
            p_.memset(lsel, 0.0)
            p_.memset(mh2, -0.5).then_inc(s_c2, 1)
            pool.wait_ge(s_c2, 7)

            def rstd(k, u, eps):
                wait_apart(pool, (s_mv[k], u + 1), (s_xn[k], u))
                p_.tensor_scalar_add(ve[k], mv[k][:, :, 1], eps).then_inc(s_ve[k], 1)
                pool.wait_ge(s_ve[k], u + 1)
                p_.tensor_tensor(rs[k], ve[k], mh2, ALU.pow).then_inc(s_rs[k], 1)

            def z_rest(u):
                pool.wait_ge(s_z1, u + 1)
                p_.tensor_tensor(zr, zf, zh[:, 0], ALU.subtract).then_inc(s_zr, 1)

            def z_part3(u):
                pool.wait_ge(s_z2, u + 1)
                p_.tensor_tensor(zh[:, 2], zr, zh[:, 1], ALU.subtract).then_inc(s_z3, 1)

            def shift(u, s):
                pool.wait_ge(s_v8, SUB * u + s + 1)
                wait(pool, s_se, SUB * u)
                p_.tensor_tensor(sd[:, s].rearrange("p (a b) -> p a b", a=S), sc[:, s, :, 0:M],
                                 v8[:, s, :, 0:1].to_broadcast([ST, S, M]), ALU.subtract).then_inc(s_sd, 1)

            def gates(u, s):
                pool.wait_ge(s_gr, SUB * u + s + 1)
                wait(pool, s_gt, SUB * u)
                p_.tensor_tensor(gg[:, s].rearrange("p (a b) -> p a b", a=S),
                                 gu[:, s].rearrange("p (a b) -> p a b", a=S),
                                 gr[:, s].unsqueeze(2).to_broadcast([ST, S, M]), ALU.mult).then_inc(s_gg, 1)

            def gate_part3(u, s):
                pool.wait_ge(s_g2, SUB * u + s + 1)
                p_.tensor_tensor(gh[:, 2, :, ST * s:ST * s + ST], grr[:, s],
                                 gh[:, 1, :, ST * s:ST * s + ST], ALU.subtract).then_inc(s_g3, 1)

            def w2_pi(u, c):
                pool.wait_ge(s_wpi, CH * u + c + 1)
                p_.tensor_tensor(w2pi[:, c], wpi[:, c], wv[:, c], ALU.mult).then_inc(s_w2pi, 1)

            def attended(u, c):
                if c == 0:
                    pool.wait_ge(s_na, u + 1)
                    pool.wait_ge(s_w2pi, CH * (u + 1))
                o = wpi[:, c].rearrange("p (b n) -> p b n", b=UB)
                p_.tensor_tensor(o, o, natt[:, c].unsqueeze(2).to_broadcast([128, UB, N]), ALU.mult).then_inc(s_o, 1)

            def residual_biased(u):
                pool.wait_ge(s_xr, 16 * (u + 1))
                wait(pool, s_h1, u)
                p_.tensor_tensor(xb, xr, bout.unsqueeze(1).to_broadcast([ST, SUB, D]), ALU.add).then_inc(s_xb, 1)

            def pass_pool(i):
                a, b, g = i, i - 1, i - 2
                if has(g):
                    rstd("G", g, EPS_LN)
                if has(b):
                    w2_pi(b, 0)
                    w2_pi(b, 1)
                if has(g - 1):
                    gate_part3(g - 1, 2)
                if has(b):
                    for c in range(2, CH):
                        w2_pi(b, c)
                if has(g):
                    z_rest(g)
                for c in range(CH):
                    if has(b):
                        attended(b, c)
                    if has(g):
                        if c == 0:
                            shift(g, 0)
                        if c == 3:
                            shift(g, 1)
                if has(g):
                    z_part3(g)
                    gates(g, 0)
                    shift(g, 2)
                if has(b):
                    residual_biased(b)
                if has(g):
                    gates(g, 1)
                    gates(g, 2)
                if has(a + 1):
                    rstd("A", a + 1, EPS_LN)
                if has(g):
                    gate_part3(g, 0)
                    gate_part3(g, 1)

            pool.wait_ge(s_w2l, 16 * (6 + UB + S))
            rstd("A", 0, EPS_LN)
            for i in range(4):
                pass_pool(i)
            with pool.Fori(4, UNITS - 1) as i:
                pass_pool(i)
            for i in range(UNITS - 1, UNITS + 2):
                pass_pool(i)
            gate_part3(UNITS - 1, 2)
            stage2_over(pool)
            pool.wait_ge(s_ones, 1)
            p_.memset(y1[G:G + 1], 1.0).then_inc(s_ones, 1)

            def gate_quad(tile, quad):
                block, j = divmod(quad, PAIRS)
                wait(pool, s_code, QUADS * tile + PAIRS * (block - 1))
                pool.wait_ge(s_gc, pool_quads(tile, quad))
                pool.wait_ge(s_hid, 2 * QUADS * tile + 2 * quad + 2)
                for half in range(2):
                    pair = slice(2 * half, 2 * half + 2)
                    p_.tensor_tensor(gated[:, block % 2, j, pair], hid[:, quad % 4, pair],
                                     gcopy.unsqueeze(1).to_broadcast([128, 2, TN]), ALU.mult).then_inc(s_pg, 1)

            def add_bias(tile):
                wait_apart(pool, (s_comb, tile + 1), (s_bl, 16 * (tile + 1)))
                p_.tensor_tensor(code, comb, bias_t, ALU.add).then_inc(s_cb, 1)

            def pool_tile(tile, first):
                for quad in POOL_QUADS:
                    gate_quad(tile, quad)
                    if quad == POOL_QUADS[0] and not first:
                        add_bias(tile - 1)

            pool_tile(0, True)
            with pool.Fori(1, TILES) as tile:
                pool_tile(tile, False)
            add_bias(TILES - 1)

        @block.scalar
        def _(act):
            a_ = nc.scalar
            def image(k):
                act.wait_ge(s_ips, k + 1)
                wait(act, s_idma[k % 2], 16 * (k // 2))
                a_.copy(img[:, k % 2], banks[k % 2][:, 0:D]).then_inc(s_iev, 1)
                act.wait_ge(s_iev, k + 1)
                act.dma_start(h0_b[8 * k:8 * k + 8, 0:NI, :], img[:, k % 2]).then_inc(s_idma[k % 2], 16)

            def mean_off(jj):
                act.wait_ge(s_tneg, jj + 1)
                wait(act, s_tmul, jj - 1)
                for bb in range(4):
                    last = a_.activation(tnorm[:, jj % 2, bb], emb[:, jj % 2, D * bb:D * bb + D], ACT.Identity,
                                         bias=tneg[:, bb:bb + 1])
                last.then_inc(s_xm, 1)

            def b2_part(part, src):
                wait(act, s_br, part)
                for o in range(2):
                    rows = slice(64 * o, 64 * o + 64)
                    last = a_.copy(b2p[rows, :, part, 16 * o:16 * o + 16], src[rows])
                last.then_inc(s_bc, 1)

            for jj in range(JJ):
                mean_off(jj)
                if jj < 4:
                    image(2 * jj)
                    image(2 * jj + 1)
                if jj == 3:
                    act.wait_ge(s_ips, 8)
                    act.dma_start(w1f, t["w1"]).then_inc(s_w1f, 16)
                    act.dma_start(w2f, t["w2"]).then_inc(s_w2f, 16)
                if jj == 7:
                    act.wait_ge(s_w1f, 32)
                    a_.copy(w1h[:, 0], w1f)
                    a_.copy(b1h[:, 0], b1f).then_inc(s_wc, 1)
                    act.wait_ge(s_b2f, 16)
                    act.wait_ge(s_zero, 1)
                    b2_part(0, b2f)
                if jj == 8:
                    act.wait_ge(s_w2f, 16)
                    w2v = w2f.rearrange("p (j o g r) -> p j o g r", j=PAIRS, o=2, g=16)
                    w2o = w2p[:].rearrange("p (j o g) c -> p j o g c", j=PAIRS, o=2)
                    for o in range(2):
                        last = a_.copy(w2o[:, :, o, :, 16 * o:16 * o + 16], w2v[:, :, o])
                    last.then_inc(s_w2c, 1)
                if jj == 9:
                    act.wait_ge(s_ws, 1)
                    a_.copy(w1h[:, 1], w1r)
                    a_.copy(b1h[:, 1], b1r).then_inc(s_wc, 1)
                    b2_part(1, b2r)
            b2_part(2, b2r)

            stage1_over(act)

            def xT(k, u):
                act.wait_ge(s_tp[k], u + 1)
                a_.copy(xt0[k], banks[0][:, 0:UT])
                a_.copy(xt1[k], banks[1][0:D1, 0:UT]).then_inc(s_xt_[k], 1)

            def w_copy(u, c):
                act.wait_ge(s_wp, CH * u + c + 1)
                wait(act, s_w2pi, CH * (u - 1) + c + 1)
                src = pair0[:, c % 2, 0:UT]
                a_.copy(wv[:, c], src).then_inc(s_wv, 1)
                for b in range(UB):
                    last = a_.activation(wsq[:, c, N * b:N * b + N], src[:, N * b:N * b + N], ACT.Square,
                                         accum_out=n2[:, c, b:b + 1])
                last.then_inc(s_wsq, 1)

            def copy_bias(u):
                act.wait_ge(s_bp, u + 1)
                wait(act, s_bd, 16 * u)
                a_.copy(bt, pair1[:, 0, 0:UT]).then_inc(s_bt, 1)

            def z_copies(u):
                act.wait_ge(s_z, u + 1)
                wait(act, s_zd, 48 * u)
                wait(act, s_z3, u)
                a_.copy(zf, pair1[:, 1, 0:UT]).then_inc(s_zf, 1)
                a_.copy(zh[:, 0], pair1[:, 1, 0:UT]).then_inc(s_z1, 1)

            def z_part2(u):
                act.wait_ge(s_zr, u + 1)
                a_.copy(zh[:, 1], zr).then_inc(s_z2, 1)

            def scores_copy(u, s):
                act.wait_ge(s_sp, SUB * u + s + 1)
                wait(act, s_mr, SUB * u)
                wait(act, s_sd, SUB * u)
                a_.copy(sc[:, s, :, 0:M], banks[2][0:ST, :].rearrange("p (a b) -> p a b", a=S)).then_inc(s_sc, 1)

            def logits_exp(u):
                act.wait_ge(s_lm, u + 1)
                a_.activation(pe_, lg, ACT.Exp, bias=nmax, accum_out=psm).then_inc(s_pe, 1)

            def scores_exp(u, s):
                act.wait_ge(s_sd, SUB * u + s + 1)
                wait(act, s_gu, SUB * u)
                a_.activation(se[:, s], sd[:, s], ACT.Exp).then_inc(s_se, 1)

            def gate_part1(u, s):
                act.wait_ge(s_gt, SUB * u + s + 1)
                if s == 0:
                    wait(act, s_gd, 48 * u)
                    wait(act, s_bp, u)
                a_.copy(gh[:, 0, :, ST * s:ST * s + ST],
                        gt_bank(s)[:, 0:4 * ST].rearrange("p (a b) -> p a b", a=4)).then_inc(s_g1, 1)

            def gate_part2(u, s):
                act.wait_ge(s_grr, SUB * u + s + 1)
                a_.copy(gh[:, 1, :, ST * s:ST * s + ST], grr[:, s]).then_inc(s_g2, 1)

            def pass_act(i):
                a, g = i, i - 2
                if has(a):
                    xT("A", a)
                if has(g - 1):
                    gate_part2(g - 1, 2)
                if has(g):
                    xT("G", g)
                if has(g):
                    z_copies(g)
                for c in range(CH):
                    if has(a):
                        w_copy(a, c)
                    if has(g):
                        if c < SUB:
                            scores_copy(g, c)
                        if c == 1:
                            z_part2(g)
                            scores_exp(g, 0)
                        if c == 4:
                            scores_exp(g, 1)
                if has(g - 1):
                    copy_bias(g - 1)
                if has(g):
                    scores_exp(g, 2)
                    gate_part1(g, 0)
                if has(a):
                    logits_exp(a)
                if has(g):
                    gate_part2(g, 0)
                    gate_part1(g, 1)
                    gate_part2(g, 1)
                    gate_part1(g, 2)

            for i in range(4):
                if i == 2:
                    act.wait_ge(s_stack, 16 * 9)
                pass_act(i)
            with act.Fori(4, UNITS) as i:
                pass_act(i)
            for i in range(UNITS, UNITS + 2):
                pass_act(i)
            gate_part2(UNITS - 1, 2)
            copy_bias(UNITS - 1)

            stage2_over(act)
            act.wait_ge(s_ones, 2)
            act.wait_ge(s_w, 64)

            def gelu(tile, pair):
                quad = pair // 2
                act.wait_ge(s_hp1, 2 * QUADS * tile + pair + 1)
                before = (tile, quad - 4) if quad >= 4 else (tile - 1, quad - 4 + QUADS)
                if before[1] in POOL_QUADS:
                    wait(act, s_pg, 2 * pool_quads(*before) - 1 + pair % 2)
                elif pair % 2 == 0:
                    wait(act, s_gat, dve_gated(*before))
                a_.activation(hid[:, quad % 4, 2 * (pair % 2):2 * (pair % 2) + 2], (pair0, pair1)[pair % 2][:, :, 0:TN],
                              ACT.Gelu_apprx_tanh).then_inc(s_hid, 1)

            def copy_gates(tile, quad):
                act.wait_ge(s_gb, QUADS * tile + quad + 1)
                wait(act, s_pg, 2 * pool_quads(tile, quad) - 2)
                a_.copy(gcopy, gate_banks[quad % 2][:, 0:TN]).then_inc(s_gc, 1)

            def copy_code(tile):
                act.wait_ge(s_code, QUADS * (tile + 1))
                a_.copy(comb, code_bank[:, 0:TN]).then_inc(s_comb, 1)

            def gelu_out(tile):
                act.wait_ge(s_f1, tile + 1)
                a_.activation(y1[0:G], out_bank[0:G, 0:TN], ACT.Gelu_apprx_tanh,
                              bias=g1b[:]).then_inc(s_y1, 1)

            def tile_act(tile, first):
                for pair in range(2 * QUADS):
                    gelu(tile, pair)
                    if pair % 2 == 1 and pair // 2 in POOL_QUADS:
                        copy_gates(tile, pair // 2)
                    if not first:
                        if pair == 9:
                            copy_code(tile - 1)
                        if pair == 2 * OUT1_AT + 5:
                            gelu_out(tile - 1)

            tile_act(0, True)
            with act.Fori(1, TILES) as tile:
                tile_act(tile, False)
            copy_code(TILES - 1)
            gelu_out(TILES - 1)

        @block.vector
        def _(dve):
            v_ = nc.vector
            v_.memset(ident[:], 0.0)
            v_.memset(sel[:], 0.0)
            v_.memset(tempc, 0.0)
            v_.memset(cbd, 0.0)
            v_.memset(maskh, 1.0)
            v_.memset(headsel, 0.0)
            v_.memset(b2p[:], 0.0)
            v_.memset(w2p[:], 0.0).then_inc(s_zero, 1)
            dve.wait_ge(s_const, 1)
            v_.tensor_copy(iota_f, iota_i).then_inc(s_cstd, 1)
            dve.wait_ge(s_tl, 16 * 7)
            v_.tensor_scalar(small_ids[0:2], small_ids[0:2], 0, None, ALU.is_gt).then_inc(s_cstd, 1)
            dve.wait_ge(s_cstd, 2)

            def onehots(jj, par):
                wait(dve, s_tps, jj - 1)
                v_.tensor_scalar(ohp[:, par].rearrange("p a b -> p (a b)"), pos_ids[:, bass.ds(jj * 448, 448)],
                                 iota_f, None, ALU.is_equal)
                v_.tensor_scalar(ohs[:, par].rearrange("p a b -> p (a b)"), small_ids[:, bass.ds(jj * 448, 448)],
                                 rowidx, None, ALU.is_equal).then_inc(s_oh, 1)

            def scaled(jj, par):
                dve.wait_ge(s_xm, jj + 1)
                dve.wait_ge(s_trs, jj + 1)
                for bb in range(4):
                    last = v_.scalar_tensor_tensor(out=tmul[:, bb], in0=tnorm[:, par, bb], scalar=trs[:, bb:bb + 1],
                                                   in1=tgam, op0=ALU.mult, op1=ALU.mult)
                last.then_inc(s_tmul, 1)

            def shifted(jj, par):
                dve.wait_ge(s_tmul, jj + 1)
                wait(dve, s_todma[par], use_count(jj, par))
                v_.tensor_tensor(tout[:, par], tmul, tbet.unsqueeze(1).to_broadcast([TT, 4, D]),
                                 ALU.add).then_inc(s_to, 1)

            def use_count(jj, par):
                if isinstance(jj, int):
                    return 64 * (jj // 2)
                return 32 * (jj - par)

            def text_step(jj, par):
                old = not isinstance(jj, int) or jj > 0
                if not isinstance(jj, int) or jj + 1 < JJ:
                    onehots(jj + 1, 1 - par)
                dve.wait_ge(s_tps, jj + 1)
                if isinstance(jj, int):
                    dve.wait_ge(s_word[par], 64 * (jj // 2 + 1))
                else:
                    dve.wait_ge(s_word[par], 32 * (jj - par) + 64)
                v_.tensor_tensor(emb[:, par].rearrange("p (a b) -> p a b", a=2),
                                 (pair0, pair1)[par][0:TT, :, 0:2 * D],
                                 word[:, par].rearrange("p (a b) d -> p a (b d)", a=2), ALU.add).then_inc(s_emb, 1)
                if old:
                    scaled(jj - 1, 1 - par)
                dve.wait_ge(s_emb, jj + 1)
                for bb in range(4):
                    last = v_.bn_stats(tst[:, bb], emb[:, par, D * bb:D * bb + D])
                last.then_inc(s_tst, 1)
                if old:
                    shifted(jj - 1, 1 - par)
                wait_apart(dve, (s_tst, jj + 1))
                for bb in range(4):
                    last = v_.bn_aggr(tmv[:, bb], tst[:, bb])
                last.then_inc(s_tmv, 1)
                dve.wait_ge(s_tmv, jj + 1)
                v_.tensor_scalar(tneg, tmv[:, :, 0], -1.0, None, ALU.mult).then_inc(s_tneg, 1)

            onehots(0, 0)
            for jj in range(3):
                text_step(jj, jj % 2)
            with dve.Fori(0, 3) as pr:
                for k in range(2):
                    text_step(2 * pr + 3 + k, 1 - k)

            def b2_rest(part, src):
                dve.wait_ge(s_bc, part + 1)
                for o in range(2):
                    rows = slice(64 * o, 64 * o + 64)
                    last = v_.tensor_tensor(b2r[rows], src[rows], b2p[rows, :, part, 16 * o:16 * o + 16],
                                            ALU.subtract)
                last.then_inc(s_br, 1)

            dve.wait_ge(s_wc, 1)
            v_.tensor_tensor(b1r, b1f, b1h[:, 0], ALU.subtract)
            v_.tensor_tensor(w1r, w1f, w1h[:, 0], ALU.subtract).then_inc(s_ws, 1)
            b2_rest(0, b2f)
            text_step(9, 1)
            text_step(10, 0)
            scaled(10, 0)
            shifted(10, 0)
            dve.wait_ge(s_wc, 2)
            v_.tensor_tensor(b1h[:, 2], b1r, b1h[:, 1], ALU.subtract)
            v_.tensor_tensor(w1h[:, 2], w1r, w1h[:, 1], ALU.subtract).then_inc(s_ws, 1)
            dve.wait_ge(s_br, 1)
            b2_rest(1, b2r)

            stage1_over(dve)
            v_.memset(sc[:, :, :, M:M + 8], SENTINEL)
            v_.memset(v4, SENTINEL).then_inc(s_c2d, 1)
            dve.wait_ge(s_c2, 7)
            dve.wait_ge(s_c2d, 1)
            dve.wait_ge(s_w2l, 16 * (6 + UB + S))

            def bn_stats(k, u, src):
                for s in range(SUB):
                    last = v_.bn_stats(st[k][:, s], src[:, s])
                last.then_inc(s_st[k], 1)

            def bn_aggr(k, u):
                wait_apart(dve, (s_st[k], u + 1))
                for s in range(SUB):
                    last = v_.bn_aggr(mv[k][:, s], st[k][:, s])
                last.then_inc(s_mv[k], 1)

            def norm(k, u, src, s):
                if s == 0:
                    dve.wait_ge(s_rs[k], u + 1)
                    wait(dve, s_tp[k], u)
                one = v_.tensor_scalar(xn[k][:, s], src[:, s], mv[k][:, s, 0:1], rs[k][:, s:s + 1],
                                       ALU.subtract, ALU.mult)
                if s == SUB - 1:
                    one.then_inc(s_xn[k], 1)

            def top8(u, s):
                n = SUB * u + s
                wait_apart(dve, (s_sc, n + 1), (s_sd, SUB * u))
                for g in range(S):
                    last = v_.max(v8[:, s, g], sc[:, s, g, 0:M])
                last.then_inc(s_v8, 1)

            def top4(u, s):
                dve.wait_ge(s_v8, SUB * u + s + 1)
                v_.tensor_copy(v4[:, s, :, 0:4], v8[:, s, :, 0:4]).then_inc(s_v4, 1)

            def mark(u, s):
                wait_apart(dve, (s_v4, SUB * u + s + 1))
                for g in range(S):
                    last = v_.match_replace(mr[:, s, g], v4[:, s, g], sc[:, s, g], CHOSEN)
                last.then_inc(s_mr, 1)

            def raw(u, s):
                n = SUB * u + s
                dve.wait_ge(s_se, n + 1)
                dve.wait_ge(s_mr, n + 1)
                wait(dve, s_gg, SUB * u)
                v_.scalar_tensor_tensor(out=gu[:, s].rearrange("p (a b) -> p a b", a=S), in0=mr[:, s, :, 0:M],
                                        scalar=CHOSEN, in1=se[:, s].rearrange("p (a b) -> p a b", a=S),
                                        op0=ALU.is_equal, op1=ALU.mult).then_inc(s_gu, 1)

            def raw_sum(u, s):
                dve.wait_ge(s_gu, SUB * u + s + 1)
                v_.tensor_reduce(gs[:, s], gu[:, s].rearrange("p (a b) -> p a b", a=S), AX.X, ALU.add).then_inc(s_gs, 1)

            def raw_recip(u, s):
                dve.wait_ge(s_gs, SUB * u + s + 1)
                v_.reciprocal(gr[:, s], gs[:, s]).then_inc(s_gr, 1)

            def rest(u, s):
                n = SUB * u + s
                dve.wait_ge(s_g1, n + 1)
                wait(dve, s_g3, SUB * u)
                v_.tensor_tensor(grr[:, s], gt_bank(s)[:, 0:4 * ST].rearrange("p (a b) -> p a b", a=4),
                                 gh[:, 0, :, ST * s:ST * s + ST], ALU.subtract).then_inc(s_grr, 1)

            def pi_recip(u):
                dve.wait_ge(s_pe, u + 1)
                v_.reciprocal(prc, psm).then_inc(s_pr, 1)

            def pi_made(u):
                dve.wait_ge(s_pr, u + 1)
                v_.tensor_scalar(pi[:, 0:N], pe_, prc, None, ALU.mult).then_inc(s_pi, 1)

            def pi_sum(u):
                dve.wait_ge(s_pi, u + 1)
                v_.tensor_reduce(pss, pi[:, 0:N], AX.X, ALU.add).then_inc(s_ps, 1)

            def pi_sum_eps(u):
                dve.wait_ge(s_ps, u + 1)
                v_.tensor_scalar(pse, pss, 1e-8, None, ALU.add).then_inc(s_pse, 1)

            def pi_complete(u):
                dve.wait_ge(s_pse, u + 1)
                v_.reciprocal(pi[:, N:N + 1], pse).then_inc(s_pix, 1)

            def w_pi(u, c):
                dve.wait_ge(s_pb, CH * u + c + 1)
                pb = pair0[:, c % 2, 0:UB * (N + 1)].rearrange("p (b n) -> p b n", b=UB)
                v_.tensor_tensor(wpi[:, c].rearrange("p (b n) -> p b n", b=UB),
                                 wv[:, c].rearrange("p (b n) -> p b n", b=UB), pb[:, :, 0:N],
                                 ALU.mult).then_inc(s_wpi, 1)
                v_.tensor_copy(rsc[:, c], pb[:, :, N]).then_inc(s_rsc, 1)

            def attn_dots(u, c):
                dve.wait_ge(s_w2pi, CH * u + c + 1)
                v_.tensor_reduce(dots[:, c], w2pi[:, c].rearrange("p (b n) -> p b n", b=UB), AX.X,
                                 ALU.add).then_inc(s_dt, 1)

            def neg_attn(u):
                dve.wait_ge(s_dt, CH * (u + 1))
                dve.wait_ge(s_rsc, CH * (u + 1))
                v_.tensor_tensor(dsc, dots, rsc, ALU.mult).then_inc(s_ds, 1)
                dve.wait_ge(s_ds, u + 1)
                v_.tensor_scalar(dmi, dsc, -1.0, -1.0, ALU.mult, ALU.add).then_inc(s_dm, 1)
                dve.wait_ge(s_dm, u + 1)
                v_.reciprocal(natt, dmi).then_inc(s_na, 1)

            def norms_floored(u):
                dve.wait_ge(s_wsq, CH * (u + 1))
                v_.tensor_scalar(n2m, n2, 1e-24, None, ALU.max).then_inc(s_nm, 1)

            def norms_inverted(u):
                dve.wait_ge(s_nm, u + 1)
                v_.reciprocal(inv, n2m).then_inc(s_inv, 1)

            def head_weights(u):
                dve.wait_ge(s_inv, u + 1)
                for b in range(UB):
                    last = v_.tensor_tensor(lsel[:, b, :, 0:HEADS], maskh,
                                            inv[:, :, b:b + 1].to_broadcast([128, CH, HEADS]), ALU.mult)
                last.then_inc(s_L, 1)

            def logits_max(u):
                dve.wait_ge(s_lg, u + 1)
                v_.tensor_scalar(lg, pair1[:, 0, 0:N], tempc, None, ALU.mult).then_inc(s_lt, 1)
                dve.wait_ge(s_lt, u + 1)
                v_.tensor_reduce(nmax, lg, AX.X, ALU.max, negate=True).then_inc(s_lm, 1)

            def residual(u, half):
                if half == 0:
                    dve.wait_ge(s_hp, u + 1)
                    dve.wait_ge(s_xb, u + 1)
                    wait(dve, s_h1d, 16 * u)
                    v_.tensor_tensor(h1[:, 0:2], banks[3][0:ST, 0:2 * D].rearrange("p (a b) -> p a b", a=2),
                                     xb[:, 0:2], ALU.add)
                else:
                    v_.tensor_tensor(h1[:, 2], banks[2][0:ST, 0:D], xb[:, 2], ALU.add).then_inc(s_h1, 1)

            def pass_dve(i):
                a, b, g = i, i - 1, i - 2
                if has(b):
                    w_pi(b, 0)
                if has(g):
                    bn_aggr("G", g)
                if has(b):
                    w_pi(b, 1)
                if has(g - 1):
                    rest(g - 1, 2)
                if has(g):
                    for s in range(SUB):
                        norm("G", g, h1, s)
                if has(g) and not has(b):
                    v_.memset(zst[96:ZROWS], 1.0).then_inc(s_ones, 1)
                if has(b):
                    w_pi(b, 2)
                    w_pi(b, 3)
                    attn_dots(b, 0)
                    attn_dots(b, 1)
                    w_pi(b, 4)
                    w_pi(b, 5)
                    for c in range(2, CH):
                        attn_dots(b, c)
                    neg_attn(b)
                if has(g):
                    top8(g, 0)
                    top4(g, 0)
                    mark(g, 0)
                    top8(g, 1)
                    top4(g, 1)
                    raw(g, 0)
                    mark(g, 1)
                    raw_sum(g, 0)
                    top8(g, 2)
                    raw_recip(g, 0)
                    top4(g, 2)
                    raw(g, 1)
                    mark(g, 2)
                if has(a):
                    norms_floored(a)
                if has(g):
                    raw_sum(g, 1)
                if has(a):
                    norms_inverted(a)
                if has(g):
                    raw_recip(g, 1)
                if has(a):
                    head_weights(a)
                if has(g):
                    raw(g, 2)
                if has(a + 1):
                    dve.wait_ge(s_x0, 16 * (a + 2))
                    bn_stats("A", a + 1, x0)
                if has(g):
                    raw_sum(g, 2)
                if has(a + 1):
                    bn_aggr("A", a + 1)
                if has(g):
                    raw_recip(g, 2)
                if has(a):
                    logits_max(a)
                if has(g):
                    rest(g, 0)
                if has(a):
                    pi_recip(a)
                    pi_made(a)
                    pi_sum(a)
                    pi_sum_eps(a)
                    pi_complete(a)
                if has(a + 1):
                    for s in range(SUB):
                        norm("A", a + 1, x0, s)
                if has(g):
                    rest(g, 1)
                if has(b):
                    residual(b, 0)
                    residual(b, 1)
                if has(b):
                    dve.wait_ge(s_h1, b + 1)
                    bn_stats("G", b, h1)

            dve.wait_ge(s_x0, 16)
            bn_stats("A", 0, x0)
            bn_aggr("A", 0)
            for s in range(SUB):
                norm("A", 0, x0, s)
            for i in range(4):
                pass_dve(i)
            with dve.Fori(4, UNITS - 1) as i:
                pass_dve(i)
            for i in range(UNITS - 1, UNITS + 2):
                pass_dve(i)
            rest(UNITS - 1, 2)

            stage2_over(dve)

            def gate_quad(tile, quad):
                dve.wait_ge(s_hid, 2 * QUADS * tile + 2 * quad + 2)
                dve.wait_ge(s_gb, QUADS * tile + quad + 1)
                block, j = divmod(quad, PAIRS)
                if j == 0 or quad - 1 in POOL_QUADS:
                    wait(dve, s_code, QUADS * tile + PAIRS * (block - 1))
                v_.tensor_tensor(gated[:, block % 2, j], hid[:, quad % 4],
                                 gate_banks[quad % 2][:, 0:TN].unsqueeze(1).to_broadcast([128, KH, TN]),
                                 ALU.mult).then_inc(s_gat, 1)

            def add_out(tile, half, par):
                dve.wait_ge(s_f2, 2 * tile + half + 1)
                if half == 0:
                    dve.wait_ge(s_h1l, 16 * (tile + 1))
                    if isinstance(tile, int):
                        dve.wait_ge(s_od[par], 16 * (tile // 2 + 1))
                    else:
                        wait(dve, s_od[par], 8 * (tile - par) + 16)
                v_.tensor_tensor(outt[:, par, 2 * half:2 * half + 2],
                                 out_bank[0:ST, 0:2 * D].rearrange("p (a b) -> p a b", a=2),
                                 h1t[:, 2 * half:2 * half + 2], ALU.add).then_inc(s_out, 1)

            def tile_dve(tile, par, first):
                for quad in range(QUADS):
                    if quad not in POOL_QUADS:
                        gate_quad(tile, quad)
                    if not first:
                        for half in range(2):
                            if quad == OUT2_AT[half] + 1:
                                add_out(tile - 1, half, 1 - par)

            tile_dve(0, 0, True)
            with dve.Fori(0, (TILES - 2) // 2) as i:
                for k in range(2):
                    tile_dve(2 * i + 1 + k, 1 - k, False)
            tile_dve(TILES - 1, 1, False)
            add_out(TILES - 1, 0, 1)
            add_out(TILES - 1, 1, 1)

        @block.tensor
        def _(pe):
            t_ = nc.tensor
            def image(k):
                wait(pe, s_iev, k - 1)
                for c in range(KC):
                    t_.matmul(banks[k % 2][:, 0:D], xt[:, c, 128 * k:128 * k + 128], wtok[:, c],
                              start=(c == 0), stop=False)
                t_.matmul(banks[k % 2][:, 0:D], ones_row, tokb, start=False, stop=True).then_inc(s_ips, 1)

            def tables(jj, par):
                pe.wait_ge(s_oh, jj + 1)
                wait(pe, s_emb, jj - 1)
                for bb in range(4):
                    o = (pair0, pair1)[par][0:TT, bb // 2, D * (bb % 2):D * (bb % 2) + D]
                    t_.matmul(o, ohp[:, par, bb], wpos, start=True, stop=False)
                    last = t_.matmul(o, ohs[:, par, bb], wsmall, start=False, stop=True)
                last.then_inc(s_tps, 1)

            pe.wait_ge(s_tl, 16 * 7)
            tables(0, 0)
            tables(1, 1)
            pe.wait_ge(s_xt, 48)
            pe.wait_ge(s_const, 2)
            for jj in range(2, 6):
                image(2 * jj - 4)
                image(2 * jj - 3)
                tables(jj, jj % 2)
            tables(6, 0)
            with pe.Fori(0, 2) as pr:
                tables(2 * pr + 7, 1)
                tables(2 * pr + 8, 0)

            stage1_over(pe)
            pe.wait_ge(s_const, 9)
            pe.wait_ge(s_c2, 7)
            pe.wait_ge(s_w2l, 16 * (6 + UB + S))

            def transposes(k, u, other_done):
                pe.wait_ge(s_xn[k], u + 1)
                wait(pe, *other_done)
                for s in range(SUB):
                    t_.transpose(banks[0][:, ST * s:ST * s + ST], xn[k][:, s, 0:128], ident[0:ST, 0:ST])
                    last = t_.transpose(banks[1][0:D1, ST * s:ST * s + ST], xn[k][:, s, 128:D],
                                        ident[0:ST, 0:ST])
                last.then_inc(s_tp[k], 1)

            def w_product(u, c):
                if c == 0:
                    pe.wait_ge(s_xt_["A"], u + 1)
                if c < 2:
                    wait(pe, s_rsc, CH * (u - 1) + 5 + c)
                else:
                    wait(pe, s_wsq, CH * u + c - 1)
                o = pair0[:, c % 2, 0:UT]
                t_.matmul(o, wq0[:, 128 * c:128 * c + 128], xt0["A"], start=True, stop=False)
                t_.matmul(o, wq1[:, 128 * c:128 * c + 128], xt1["A"], start=False, stop=True).then_inc(s_wp, 1)

            def bias(u):
                pe.wait_ge(s_g3, SUB * (u + 1))
                wait(pe, s_lt, u + 3 if has(u + 2) else UNITS)
                for i in range(6):
                    for j in range(PAIRS):
                        mm = t_.matmul(pair1[32 * j:32 * j + 32, 0, 0:UT], b2p[:, j, WP[i]], gh[:, ZP[i], j],
                                       start=(i == 0), stop=(i == 5), skip_group_check=True)
                mm.then_inc(s_bp, 1)

            def z_product(u):
                pe.wait_ge(s_xt_["G"], u + 1)
                wait(pe, s_grr, SUB * u)
                t_.matmul(pair1[:, 1, 0:UT], pz0, xt0["G"], start=True, stop=False)
                t_.matmul(pair1[:, 1, 0:UT], pz1, xt1["G"], start=False, stop=True).then_inc(s_z, 1)

            def scores(u, s):
                if s == 0:
                    pe.wait_ge(s_zf, u + 1)
                    pe.wait_ge(s_h1, u + 1)
                wait(pe, s_sc, SUB * u + s)
                t_.matmul(banks[2][0:ST, :], zf[:, ST * s:ST * s + ST], cbd, start=True, stop=True).then_inc(s_sp, 1)

            def logits(u):
                pe.wait_ge(s_L, u + 1)
                wait(pe, s_bt, u - 2)
                for b in range(UB):
                    for c in range(CH):
                        last = t_.matmul(pair1[32 * b:32 * b + 32, 0, 0:N], lsel[:, b, c],
                                         wsq[:, c, N * b:N * b + N], start=(c == 0), stop=(c == CH - 1))
                last.then_inc(s_lg, 1)

            def spread_pi(u, c):
                pe.wait_ge(s_pix, u + 1)
                if c < 2:
                    pe.wait_ge(s_wsq, CH * u + 5 + c)
                else:
                    wait(pe, s_rsc, CH * u + c - 1)
                for b in range(UB):
                    last = t_.matmul(pair0[:, c % 2, (N + 1) * b:(N + 1) * (b + 1)], headsel[:, b, c],
                                     pi, start=True, stop=True)
                last.then_inc(s_pb, 1)

            def gates_transposed(u, s):
                pe.wait_ge(s_z1, u + 1)
                pe.wait_ge(s_gg, SUB * u + s + 1)
                for q in range(4):
                    last = t_.transpose(gt_bank(s)[:, ST * q:ST * q + ST], gg[:, s, 128 * q:128 * q + 128],
                                        ident[0:ST, 0:ST])
                last.then_inc(s_gt, 1)

            def out_product(u, s):
                if s == 0:
                    pe.wait_ge(s_o, CH * (u + 1))
                    wait(pe, s_h1, u)
                if s == 2:
                    wait(pe, s_sc, SUB * u)
                o = banks[3][0:ST, D * s:D * s + D] if s < 2 else banks[2][0:ST, 0:D]
                for c in range(CH):
                    last = t_.matmul(o, wpi[:, c, ST * s:ST * s + ST], wout[:, c], start=(c == 0), stop=(c == CH - 1))
                if s == 2:
                    last.then_inc(s_hp, 1)

            def pass_pe(i):
                a, b, g = i, i - 1, i - 2
                gates_read = (s_grr, SUB * (g - 1) + 2)
                if has(b):
                    spread_pi(b, 0)
                    spread_pi(b, 1)
                if has(a):
                    transposes("A", a, gates_read)
                if has(b):
                    spread_pi(b, 2)
                    spread_pi(b, 3)
                if has(g):
                    transposes("G", g, (s_xt_["A"], a + 1) if has(a) else gates_read)
                if has(b):
                    spread_pi(b, 4)
                    spread_pi(b, 5)
                if has(g):
                    z_product(g)
                for c in range(CH):
                    if has(a):
                        w_product(a, c)
                    if has(g) and c < SUB:
                        scores(g, c)
                if has(g - 1):
                    bias(g - 1)
                if has(b):
                    out_product(b, 0)
                if has(g):
                    gates_transposed(g, 0)
                if has(a):
                    logits(a)
                if has(b):
                    out_product(b, 1)
                if has(g):
                    gates_transposed(g, 1)
                if has(b):
                    out_product(b, 2)
                if has(g):
                    gates_transposed(g, 2)

            for i in range(4):
                pass_pe(i)
            with pe.Fori(4, UNITS) as i:
                pass_pe(i)
            for i in range(UNITS, UNITS + 2):
                pass_pe(i)
            bias(UNITS - 1)

            pe.wait_ge(s_bt, UNITS)
            pe.wait_ge(s_grr, SUB * UNITS)
            pe.wait_ge(s_stack, 16 * 9)
            pe.wait_ge(s_ones, 1)
            pe.wait_ge(s_w, 64)

            def hidden(tile, pair):
                block, j = divmod(pair // 2, PAIRS)
                o, eb = divmod(block, EB)
                if pair % QUADS == 0:
                    pe.wait_ge(s_zl[o], 96 * (tile + 1))
                wait(pe, s_hid, 2 * QUADS * tile + pair - 1)
                for a in range(2):
                    x = chunk(2 * j + o, eb, 2 * (pair % 2) + a) * 128
                    mm = t_.matmul((pair0, pair1)[pair % 2][:, a, 0:TN], w1s[:, x:x + 128], zst[:, o, j],
                                   start=True, stop=True)
                mm.then_inc(s_hp1, 1)

            def spread(tile, quad):
                block, j = divmod(quad, PAIRS)
                if quad % (QUADS // 4) == 0:
                    pe.wait_ge(s_gl[block // 2], 192 * (tile + 1))
                before = (tile, quad - 2) if quad >= 2 else (tile - 1, quad - 2 + QUADS)
                if before[1] in POOL_QUADS:
                    pe.wait_ge(s_gc, pool_quads(*before))
                else:
                    wait(pe, s_gat, dve_gated(*before))
                rows = slice(64 * (j % 2), 64 * (j % 2) + 48)
                t_.matmul(gate_banks[quad % 2][:, 0:TN], sel[rows], gst[rows, block, j // 2],
                          start=True, stop=True).then_inc(s_gb, 1)

            def decode(tile, block, k):
                if k == 0:
                    pe.wait_ge(s_gat, dve_gated(tile, PAIRS * block + PAIRS - 1))
                    wait(pe, s_pg, 2 * pool_quads(tile, PAIRS * block + PAIRS - 1))
                    if block == 0:
                        wait(pe, s_comb, tile)
                o, eb = divmod(block, EB)
                for j in range(PAIRS):
                    mm = t_.matmul(code_bank[32 * j:32 * j + 32, 0:TN], w2p[:, chunk(2 * j + o, eb, k)],
                                   gated[:, block % 2, j, k], start=(block == 0 and k == 0),
                                   stop=(block == BLOCKS - 1 and k == KH - 1), skip_group_check=True)
                mm.then_inc(s_code, 1)

            def out1(tile):
                pe.wait_ge(s_cb, tile + 1)
                pe.wait_ge(s_h1l, 16 * (tile + 1))
                t_.matmul(out_bank[0:G, 0:TN], g1w[:], code, start=True, stop=True).then_inc(s_f1, 1)

            def out2(tile, half):
                pe.wait_ge(s_y1, tile + 1)
                if half == 1:
                    pe.wait_ge(s_out, 2 * tile + 1)
                for k in range(2):
                    x = ST * (2 * half + k)
                    mm = t_.matmul(out_bank[0:ST, D * k:D * k + D], y1[:, x:x + ST], g2w[:],
                                   start=True, stop=True)
                mm.then_inc(s_f2, 1)

            def tile_pe(tile, first, last):
                def spread_next(quad):
                    if quad + 1 < QUADS:
                        spread(tile, quad + 1)
                    elif not last:
                        spread(tile + 1, 0)

                def hidden_ahead(quad, ahead):
                    pair = 2 * quad + ahead
                    if pair < 2 * QUADS:
                        hidden(tile, pair)
                    elif not last:
                        hidden(tile + 1, pair - 2 * QUADS)

                def decode_next(quad):
                    block, k = divmod(quad - PAIRS, KH)
                    if block >= 0:
                        decode(tile, block, k)
                    elif not first:
                        decode(tile - 1, BLOCKS - 1, k)

                for quad in range(QUADS):
                    spread_next(quad)
                    hidden_ahead(quad, AHEAD)
                    decode_next(quad)
                    hidden_ahead(quad, AHEAD + 1)
                    if not first:
                        if quad == OUT1_AT:
                            out1(tile - 1)
                        for half in range(2):
                            if quad == OUT2_AT[half]:
                                out2(tile - 1, half)

            spread(0, 0)
            for pair in range(AHEAD):
                hidden(0, pair)
            tile_pe(0, True, False)
            with pe.Fori(1, TILES - 1) as tile:
                tile_pe(tile, False, False)
            tile_pe(TILES - 1, False, True)
            for k in range(KH):
                decode(TILES - 1, BLOCKS - 1, k)
            out1(TILES - 1)
            out2(TILES - 1, 0)
            out2(TILES - 1, 1)


def kernel(**inputs):
    import concourse.bacc as bacc
    from concourse.bass_utils import run_bass_kernel_spmd as run

    a = {k: np.ascontiguousarray(v) for k, v in inputs.items()}

    def ids(x):
        return x.reshape(4, 16, 11, 7).transpose(2, 0, 1, 3)

    m10, m01 = a["mask_BS_i1_0"], a["mask_BS_i0_1"]
    i3, i9 = a["itok_BS_0_3"], a["itok_BS_0_9"]
    tables = [("L0_txt_W_type", m10), ("L0_txt_W_match_tok", m10), ("L0_txt_W_match_ent", m01),
              ("L0_txt_W_sf_tok", i3), ("L0_txt_W_sf_ent", i3), ("L0_txt_W_etype", i9),
              ("L0_txt_W_atype_ent", m10)]
    rows = [a[n].shape[0] for n, _ in tables]
    arrays = {
        "x": a["x"].reshape(64, 3, 4, 16, 4, 16).transpose(1, 3, 5, 0, 2, 4).reshape(768, 1024),
        "tok_w": a["L0_tok_W"].T,
        "tok_b": a["L0_tok_b"].reshape(1, -1),
        "word_ids": ids(a["x_txt"]).transpose(2, 3, 0, 1).reshape(112, 44),
        "pos_ids": ids(a["pos_BS"]).reshape(1, -1),
        "small_ids": np.concatenate([np.repeat(ids(i).reshape(1, -1), r, 0) for (_, i), r in zip(tables, rows)]),
        "row_index": np.concatenate([np.arange(r) for r in rows]).astype(np.float32).reshape(-1, 1),
        "w_word": a["L0_txt_W_word"],
        "w_pos": a["L0_txt_W_pos"],
        "w_small": np.concatenate([a[n] for n, _ in tables]),
        "gamma": a["L0_txt_ln_gamma"].reshape(1, -1),
        "beta": a["L0_txt_ln_beta"].reshape(1, -1),
        "w_qkv": a["L0_attn_w_qkv"],
        "temp": a["L0_attn_temp"],
        "w_out": a["L0_attn_w_out"],
        "b_out": a["L0_attn_b_out"].reshape(1, -1),
        "pz": a["L0_ffn_P"].transpose(1, 0, 2).reshape(192, 128),
        "ct": a["L0_ffn_C"].transpose(0, 2, 1).reshape(128, 64),
        "w1": a["L0_ffn_W1"].reshape(8, 4, 16, 16, 4, 8).transpose(3, 0, 1, 4, 2, 5).reshape(128, 2048),
        "b1": a["L0_ffn_b1"].reshape(8, 4, 16, 4, 8).transpose(0, 1, 3, 2, 4).reshape(128, 128),
        "w2": a["L0_ffn_W2"].reshape(8, 4, 16, 4, 8, 16).transpose(2, 4, 0, 1, 3, 5).reshape(128, 2048),
        "b2": a["L0_ffn_b2"].reshape(4, 2, 64, 16).transpose(1, 2, 0, 3).reshape(128, 4, 16),
        "g1": a["L0_ffn_G1"],
        "g1b": a["L0_ffn_g1b"].reshape(-1, 1),
        "g2": a["L0_ffn_G2"],
        "g2b": a["L0_ffn_g2b"].reshape(1, -1),
    }
    nc = bacc.Bacc("TRN2", target_bir_lowering=False, num_devices=1)
    feed, t = {}, {}
    for name, v in arrays.items():
        v = np.ascontiguousarray(v)
        feed["in_" + name] = v
        t[name] = nc.dram_tensor("in_" + name, v.shape, mybir.dt.from_np(v.dtype), kind="ExternalInput").ap()
    t["out"] = nc.dram_tensor("out_h", (B, N, D), F32, kind="ExternalOutput").ap()
    build(nc, t)
    r = run(nc, [feed], core_ids=[0])
    return r.results[0]["out_h"]
```
